# Optimizing a Trainium2 kernel written in Bass

```python
import numpy as np
import jax
import jax.numpy as jnp

def _softmax(x, axis=-1):
    return jax.nn.softmax(x, axis=axis)

def _gelu(x):
    return jax.nn.gelu(x, approximate=True)

def _silu(x):
    return jax.nn.silu(x)

def _sigmoid(x):
    return jax.nn.sigmoid(x)

def _layernorm(x, axis=-1, eps=1e-05):
    m = jnp.mean(x, axis=axis, keepdims=True)
    v = jnp.var(x, axis=axis, keepdims=True)
    return (x - m) / jnp.sqrt(v + eps)

def _scatter_add(tgt, idx, src, axis=0):
    return tgt.at[idx].add(src)

def _segment_sum(src, seg, n):
    return jax.ops.segment_sum(src, seg, n)
kernel_name = 'mk_gps_d2_gnn_r16_e6b60b'

def setup_inputs(seed: int=0):
    np.random.seed(seed)
    _w = jnp.asarray

    def _rec_inputs():
        import jax
        import jax.numpy as jnp
        _gk = jax.random.key(seed)
        x = -0.0002117 + 1 * jax.random.normal(jax.random.fold_in(_gk, 1), (6250, 256), jnp.float32)
        src = jax.random.randint(jax.random.fold_in(_gk, 2), (100000,), 0, 6250, jnp.int32)
        dst = jnp.minimum((6250 * jax.random.uniform(jax.random.fold_in(_gk, 3), (100000,)) ** 2.0).astype(jnp.int32), 99999)
        _o = jnp.argsort(dst, stable=True)
        src = src[_o]
        dst = dst[_o]
        edge_attr_10 = jax.random.uniform(jax.random.fold_in(_gk, 12), (100000, 10), jnp.float32, 0.0, 1)
        edge_attr_4 = 0.00109026 + 0.999989 * jax.random.normal(jax.random.fold_in(_gk, 13), (100000, 4), jnp.float32)
        return (x, src, dst, edge_attr_10, edge_attr_4)
    x, src, dst, edge_attr_10, edge_attr_4 = _rec_inputs()

    def _L0_gnn_setup():
        import jax, jax.numpy as jnp
        import numpy as np
        N_NODES = 6250
        N_EDGES = 20000
        D_IN, D_HID, D_OUT = (256, 1024, 256)
        BN_EPS = 1e-05
        key = jax.random.key(seed)
        ks = jax.random.split(key, 6)
        x = jax.random.normal(ks[0], (N_NODES, D_IN), dtype=jnp.float32)
        edge_index = jax.random.randint(ks[1], (2, N_EDGES), 0, N_NODES, dtype=jnp.int64)
        W1 = jax.random.normal(ks[2], (D_IN, D_HID), dtype=jnp.float32) * (1.0 / np.sqrt(D_IN))
        b1 = jnp.zeros((D_HID,), dtype=jnp.float32)
        gamma = jnp.ones((D_HID,), dtype=jnp.float32)
        beta = jnp.zeros((D_HID,), dtype=jnp.float32)
        W2 = jax.random.normal(ks[3], (D_HID, D_OUT), dtype=jnp.float32) * (1.0 / np.sqrt(D_HID))
        b2 = jnp.zeros((D_OUT,), dtype=jnp.float32)
        return {'x': x, 'edge_index': edge_index, 'W1': W1, 'b1': b1, 'gamma': gamma, 'beta': beta, 'W2': W2, 'b2': b2}
    _L0_gnn_all = _L0_gnn_setup()
    _L0_gnn_in = {k: v for k, v in _L0_gnn_all.items() if k in ('W1', 'b1', 'gamma', 'beta', 'W2', 'b2')}
    del _L0_gnn_all

    def _L0_mix_setup():
        import jax, jax.numpy as jnp
        import numpy as np
        EPS_NORM = 1e-06
        EPS_ATTN = 1e-06
        HEADS = 8

        def rmsnorm(x, w):
            ms = jnp.mean(x * x, axis=-1, keepdims=True)
            return w * (x * jax.lax.rsqrt(ms + EPS_NORM))

        def linear_attention(x, w_qkv, w_out, b_out):
            B, N, D = x.shape
            hd = D // HEADS
            qkv = (x @ w_qkv).reshape(B, N, 3, HEADS, hd)
            q, k, v = (qkv[:, :, 0], qkv[:, :, 1], qkv[:, :, 2])
            q = jax.nn.elu(q) + 1.0
            k = jax.nn.elu(k) + 1.0
            kv = jnp.einsum('bnhd,bnhm->bhdm', k, v)
            z = 1.0 / (jnp.einsum('bnhd,bhd->bnh', q, k.sum(axis=1)) + EPS_ATTN)
            out = jnp.einsum('bnhd,bhdm,bnh->bnhm', q, kv, z)
            out = out.reshape(B, N, D)
            return out @ w_out + b_out
        key = jax.random.key(seed)
        ks = jax.random.split(key, 4)
        B, N, D = (16, 512, 256)
        x = jax.random.normal(ks[0], (B, N, D), dtype=jnp.float32)
        w_norm1 = jnp.ones((D,), dtype=jnp.float32)
        w_qkv = jax.random.normal(ks[1], (D, 3 * D), dtype=jnp.float32) * 0.02
        w_out = jax.random.normal(ks[2], (D, D), dtype=jnp.float32) * 0.02
        b_out = jnp.zeros((D,), dtype=jnp.float32)
        w_norm2 = jnp.ones((D,), dtype=jnp.float32)
        return {'x': x, 'w_norm1': w_norm1, 'w_qkv': w_qkv, 'w_out': w_out, 'b_out': b_out, 'w_norm2': w_norm2}
    _L0_mix_all = _L0_mix_setup()
    _L0_mix_in = {k: v for k, v in _L0_mix_all.items() if k in ('w_norm1', 'w_qkv', 'w_out', 'b_out', 'w_norm2')}
    del _L0_mix_all

    def _L0_ffn_setup():
        import jax, jax.numpy as jnp
        import numpy as np
        E, D, H, TOP_K = (6, 256, 256, 2)
        ROUTER_H = D // 2
        key = jax.random.key(seed)
        ks = jax.random.split(key, 12)
        s = 1.0 / np.sqrt(D)
        sh = 1.0 / np.sqrt(H)
        sr = 1.0 / np.sqrt(ROUTER_H)
        return {'features': jax.random.normal(ks[0], (8, 256, D), dtype=jnp.float32), 'router_w1': jax.random.uniform(ks[1], (D, ROUTER_H), jnp.float32, -s, s), 'router_b1': jnp.zeros((ROUTER_H,), jnp.float32), 'router_w2': jax.random.uniform(ks[2], (ROUTER_H, E), jnp.float32, -sr, sr), 'router_b2': jnp.zeros((E,), jnp.float32), 'expert_w1': jax.random.uniform(ks[3], (E, D, H), jnp.float32, -s, s), 'expert_b1': jnp.zeros((E, H), jnp.float32), 'expert_w2': jax.random.uniform(ks[4], (E, H, H), jnp.float32, -sh, sh), 'expert_b2': jnp.zeros((E, H), jnp.float32), 'expert_w3': jax.random.uniform(ks[5], (E, H, D), jnp.float32, -sh, sh), 'expert_b3': jnp.zeros((E, D), jnp.float32)}
    _L0_ffn_all = _L0_ffn_setup()
    _L0_ffn_in = {k: v for k, v in _L0_ffn_all.items() if k in ('router_w1', 'router_b1', 'router_w2', 'router_b2', 'expert_w1', 'expert_b1', 'expert_w2', 'expert_b2', 'expert_w3', 'expert_b3')}
    del _L0_ffn_all

    def _L1_gnn_setup():
        import jax, jax.numpy as jnp
        import numpy as np
        MUL = 64
        N_NODES = 3125
        N_EDGES = 50000
        NUM_NEIGHBORS = 16.0
        SILU_NORM = 1.679177
        key = jax.random.key(seed)
        ks = jax.random.split(key, 9)
        node_in = jax.random.normal(ks[0], (N_NODES, 4 * MUL), dtype=jnp.float32)
        edge_src = jax.random.randint(ks[1], (N_EDGES,), 0, N_NODES)
        edge_dst = jax.random.randint(ks[2], (N_EDGES,), 0, N_NODES)
        edge_attr = jax.random.normal(ks[3], (N_EDGES, 4), dtype=jnp.float32)
        edge_len_emb = jax.random.uniform(ks[4], (N_EDGES, 10), dtype=jnp.float32)
        w_00_0 = jax.random.normal(ks[5], (MUL, MUL), dtype=jnp.float32)
        w_11_0 = jax.random.normal(ks[6], (MUL, MUL), dtype=jnp.float32)
        w_01_1 = jax.random.normal(ks[7], (MUL, MUL), dtype=jnp.float32)
        w_10_1 = jax.random.normal(ks[8], (MUL, MUL), dtype=jnp.float32)
        kf = jax.random.split(jax.random.fold_in(key, 1), 2)
        fc_w1 = jax.random.normal(kf[0], (10, 64), dtype=jnp.float32)
        fc_w2 = jax.random.normal(kf[1], (64, 1), dtype=jnp.float32)
        return {'node_in': node_in, 'edge_attr': edge_attr, 'edge_len_emb': edge_len_emb, 'w_00_0': w_00_0, 'w_11_0': w_11_0, 'w_01_1': w_01_1, 'w_10_1': w_10_1, 'fc_w1': fc_w1, 'fc_w2': fc_w2, 'edge_src': edge_src, 'edge_dst': edge_dst}
    _L1_gnn_all = _L1_gnn_setup()
    _L1_gnn_in = {k: v for k, v in _L1_gnn_all.items() if k in ('w_00_0', 'w_11_0', 'w_01_1', 'w_10_1', 'fc_w1', 'fc_w2')}
    del _L1_gnn_all

    def _L1_mix_setup():
        import jax, jax.numpy as jnp
        import numpy as np
        HEADS = 8
        DIM_HEAD = 64
        EPS = 1e-05

        def _inst_norm_lastdim(t):
            mu = jnp.mean(t, axis=-1, keepdims=True)
            var = jnp.mean(jnp.square(t - mu), axis=-1, keepdims=True)
            return (t - mu) * jax.lax.rsqrt(var + EPS)
        key = jax.random.key(seed)
        k1, k2, k3, k4 = jax.random.split(key, 4)
        b, n, dim = (4, 512, 256)
        inner = HEADS * DIM_HEAD
        x = jax.random.normal(k1, (b, n, dim), dtype=jnp.float32)
        Wqkv = jax.random.normal(k2, (3 * inner, dim), dtype=jnp.float32) * (1.0 / np.sqrt(dim))
        Wout = jax.random.normal(k3, (dim, inner), dtype=jnp.float32) * (1.0 / np.sqrt(inner))
        bout = jax.random.normal(k4, (dim,), dtype=jnp.float32) * 0.01
        return {'x': x, 'Wqkv': Wqkv, 'Wout': Wout, 'bout': bout}
    _L1_mix_all = _L1_mix_setup()
    _L1_mix_in = {k: v for k, v in _L1_mix_all.items() if k in ('Wqkv', 'Wout', 'bout')}
    del _L1_mix_all

    def _L1_ffn_setup():
        import math
        import jax, jax.numpy as jnp
        import numpy as np
        CAPACITY_FACTOR = 1.25
        TOP_K = 2
        LN_EPS = 1e-05

        def _layer_norm(x, gamma, beta):
            mu = jnp.mean(x, axis=-1, keepdims=True)
            var = jnp.var(x, axis=-1, keepdims=True)
            return (x - mu) * jax.lax.rsqrt(var + LN_EPS) * gamma + beta
        key = jax.random.key(seed)
        ks = jax.random.split(key, 4)
        B, S, D, F, E = (8, 256, 256, 512, 8)
        x = jax.random.normal(ks[0], (B, S, D), dtype=jnp.float32)
        Wr = jax.random.normal(ks[1], (D, E), dtype=jnp.float32) / np.sqrt(D)
        br = jnp.zeros((E,), jnp.float32)
        W1 = jax.random.normal(ks[2], (E, D, F), dtype=jnp.float32) / np.sqrt(D)
        b1 = jnp.zeros((E, F), jnp.float32)
        W2 = jax.random.normal(ks[3], (E, F, D), dtype=jnp.float32) / np.sqrt(F)
        b2 = jnp.zeros((E, D), jnp.float32)
        gamma = jnp.ones((D,), jnp.float32)
        beta = jnp.zeros((D,), jnp.float32)
        return {'x': x, 'Wr': Wr, 'br': br, 'W1': W1, 'b1': b1, 'W2': W2, 'b2': b2, 'gamma': gamma, 'beta': beta}
    _L1_ffn_all = _L1_ffn_setup()
    _L1_ffn_in = {k: v for k, v in _L1_ffn_all.items() if k in ('Wr', 'br', 'W1', 'b1', 'W2', 'b2', 'gamma', 'beta')}
    del _L1_ffn_all
    return {'x': x, 'src': src, 'dst': dst, 'edge_attr_10': edge_attr_10, 'edge_attr_4': edge_attr_4, 'L0_gnn_W1': _L0_gnn_in['W1'], 'L0_gnn_b1': _L0_gnn_in['b1'], 'L0_gnn_gamma': _L0_gnn_in['gamma'], 'L0_gnn_beta': _L0_gnn_in['beta'], 'L0_gnn_W2': _L0_gnn_in['W2'], 'L0_gnn_b2': _L0_gnn_in['b2'], 'L0_mix_w_norm1': _L0_mix_in['w_norm1'], 'L0_mix_w_qkv': _L0_mix_in['w_qkv'], 'L0_mix_w_out': _L0_mix_in['w_out'], 'L0_mix_b_out': _L0_mix_in['b_out'], 'L0_mix_w_norm2': _L0_mix_in['w_norm2'], 'L0_ffn_router_w1': _L0_ffn_in['router_w1'], 'L0_ffn_router_b1': _L0_ffn_in['router_b1'], 'L0_ffn_router_w2': _L0_ffn_in['router_w2'], 'L0_ffn_router_b2': _L0_ffn_in['router_b2'], 'L0_ffn_expert_w1': _L0_ffn_in['expert_w1'], 'L0_ffn_expert_b1': _L0_ffn_in['expert_b1'], 'L0_ffn_expert_w2': _L0_ffn_in['expert_w2'], 'L0_ffn_expert_b2': _L0_ffn_in['expert_b2'], 'L0_ffn_expert_w3': _L0_ffn_in['expert_w3'], 'L0_ffn_expert_b3': _L0_ffn_in['expert_b3'], 'L1_gnn_w_00_0': _L1_gnn_in['w_00_0'], 'L1_gnn_w_11_0': _L1_gnn_in['w_11_0'], 'L1_gnn_w_01_1': _L1_gnn_in['w_01_1'], 'L1_gnn_w_10_1': _L1_gnn_in['w_10_1'], 'L1_gnn_fc_w1': _L1_gnn_in['fc_w1'], 'L1_gnn_fc_w2': _L1_gnn_in['fc_w2'], 'L1_mix_Wqkv': _L1_mix_in['Wqkv'], 'L1_mix_Wout': _L1_mix_in['Wout'], 'L1_mix_bout': _L1_mix_in['bout'], 'L1_ffn_Wr': _L1_ffn_in['Wr'], 'L1_ffn_br': _L1_ffn_in['br'], 'L1_ffn_W1': _L1_ffn_in['W1'], 'L1_ffn_b1': _L1_ffn_in['b1'], 'L1_ffn_W2': _L1_ffn_in['W2'], 'L1_ffn_b2': _L1_ffn_in['b2'], 'L1_ffn_gamma': _L1_ffn_in['gamma'], 'L1_ffn_beta': _L1_ffn_in['beta']}

def reference(x, src, dst, edge_attr_10, edge_attr_4, L0_gnn_W1, L0_gnn_b1, L0_gnn_gamma, L0_gnn_beta, L0_gnn_W2, L0_gnn_b2, L0_mix_w_norm1, L0_mix_w_qkv, L0_mix_w_out, L0_mix_b_out, L0_mix_w_norm2, L0_ffn_router_w1, L0_ffn_router_b1, L0_ffn_router_w2, L0_ffn_router_b2, L0_ffn_expert_w1, L0_ffn_expert_b1, L0_ffn_expert_w2, L0_ffn_expert_b2, L0_ffn_expert_w3, L0_ffn_expert_b3, L1_gnn_w_00_0, L1_gnn_w_11_0, L1_gnn_w_01_1, L1_gnn_w_10_1, L1_gnn_fc_w1, L1_gnn_fc_w2, L1_mix_Wqkv, L1_mix_Wout, L1_mix_bout, L1_ffn_Wr, L1_ffn_br, L1_ffn_W1, L1_ffn_b1, L1_ffn_W2, L1_ffn_b2, L1_ffn_gamma, L1_ffn_beta):
    import jax
    import jax.numpy as jnp

    def _L0_gnn_ref(x, edge_index, W1, b1, gamma, beta, W2, b2):
        import jax, jax.numpy as jnp
        import numpy as np
        N_NODES = 6250
        N_EDGES = 20000
        D_IN, D_HID, D_OUT = (256, 1024, 256)
        BN_EPS = 1e-05
        src, dst = (edge_index[0], edge_index[1])
        agg = jax.ops.segment_sum(x[src], dst, num_segments=x.shape[0])
        h = agg + x
        h1 = h @ W1 + b1
        mean = jnp.mean(h1, axis=0)
        var = jnp.mean(jnp.square(h1 - mean), axis=0)
        h1 = (h1 - mean) * jax.lax.rsqrt(var + BN_EPS) * gamma + beta
        h1 = jax.nn.relu(h1)
        out = jax.nn.relu(h1 @ W2 + b2)
        return out

    def _L0_mix_ref(x, w_norm1, w_qkv, w_out, b_out, w_norm2):
        import jax, jax.numpy as jnp
        import numpy as np
        EPS_NORM = 1e-06
        EPS_ATTN = 1e-06
        HEADS = 8

        def rmsnorm(x, w):
            ms = jnp.mean(x * x, axis=-1, keepdims=True)
            return w * (x * jax.lax.rsqrt(ms + EPS_NORM))

        def linear_attention(x, w_qkv, w_out, b_out):
            B, N, D = x.shape
            hd = D // HEADS
            qkv = (x @ w_qkv).reshape(B, N, 3, HEADS, hd)
            q, k, v = (qkv[:, :, 0], qkv[:, :, 1], qkv[:, :, 2])
            q = jax.nn.elu(q) + 1.0
            k = jax.nn.elu(k) + 1.0
            kv = jnp.einsum('bnhd,bnhm->bhdm', k, v)
            z = 1.0 / (jnp.einsum('bnhd,bhd->bnh', q, k.sum(axis=1)) + EPS_ATTN)
            out = jnp.einsum('bnhd,bhdm,bnh->bnhm', q, kv, z)
            out = out.reshape(B, N, D)
            return out @ w_out + b_out
        h = x + linear_attention(rmsnorm(x, w_norm1), w_qkv, w_out, b_out)
        return h + rmsnorm(h, w_norm2)

    def _L0_ffn_ref(features, router_w1, router_b1, router_w2, router_b2, expert_w1, expert_b1, expert_w2, expert_b2, expert_w3, expert_b3):
        import jax, jax.numpy as jnp
        import numpy as np
        E, D, H, TOP_K = (6, 256, 256, 2)
        ROUTER_H = D // 2
        rh = jax.nn.relu(features @ router_w1 + router_b1)
        expert_logits = jax.nn.softmax(rh @ router_w2 + router_b2, axis=-1)
        top_w, top_i = jax.lax.top_k(expert_logits, TOP_K)
        routing_weights = jax.nn.softmax(top_w, axis=-1)
        h1 = jax.nn.relu(jnp.einsum('bsd,edh->bseh', features, expert_w1) + expert_b1)
        h2 = jax.nn.relu(jnp.einsum('bseh,ehf->bsef', h1, expert_w2) + expert_b2)
        expert_out = jnp.einsum('bsef,efo->bseo', h2, expert_w3) + expert_b3
        sel = jnp.take_along_axis(expert_out, top_i[:, :, :, None], axis=2)
        combined = jnp.sum(sel * routing_weights[..., None], axis=2)
        return combined

    def _L1_gnn_ref(node_in, edge_attr, edge_len_emb, w_00_0, w_11_0, w_01_1, w_10_1, fc_w1, fc_w2, edge_src, edge_dst):
        import jax, jax.numpy as jnp
        import numpy as np
        MUL = 64
        N_NODES = 3125
        N_EDGES = 50000
        NUM_NEIGHBORS = 16.0
        SILU_NORM = 1.679177
        src = node_in[edge_src]
        s0 = src[:, :MUL]
        s1 = src[:, MUL:].reshape(-1, MUL, 3)
        a0 = edge_attr[:, 0:1]
        a1 = edge_attr[:, 1:4]
        alpha = np.float32(1.0 / np.sqrt(2.0 * MUL))
        inv_sqrt3 = np.float32(1.0 / np.sqrt(3.0))
        out0 = alpha * (jnp.einsum('ei,io->eo', s0 * a0, w_00_0) + inv_sqrt3 * jnp.einsum('eim,em,io->eo', s1, a1, w_11_0))
        out1 = alpha * (jnp.einsum('ei,io,em->eom', s0, w_01_1, a1) + jnp.einsum('eim,io->eom', s1 * a0[:, :, None], w_10_1))
        msg_ang = jnp.concatenate([out0, out1.reshape(-1, 3 * MUL)], axis=1)
        h = jax.nn.silu(edge_len_emb @ fc_w1 / np.float32(np.sqrt(10.0))) * np.float32(SILU_NORM)
        msg_rad = h @ fc_w2 / np.float32(np.sqrt(64.0))
        messages = msg_ang * msg_rad
        agg = jax.ops.segment_sum(messages, edge_dst, num_segments=node_in.shape[0])
        return agg / np.float32(np.sqrt(NUM_NEIGHBORS))

    def _L1_mix_ref(x, Wqkv, Wout, bout):
        import jax, jax.numpy as jnp
        import numpy as np
        HEADS = 8
        DIM_HEAD = 64
        EPS = 1e-05

        def _inst_norm_lastdim(t):
            mu = jnp.mean(t, axis=-1, keepdims=True)
            var = jnp.mean(jnp.square(t - mu), axis=-1, keepdims=True)
            return (t - mu) * jax.lax.rsqrt(var + EPS)
        b, n, dim = x.shape
        qkv = jnp.einsum('bnc,fc->bnf', x, Wqkv)
        q, k, v = jnp.split(qkv, 3, axis=-1)

        def to_heads(t):
            return t.reshape(b, n, HEADS, DIM_HEAD).transpose(0, 2, 1, 3)
        q, k, v = (to_heads(q), to_heads(k), to_heads(v))
        k = _inst_norm_lastdim(k)
        v = _inst_norm_lastdim(v)
        dots = jnp.einsum('bhnd,bhne->bhde', k, v)
        out = jnp.einsum('bhnd,bhde->bhne', q, dots) / n
        out = out.transpose(0, 2, 1, 3).reshape(b, n, HEADS * DIM_HEAD)
        return jnp.einsum('bnf,cf->bnc', out, Wout) + bout

    def _L1_ffn_ref(x, Wr, br, W1, b1, W2, b2, gamma, beta):
        import math
        import jax, jax.numpy as jnp
        import numpy as np
        CAPACITY_FACTOR = 1.25
        TOP_K = 2
        LN_EPS = 1e-05

        def _layer_norm(x, gamma, beta):
            mu = jnp.mean(x, axis=-1, keepdims=True)
            var = jnp.var(x, axis=-1, keepdims=True)
            return (x - mu) * jax.lax.rsqrt(var + LN_EPS) * gamma + beta
        B, S, D = x.shape
        E = Wr.shape[1]
        N = B * S
        K = TOP_K
        logits = jnp.mean(x, axis=1) @ Wr + br
        routing_weights = jax.nn.softmax(logits, axis=-1)
        capacity = float(math.ceil(N * CAPACITY_FACTOR / E))
        expected_loads = routing_weights.sum(axis=0) * (N / B)
        scale = jnp.where(expected_loads > capacity, capacity / expected_loads, 1.0)
        routing_weights = jax.nn.softmax(routing_weights * scale, axis=-1)
        rw_tok = jnp.broadcast_to(routing_weights[:, None, :], (B, S, E)).reshape(N, E)
        top_w, top_i = jax.lax.top_k(rw_tok, K)
        top_w = jax.nn.softmax(top_w, axis=-1)
        xf = x.reshape(N, D)
        h = jax.nn.gelu(jnp.einsum('nd,edf->enf', xf, W1) + b1[:, None, :], approximate=False)
        y = jnp.einsum('enf,efd->end', h, W2) + b2[:, None, :]
        w_dense = jnp.zeros((N, E), x.dtype).at[jnp.arange(N)[:, None], top_i].add(top_w)
        out = jnp.einsum('ne,end->nd', w_dense, y).reshape(B, S, D)
        out = _layer_norm(out + x, gamma, beta)
        return out
    edge_index = jnp.stack([src, dst])
    xn = _layernorm(x, axis=-1)
    x = x + _L0_gnn_ref(xn, edge_index, L0_gnn_W1, L0_gnn_b1, L0_gnn_gamma, L0_gnn_beta, L0_gnn_W2, L0_gnn_b2) + _L0_mix_ref(xn[None], L0_mix_w_norm1, L0_mix_w_qkv, L0_mix_w_out, L0_mix_b_out, L0_mix_w_norm2)[0]
    x = x + _L0_ffn_ref(_layernorm(x, axis=-1)[None], L0_ffn_router_w1, L0_ffn_router_b1, L0_ffn_router_w2, L0_ffn_router_b2, L0_ffn_expert_w1, L0_ffn_expert_b1, L0_ffn_expert_w2, L0_ffn_expert_b2, L0_ffn_expert_w3, L0_ffn_expert_b3)[0]
    xn = _layernorm(x, axis=-1)
    x = x + _L1_gnn_ref(xn, edge_attr_4, edge_attr_10, L1_gnn_w_00_0, L1_gnn_w_11_0, L1_gnn_w_01_1, L1_gnn_w_10_1, L1_gnn_fc_w1, L1_gnn_fc_w2, src, dst) + _L1_mix_ref(xn[None], L1_mix_Wqkv, L1_mix_Wout, L1_mix_bout)[0]
    x = x + _L1_ffn_ref(_layernorm(x, axis=-1)[None], L1_ffn_Wr, L1_ffn_br, L1_ffn_W1, L1_ffn_b1, L1_ffn_W2, L1_ffn_b2, L1_ffn_gamma, L1_ffn_beta)[0]
    return x

_drawn_inputs = setup_inputs


def setup_inputs(seed=0):
    import zlib

    import numpy as np

    out = dict(_drawn_inputs(seed))
    spreads = {'L0_gnn_b1': (0.0, 0.8),
     'L0_gnn_gamma': (1.0, 0.2),
     'L0_gnn_beta': (0.0, 0.443),
     'L0_gnn_b2': (0.0, 0.1),
     'L0_mix_w_norm1': (1.0, 0.6),
     'L0_mix_b_out': (0.0, 0.1),
     'L0_mix_w_norm2': (1.0, 0.2),
     'L0_ffn_router_b1': (0.0, 0.652),
     'L0_ffn_router_b2': (0.0, 0.429),
     'L0_ffn_expert_b1': (0.0, 0.8),
     'L0_ffn_expert_b2': (0.0, 0.8),
     'L0_ffn_expert_b3': (0.0, 0.325),
     'L1_ffn_br': (0.0, 0.1),
     'L1_ffn_b1': (0.0, 0.689),
     'L1_ffn_b2': (0.0, 0.514),
     'L1_ffn_gamma': (1.0, 0.2),
     'L1_ffn_beta': (0.0, 0.345)}
    factors = {'L0_mix_w_qkv': 8.0,
     'L0_mix_w_out': 8.0,
     'L0_ffn_expert_w1': 3.414,
     'L0_ffn_expert_w2': 2.908,
     'L1_mix_bout': 8.0}
    for name, (base, spread) in spreads.items():
        noise = np.random.default_rng([zlib.crc32(name.encode()), seed]).standard_normal(out[name].shape)
        drawn = base * np.exp(spread * noise) if base else spread * noise
        out[name] = jnp.asarray(drawn.astype(out[name].dtype))
    for name, factor in factors.items():
        out[name] = (out[name] * factor).astype(out[name].dtype)
    return out
```

```python
from contextlib import ExitStack

import concourse.bass as bass
from concourse import mybir

F32 = mybir.dt.float32
I32 = mybir.dt.int32
U32 = mybir.dt.uint32
ALU = mybir.AluOpType
ACT = mybir.ActivationFunctionType
AX = mybir.AxisListType.X
ds = bass.ds

N, D, E = 6250, 256, 100000
P = 128
TN = 125
BN = 2 * TN
NB = N // BN
DC = D // P
WIN = 64
NPAD = N + WIN
GE = 2 * TN
NG = E // GE
RR = 100
RU = E // RR
ST = RU // TN
HID = 1024
LN_EPS = 1e-5
H0, HD0 = 8, 32
NE0, RH0 = 6, 128
H1, HD1 = 8, 64
NE1, F1 = 8, 512
MUL = 64
NEG = -1.0


class Steps:

    def __init__(self, sem, *names):
        self.sem, self.names, self.at = sem, names, 0

    def done(self, ins, name):
        assert self.names[self.at % len(self.names)] == name, (self.names, self.at, name)
        self.at += 1
        ins.then_inc(self.sem, 1)

    def wait(self, eng, i, name):
        value = i * len(self.names) + self.names.index(name) + 1
        if not isinstance(value, int) or value > 0:
            eng.wait_ge(self.sem, value)


class Landing:

    def __init__(self, sems, per=1):
        self.sems, self.per = sems, per

    def start(self, ins, u):
        ins.then_inc(self.sems[u], 16)

    def wait(self, eng, u, h):
        value = 16 * self.per * (h + 1)
        if not isinstance(value, int) or value > 0:
            eng.wait_ge(self.sems[u], value)


def pipeline(eng, n, stages, unroll=2):
    deepest = max(lag for _, lag in stages)
    steps = n + deepest
    first = deepest + unroll

    def one(s, k=None):
        for fn, lag in stages:
            i = s - lag
            if k is not None:
                fn(k * unroll + i, i % unroll, k + i // unroll)
            elif 0 <= i < n:
                fn(i, i % unroll, i // unroll)

    turns = max(0, (n - first) // unroll)
    if turns < 2:
        first, turns = steps, 0
    for s in range(min(first, steps)):
        one(s)
    if turns:
        with eng.Fori(0, turns) as k:
            for u in range(unroll):
                one(first + u, k)
    for s in range(first + turns * unroll, steps):
        one(s)


def gps_kernel(nc, A, out):
    top = ExitStack()
    sem_names = iter(range(10000))

    def sem(name):
        return top.enter_context(nc.semaphore(f"{name}_{next(sem_names)}"))

    def recycle(sems):
        nc.clear_and_free_semaphores(sems)
        nc.all_engine_barrier()

    class Phase:

        def __init__(self, name):
            self.name, self.ctx, self.sems = name, ExitStack(), []

        def __enter__(self):
            return self

        def __exit__(self, *a):
            self.ctx.close()
            if a[0] is None:
                recycle(self.sems)

        def sb(self, name, shape, dt=F32):
            return self.ctx.enter_context(nc.sbuf_tensor(f"{self.name}_{name}", shape, dt))

        def sem(self, name):
            self.sems.append(nc.alloc_semaphore(name=f"{self.name}_{name}"))
            return self.sems[-1]

        def steps(self, name, *names):
            return Steps(self.sem(name), *names)

        def landing(self, name, slots, per=1):
            return Landing([self.sem(f"{name}{u}") for u in range(slots)], per)

    def sb(name, shape, dt=F32):
        return top.enter_context(nc.sbuf_tensor(name, shape, dt))

    def scratch(name, shape, dt=F32):
        return nc.dram_tensor(name, shape, dt).ap()

    def rows_of(dram, i):
        return dram[ds(i * BN, BN), :].rearrange("(t p) f -> p t f", t=2)

    def chunked(dram):
        return dram.rearrange("(c p) n -> p c n", p=P)

    with top:
        ps = top.enter_context(nc.psum_tensor("ps", [P, 8, 512], F32))

        ident = sb("ident", [P, P])
        ones = sb("ones", [P, P])
        iota = sb("iota", [P, P])
        neg_half = sb("neg_half", [P, 16])
        layer0 = top.enter_context(ExitStack())
        cols = layer0.enter_context(nc.sbuf_tensor("cols", [P, DC, NPAD], F32))

        xn_d = scratch("xn_d", (N, D))
        xp_d = scratch("xp_d", (N, D))
        h1_d = scratch("h1_d", (NB, P, 8 * BN))
        x1_d = scratch("x1_d", (N, D))
        f1_d = scratch("f1_d", (N, D))
        x2_d = scratch("x2_d", (N, D))
        xm_d = scratch("xm_d", (N, D))
        xmT_d = scratch("xmT_d", (NB, P, DC * BN))
        x3_d = scratch("x3_d", (N, D))
        f3T_d = scratch("f3T_d", (2 * NB, P, DC * TN))
        f3_d = scratch("f3_d", (N, D))
        idx_d = scratch("idx_d", (P, RR * ST), I32)
        rel_d = scratch("rel_d", (P, RR * ST))
        left_d = scratch("left_d", (P, RR * ST))
        w_d = scratch("w_d", (P, RR * ST * 4))
        base_d = scratch("base_d", (1, NG), I32)
        flag_d = scratch("flag_d", (1, 1), I32)
        fsum_d = scratch("fsum_d", (P, DC * 2 * NB))
        mix1_d = scratch("mix1_d", (P, DC * D))

        s_const = sem("const")
        s_held = {engine: sem(f"held_{engine}") for engine in ("DVE", "PE", "Pool")}
        with nc.Block() as block:
            @block.gpsimd
            def _(e):
                e.memset(ident[:, :], 0.0).then_inc(s_const, 1)
                e.iota(iota[:, :], pattern=[[1, P]], base=0, channel_multiplier=0,
                       allow_small_or_imprecise_dtypes=True).then_inc(s_const, 1)
                e.memset(ones[:, :], 1.0).then_inc(s_const, 1)
                e.memset(neg_half[:, :], -0.5).then_inc(s_const, 1)
                e.memset(cols[:, :, N:NPAD], 0.0).then_inc(s_const, 1)
                e.wait_ge(s_const, 1)
                e.affine_select(out=ident[:, :], in_=ident[:, :], compare_op=ALU.not_equal, fill=1.0, base=0,
                                pattern=[[-1, P]], channel_multiplier=1).then_inc(s_const, 1)
                e.wait_ge(s_const, 6)

        def chained(e, ins, s, box):
            box[0] += 1
            ins.then_inc(s, 1)
            e.wait_ge(s, box[0])

        with Phase("p0") as ph:
            raw_i = ph.sb("raw_i", [RR, 2, RU], I32)
            raw_f = ph.sb("raw_f", [RR, 2, RU])
            idx = ph.sb("idx", [TN, RR, ST], I32)
            dst = ph.sb("dst", [TN, NG, 2])
            base = ph.sb("base", [TN, NG])
            base_i = ph.sb("base_i", [1, NG], I32)
            rel = ph.sb("rel", [TN, NG, 2])
            ok = ph.sb("ok", [TN, NG, 2])
            left = ph.sb("left", [TN, NG, 2])
            bad = ph.sb("bad", [TN, 1])
            flag = ph.sb("flag", [1, 1], I32)
            s_in, s_f, s_t, s_c, s_b, s_x, s_g, s_out = (ph.sem(n) for n in
                                                         ("in", "f", "t", "c", "b", "x", "g", "out"))
            with nc.Block() as block:
                @block.sync
                def _(e):
                    for k, name in enumerate(("src", "dst")):
                        e.dma_start(raw_i[:, k, :], A[name].rearrange("(r u) -> r u", u=RU)).then_inc(s_in, 16)
                    e.wait_ge(s_x, 1)
                    e.dma_start(idx_d[0:TN, :], idx[:, :, :].rearrange("p r s -> p (r s)")).then_inc(s_out, 16)
                    e.dma_start(rel_d[0:TN, :], rel[:, :, :].rearrange("p g j -> p (g j)")).then_inc(s_out, 16)
                    e.dma_start(left_d[0:TN, :], left[:, :, :].rearrange("p g j -> p (g j)")).then_inc(s_out, 16)
                    e.dma_start(base_d[:, :], base_i[:, :]).then_inc(s_out, 16)
                    e.dma_start(flag_d[:, :], flag[:, :]).then_inc(s_out, 16)
                    e.wait_ge(s_out, 5 * 16)

                @block.tensor
                def _(e):
                    e.wait_ge(s_f, 2)
                    for k in range(2):
                        for s in range(ST):
                            at = (s % 4) * RR
                            mm = e.transpose(ps[0:TN, 2 * k + s // 4, at:at + RR],
                                             raw_f[:, k, s * TN:(s + 1) * TN], ident[0:RR, 0:RR])
                    mm.then_inc(s_t, 1)
                    e.wait_ge(s_c, 4)
                    e.matmul(ps[0:TN, 4, 0:NG], ones[0:1, 0:TN], dst[0:1, :, 0],
                             start=True, stop=True).then_inc(s_b, 1)
                    e.wait_ge(s_g, 1)
                    e.matmul(ps[0:1, 5, 0:1], bad[:, :], ones[0:TN, 0:1], start=True, stop=True).then_inc(s_b, 1)

                @block.vector
                def _(e):
                    e.wait_ge(s_in, 32)
                    for k in range(2):
                        e.tensor_copy(raw_f[:, k, :], raw_i[:, k, :]).then_inc(s_f, 1)
                    e.wait_ge(s_t, 1)
                    for k, to in enumerate((idx[:, :, :], dst[:, :, :].rearrange("p (r q) j -> p r (q j)", r=RR))):
                        for b in range(2):
                            e.tensor_copy(to[:, :, 4 * b:4 * b + 4],
                                          ps[0:TN, 2 * k + b, 0:4 * RR].rearrange("p (s r) -> p r s", s=4))\
                             .then_inc(s_c, 1)
                    box = [0]
                    s_v = ph.sem("v")

                    def step(ins):
                        chained(e, ins, s_v, box)
                    e.wait_ge(s_b, 1)
                    step(e.tensor_scalar(base[:, :], ps[0:TN, 4, 0:NG], 0.0, float(N), ALU.max, ALU.min))
                    step(e.tensor_copy(base_i[:, :], base[0:1, :]))
                    e.wait_ge(s_c, 4)
                    wide = base[:, :].unsqueeze(2).broadcast_to([TN, NG, 2])
                    step(e.tensor_tensor(rel[:, :, :], dst[:, :, :], wide, ALU.subtract))
                    step(e.tensor_scalar(left[:, :, :], rel[:, :, :], 0.0, None, ALU.is_ge))
                    step(e.scalar_tensor_tensor(ok[:, :, :], rel[:, :, :], float(WIN), left[:, :, :],
                                                ALU.is_lt, ALU.mult))
                    step(e.scalar_tensor_tensor(rel[:, :, :], rel[:, :, :], 1.0, ok[:, :, :], ALU.add, ALU.mult))
                    step(e.tensor_scalar(rel[:, :, :], rel[:, :, :], -1.0, None, ALU.add))
                    step(e.tensor_scalar(ok[:, :, :], ok[:, :, :], -1.0, 1.0, ALU.mult, ALU.add))
                    e.tensor_reduce(bad[:, :], ok[:, :, :].rearrange("p g j -> p (g j)"), AX, ALU.add).then_inc(s_g, 1)
                    step(e.scalar_tensor_tensor(left[:, :, :], dst[:, :, :], 1.0, ok[:, :, :], ALU.add, ALU.mult))
                    step(e.tensor_scalar(left[:, :, :], left[:, :, :], -1.0, None, ALU.add))
                    e.wait_ge(s_b, 2)
                    step(e.tensor_copy(flag[:, :], ps[0:1, 5, 0:1]))
                    e.sem_inc(s_x, 1)

        UU, K1, C1 = 10, 10, 64
        NU = RU // UU
        with Phase("p0r") as ph:
            emb = ph.sb("emb", [RR, 4, UU * K1])
            embT = ph.sb("embT", [UU * K1, 2, RR])
            w1b = ph.sb("w1b", [UU * K1, UU, C1])
            w2r = ph.sb("w2r", [RR, C1])
            hs = ph.sb("hs", [RR, 2, UU, C1])
            hw = ph.sb("hw", [RR, 2, UU, C1])
            rad = ph.sb("rad", [RR, RU])
            attr = ph.sb("attr", [RR, RU, 4])
            wr = ph.sb("wr", [RR, 4, RU])
            wt = ph.sb("wt", [TN, RR, ST, 4])
            s_z, s_w, s_a, s_wr, s_t, s_e, s_o, s_ws = (ph.sem(n) for n in ("z", "w", "a", "wr", "t", "e", "o", "ws"))
            e_in = ph.landing("emb", 4)
            turn = ph.steps("turn", "turn")
            copied = ph.steps("copied", "embT")
            hid = ph.steps("hid", "hid")
            act = ph.steps("act", "silu")
            rads = ph.steps("rads", "mul", "sum")
            ORDER = (1, 0, 2, 3)
            with nc.Block() as block:
                @block.sync
                def _(e):
                    e.wait_ge(s_z, 1)
                    for u in range(UU):
                        e.dma_start(w1b[u * K1:(u + 1) * K1, u, :], A["L1_gnn_fc_w1"]).then_inc(s_w, 16)
                    e.dma_start(w2r[:, :], A["L1_gnn_fc_w2"].rearrange("c a -> (a c)").partition_broadcast(RR))\
                     .then_inc(s_w, 16)
                    raw = A["edge_attr_10"].rearrange("(r v u) k -> v r (u k)", r=RR, u=UU)

                    def load(i, u, h):
                        turn.wait(e, i - 4, "turn")
                        e_in.start(e.dma_start(emb[:, u, :], raw[ds(i, 1), :, :].rearrange("v r k -> (v r) k")), u)
                    pipeline(e, NU, [(load, 0)], unroll=4)
                    e.dma_start(attr[:, :, :], A["edge_attr_4"].rearrange("(r u) k -> r u k", r=RR)).then_inc(s_a, 16)
                    e.wait_ge(s_e, ST)
                    e.dma_start(w_d[0:TN, :], wt[:, :, :, :].rearrange("p r s k -> p (r s k)")).then_inc(s_o, 16)
                    e.wait_ge(s_o, 16)

                @block.gpsimd
                def _(e):
                    e.memset(w1b[:, :, :], 0.0).then_inc(s_z, 1)

                @block.tensor
                def _(e):
                    e.wait_ge(s_w, 16 * (UU + 1))

                    def turned(i, u, h):
                        e_in.wait(e, u, h)
                        copied.wait(e, i - 1, "embT")
                        turn.done(e.transpose(ps[0:UU * K1, 0, 0:RR], emb[:, u, :], ident[0:RR, 0:RR]), "turn")

                    def hidden(i, u, h):
                        copied.wait(e, i, "embT")
                        act.wait(e, i - 1, "silu")
                        for k in range(2):
                            half = slice(k * UU // 2, (k + 1) * UU // 2)
                            mm = e.matmul(ps[0:RR, 2 + k, 0:UU * C1 // 2], embT[:, u % 2, :],
                                          w1b[:, half, :].rearrange("p u c -> p (u c)"), start=True, stop=True)
                        hid.done(mm, "hid")
                    pipeline(e, NU, [(turned, 0), (hidden, 1)], unroll=4)
                    e.wait_ge(s_wr, 4)
                    for s in range(ST):
                        if s >= 2:
                            e.wait_ge(s_e, s - 1)
                        for k in range(4):
                            mm = e.transpose(ps[0:TN, 4 + s % 2, k * RR:(k + 1) * RR],
                                             wr[:, k, s * TN:(s + 1) * TN], ident[0:RR, 0:RR])
                        mm.then_inc(s_t, 1)

                @block.scalar
                def _(e):
                    def copy(i, u, h):
                        turn.wait(e, i, "turn")
                        hid.wait(e, i - 2, "hid")
                        copied.done(e.activation(embT[:, u % 2, :], ps[0:UU * K1, 0, 0:RR], ACT.Copy), "embT")

                    def silu(i, u, h):
                        hid.wait(e, i, "hid")
                        rads.wait(e, i - 2, "mul")
                        act.done(e.activation(hs[:, u % 2, :, :],
                                              ps[0:RR, 2:4, 0:UU * C1 // 2], ACT.Silu, scale=K1 ** -0.5), "silu")
                    pipeline(e, NU, [(copy, 0), (silu, 1)], unroll=4)

                @block.vector
                def _(e):
                    e.wait_ge(s_w, 16 * (UU + 1))
                    e.tensor_scalar(w2r[:, :], w2r[:, :], 1.679177 / 8.0, None, ALU.mult).then_inc(s_ws, 1)
                    e.wait_ge(s_ws, 1)

                    def mul(i, u, h):
                        act.wait(e, i, "silu")
                        rads.done(e.tensor_tensor(hw[:, u % 2, :, :], hs[:, u % 2, :, :],
                                                  w2r[:, :].unsqueeze(1).broadcast_to([RR, UU, C1]), ALU.mult), "mul")
                        rads.wait(e, i, "mul")
                        rads.done(e.tensor_reduce(rad[:, ds(i * UU, UU)], hw[:, u % 2, :, :], AX, ALU.add), "sum")
                    pipeline(e, NU, [(mul, 0)], unroll=4)
                    e.wait_ge(s_a, 16)
                    rads.wait(e, NU - 1, "sum")
                    for k, m in enumerate(ORDER):
                        e.tensor_tensor(wr[:, k, :], attr[:, :, m], rad[:, :], ALU.mult).then_inc(s_wr, 1)
                    for s in range(ST):
                        e.wait_ge(s_t, s + 1)
                        e.tensor_copy(wt[:, :, s, :], ps[0:TN, 4 + s % 2, 0:4 * RR].rearrange("p (k r) -> p r k", k=4))\
                         .then_inc(s_e, 1)

        with Phase("p1") as ph:
            qT = ph.sb("qT", [P, DC, N])
            kv_acc = ph.sb("kv_acc", [P, DC * P + DC * HD0])
            inner = Phase("p1a")
            xin = inner.sb("xin", [TN, 2, 2, D])
            st = inner.sb("st", [TN, 2, 2, 6])
            mv = inner.sb("mv", [TN, 2, 2, 2])
            pre = inner.sb("pre", [TN, 2, 2, 2])
            rs = inner.sb("rs", [TN, 2, 2, 2])
            xn = inner.sb("xn", [TN, 2, 2, D])
            xr = inner.sb("xr", [TN, 2, 2, D])
            xrT = inner.sb("xrT", [P, 2, DC, BN])
            wqkv = inner.sb("wqkv", [P, DC, 3 * D])
            wn1 = inner.sb("wn1", [P, DC])
            ek = inner.sb("ek", [TN, 2, D])
            rk = inner.sb("rk", [TN, 2, D])
            k1 = inner.sb("k1", [TN, 2, 2, D])
            v1 = inner.sb("v1", [TN, 2, 2, D])
            eq = inner.sb("eq", [P, DC, BN])
            rq = inner.sb("rq", [P, DC, BN])
            s_w = inner.sem("w")
            s_ws = inner.sem("ws")
            x_in = inner.landing("x", 2)
            xn_out = inner.landing("xn", 2)
            stats = inner.steps("stats", "stats0", "stats1", "aggr0", "aggr1", "pre0", "pre1")
            root = inner.steps("root", "root")
            norm = inner.steps("norm", "xn0", "xn1", "xr0", "xr1")
            turn = inner.steps("turn", "xnT", "xrT")
            copied = inner.steps("copied", "cols", "xrT")
            proj = inner.steps("proj", "k", "q")
            acts = inner.steps("acts", "ek", "rk", "v", "eq", "rq")
            feat = inner.steps("feat", "k", "q")
            kvs = inner.steps("kvs", "kv")
            accd = inner.steps("accd", "acc")
            s_z = inner.sem("z")

            with nc.Block() as block:
                @block.sync
                def _(e):
                    e.dma_start(wqkv[:, :, :], chunked(A["L0_mix_w_qkv"])).then_inc(s_w, 16)
                    e.dma_start(wn1[:, :], A["L0_mix_w_norm1"].rearrange("(c p) -> p c", p=P),
                                allow_slow_non_contiguous=True).then_inc(s_w, 16)

                    def load(i, u, h):
                        norm.wait(e, i - 2, "xr1")
                        x_in.start(e.dma_start(xin[:, u, :, :], rows_of(A["x"], i)), u)

                    def store(i, u, h):
                        norm.wait(e, i, "xn1")
                        xn_out.start(e.dma_start(rows_of(xn_d, i), xn[:, u, :, :]), u)
                    pipeline(e, NB, [(load, 0), (store, 2)])
                    for u in range(2):
                        xn_out.wait(e, u, (NB - 1 - u) // 2)

                @block.gpsimd
                def _(e):
                    def roots(i, u, h):
                        stats.wait(e, i, "pre1")
                        norm.wait(e, i - 2, "xr1")
                        root.done(e.tensor_tensor(rs[:, u, :, :], pre[:, u, :, :],
                                                  neg_half[0:TN, 0:4].rearrange("p (a b) -> p a b", a=2),
                                                  ALU.pow), "root")
                    pipeline(e, NB, [(roots, 0)])

                @block.vector
                def _(e):
                    e.memset(kv_acc[:, :], 0.0).then_inc(s_z, 1)
                    e.wait_ge(s_w, 32)
                    for c in range(DC):
                        e.tensor_scalar(wqkv[:, c, :], wqkv[:, c, :], wn1[:, c:c + 1], None,
                                        ALU.mult).then_inc(s_ws, 1)

                    def stage_stats(i, u, h):
                        x_in.wait(e, u, h)
                        for t in range(2):
                            stats.done(e.bn_stats(st[:, u, t, :], xin[:, u, t, :]), f"stats{t}")
                        stats.wait(e, i, "stats1")
                        e.sem_inc(s_held["DVE"], 1)
                        for t in range(2):
                            stats.done(e.bn_aggr(mv[:, u, t, :], st[:, u, t, :]), f"aggr{t}")
                        stats.wait(e, i, "aggr1")
                        root.wait(e, i - 2, "root")
                        stats.done(e.tensor_scalar(pre[:, u, :, 0], mv[:, u, :, 1], 1.0, LN_EPS,
                                                   ALU.mult, ALU.add), "pre0")
                        stats.done(e.tensor_scalar(pre[:, u, :, 1], mv[:, u, :, 1], 1.0 + 1e-6, 1e-6 * LN_EPS,
                                                   ALU.mult, ALU.add), "pre1")

                    def stage_norm(i, u, h):
                        root.wait(e, i, "root")
                        turn.wait(e, i - 2, "xrT")
                        xn_out.wait(e, u, h - 1)
                        for k, dst in enumerate((xn, xr)):
                            for t in range(2):
                                norm.done(e.tensor_scalar(dst[:, u, t, :], xin[:, u, t, :],
                                                          mv[:, u, t, 0:1], rs[:, u, t, k:k + 1],
                                                          ALU.subtract, ALU.mult), f"{('xn', 'xr')[k]}{t}")

                    def stage_feat(i, u, h):
                        kvs.wait(e, i - 2, "kv")
                        acts.wait(e, i, "rk")
                        feat.done(e.scalar_tensor_tensor(k1[:, u, :, :], ek[:, :, :], 1.0, rk[:, :, :],
                                                         ALU.min, ALU.add), "k")
                        acts.wait(e, i, "rq")
                        feat.done(e.scalar_tensor_tensor(qT[:, :, ds(i * BN, BN)], eq[:, :, :], 1.0,
                                                         rq[:, :, :], ALU.min, ALU.add), "q")

                    def stage_acc(i, u, h):
                        kvs.wait(e, i, "kv")
                        if isinstance(i, int) and i == 0:
                            e.wait_ge(s_z, 1)
                        accd.wait(e, i - 1, "acc")
                        accd.done(e.tensor_tensor(kv_acc[:, :], kv_acc[:, :], ps[:, 5, 0:320], ALU.add), "acc")
                    pipeline(e, NB, [(stage_acc, 4), (stage_feat, 3), (stage_norm, 1), (stage_stats, 0)])

                @block.tensor
                def _(e):
                    e.wait_ge(s_ws, DC)

                    def stage_turn(i, u, h):
                        norm.wait(e, i, "xr1")
                        for k, (src, name) in enumerate(((xn, "xnT"), (xr, "xrT"))):
                            copied.wait(e, i - 1, ("cols", "xrT")[k])
                            for c in range(DC):
                                for t in range(2):
                                    at = c * BN + t * TN
                                    mm = e.transpose(ps[:, k, at:at + TN], src[:, u, t, c * P:(c + 1) * P],
                                                     ident[0:TN, 0:TN])
                            turn.done(mm, name)

                    def stage_proj(i, u, h):
                        copied.wait(e, i, "xrT")
                        acts.wait(e, i - 1, "v")
                        for t in range(2):
                            for c in range(DC):
                                mm = e.matmul(ps[0:TN, 2 + t, :], xrT[:, u, c, t * TN:(t + 1) * TN],
                                              wqkv[:, c, D:3 * D], start=(c == 0), stop=(c == DC - 1))
                        proj.done(mm, "k")
                        acts.wait(e, i - 1, "rq")
                        for o in range(DC):
                            for c in range(DC):
                                mm = e.matmul(ps[:, 4, o * BN:(o + 1) * BN], wqkv[:, c, o * P:(o + 1) * P],
                                              xrT[:, u, c, :], start=(c == 0), stop=(c == DC - 1))
                        proj.done(mm, "q")

                    def stage_kv(i, u, h):
                        feat.wait(e, i, "k")
                        acts.wait(e, i, "v")
                        accd.wait(e, i - 1, "acc")
                        for c in range(DC):
                            cs = slice(c * P, (c + 1) * P)
                            for t in range(2):
                                e.matmul(ps[:, 5, cs], v1[:, u, t, cs], k1[:, u, t, cs],
                                         start=(t == 0), stop=(t == 1))
                            for t in range(2):
                                at = DC * P + c * HD0
                                mm = e.matmul(ps[:, 5, at:at + HD0], k1[:, u, t, cs], ones[0:TN, 0:HD0],
                                              start=(t == 0), stop=(t == 1))
                        kvs.done(mm, "kv")
                    pipeline(e, NB, [(stage_kv, 4), (stage_proj, 2), (stage_turn, 1)])

                @block.scalar
                def _(e):
                    def stage_copy(i, u, h):
                        turn.wait(e, i, "xnT")
                        copied.done(e.activation(cols[:, :, ds(i * BN, BN)],
                                                 ps[:, 0, 0:2 * BN].rearrange("p (c n) -> p c n", c=DC),
                                                 ACT.Copy), "cols")
                        turn.wait(e, i, "xrT")
                        proj.wait(e, i - 2, "q")
                        copied.done(e.activation(xrT[:, u, :, :],
                                                 ps[:, 1, 0:2 * BN].rearrange("p (c n) -> p c n", c=DC),
                                                 ACT.Copy), "xrT")

                    def stage_acts(i, u, h):
                        proj.wait(e, i, "k")
                        feat.wait(e, i - 1, "k")
                        acts.done(e.activation(ek[:, :, :], ps[0:TN, 2:4, 0:D], ACT.Exp), "ek")
                        acts.done(e.activation(rk[:, :, :], ps[0:TN, 2:4, 0:D], ACT.Relu), "rk")
                        kvs.wait(e, i - 2, "kv")
                        acts.done(e.activation(v1[:, u, :, :], ps[0:TN, 2:4, D:2 * D], ACT.Copy), "v")
                        proj.wait(e, i, "q")
                        feat.wait(e, i - 1, "q")
                        bank = ps[:, 4, 0:2 * BN].rearrange("p (c n) -> p c n", c=DC)
                        acts.done(e.activation(eq[:, :, :], bank, ACT.Exp), "eq")
                        acts.done(e.activation(rq[:, :, :], bank, ACT.Relu), "rq")
                    pipeline(e, NB, [(stage_acts, 2), (stage_copy, 1)])
            inner.__exit__(None)

            inner = Phase("p2")
            wout = inner.sb("wout", [P, DC, D])
            bout = inner.sb("bout", [TN, D])
            wn2 = inner.sb("wn2", [TN, D])
            diag = inner.sb("diag", [P, P])
            kvd = inner.sb("kvd", [P, DC, P])
            ksd = inner.sb("ksd", [P, DC, P])
            mix = inner.sb("mix", [P, DC, D])
            den = inner.sb("den", [P, 2, DC, BN])
            qz = inner.sb("qz", [P, 2, DC, BN])
            xnr = inner.sb("xnr", [TN, 2, 2, D])
            xr0 = inner.sb("xr0", [TN, 2, 2, D])
            hh = inner.sb("hh", [TN, 2, 2, D])
            sq = inner.sb("sq", [TN, D])
            ss = inner.sb("ss", [TN, 2, 2])
            rr = inner.sb("rr", [TN, 2, 2])
            hw = inner.sb("hw", [TN, 2, 2, D])
            s_w = inner.sem("w")
            s_d = inner.sem("d")
            s_p = inner.sem("p")
            s_m = inner.sem("m")
            xn_in = inner.landing("xn", 2, 2)
            xp_out = inner.landing("xp", 2)
            dens = inner.steps("dens", "den")
            zs = inner.steps("zs", "eps", "inv", "qz")
            outs = inner.steps("outs", "out")
            hsum = inner.steps("hsum", "xb", "h")
            sqs = inner.steps("sqs", "sq0", "sq1")
            msq = inner.steps("msq", "ms")
            roots2 = inner.steps("roots", "root")
            fin = inner.steps("fin", "hw", "hx", "y0", "y1")
            with nc.Block() as block:
                @block.sync
                def _(e):
                    e.dma_start(wout[:, :, :], chunked(A["L0_mix_w_out"])).then_inc(s_w, 16)
                    e.dma_start(bout[:, :], A["L0_mix_b_out"].partition_broadcast(TN)).then_inc(s_w, 16)
                    e.dma_start(wn2[:, :], A["L0_mix_w_norm2"].partition_broadcast(TN)).then_inc(s_w, 16)

                    def load(i, u, h):
                        fin.wait(e, i - 2, "y1")
                        xn_in.start(e.dma_start(xnr[:, u, :, :], rows_of(xn_d, i)), u)
                        xn_in.start(e.dma_start(xr0[:, u, :, :], rows_of(A["x"], i)), u)

                    def store(i, u, h):
                        fin.wait(e, i, "y1")
                        xp_out.start(e.dma_start(rows_of(xp_d, i), hh[:, u, :, :]), u)
                    pipeline(e, NB, [(store, 2), (load, 0)])
                    for u in range(2):
                        xp_out.wait(e, u, (NB - 1 - u) // 2)

                @block.gpsimd
                def _(e):
                    e.memset(diag[:, :], 0.0).then_inc(s_d, 1)
                    e.wait_ge(s_d, 1)
                    for q in range(4):
                        qs = slice(q * HD0, (q + 1) * HD0)
                        e.memset(diag[qs, qs], 1.0).then_inc(s_d, 1)

                    def root(i, u, h):
                        msq.wait(e, i, "ms")
                        roots2.done(e.tensor_tensor(rr[:, u, :], ss[:, u, :], neg_half[0:TN, 0:2], ALU.pow), "root")
                    pipeline(e, NB, [(root, 0)])

                @block.vector
                def _(e):
                    e.wait_ge(s_d, 5)
                    for c in range(DC):
                        e.tensor_tensor(kvd[:, c, :], kv_acc[:, c * P:(c + 1) * P], diag[:, :],
                                        ALU.mult).then_inc(s_p, 1)
                        at = DC * P + c * HD0
                        e.tensor_tensor(ksd[:, c, :].rearrange("p (a b) -> p a b", a=4),
                                        diag[:, :].rearrange("p (a b) -> p a b", a=4),
                                        kv_acc[:, at:at + HD0].unsqueeze(1).broadcast_to([P, 4, HD0]),
                                        ALU.mult).then_inc(s_p, 1)
                    e.wait_ge(s_m, 1)
                    e.tensor_copy(mix[:, :, :], ps[:, 0, :].rearrange("p (c n) -> p c n", c=DC)).then_inc(s_p, 1)
                    e.wait_ge(s_w, 48)

                    def stage_z(i, u, h):
                        dens.wait(e, i, "den")
                        outs.wait(e, i - 2, "out")
                        bank = ps[:, 1, 0:2 * BN].rearrange("p (c n) -> p c n", c=DC)
                        zs.done(e.tensor_scalar(den[:, u, :, :], bank, 1e-6, None, ALU.add), "eps")
                        zs.wait(e, i, "eps")
                        zs.done(e.reciprocal(den[:, u, :, :], den[:, u, :, :]), "inv")
                        zs.wait(e, i, "inv")
                        zs.done(e.tensor_tensor(qz[:, u, :, :], qT[:, :, ds(i * BN, BN)], den[:, u, :, :],
                                                ALU.mult), "qz")

                    def stage_h(i, u, h):
                        xn_in.wait(e, u, h)
                        xp_out.wait(e, u, h - 1)
                        hsum.done(e.tensor_tensor(xnr[:, u, :, :], xnr[:, u, :, :],
                                                  bout[:, :].unsqueeze(1).broadcast_to([TN, 2, D]), ALU.add), "xb")
                        outs.wait(e, i, "out")
                        hsum.wait(e, i, "xb")
                        hsum.done(e.tensor_tensor(hh[:, u, :, :], xnr[:, u, :, :],
                                                  ps[0:TN, 2, :].rearrange("p (t f) -> p t f", t=2), ALU.add), "h")

                    def stage_ms(i, u, h):
                        sqs.wait(e, i, "sq1")
                        msq.done(e.tensor_scalar(ss[:, u, :], ss[:, u, :], 1.0 / D, 1e-6, ALU.mult, ALU.add), "ms")

                    def stage_fin(i, u, h):
                        hsum.wait(e, i, "h")
                        sqs.wait(e, i, "sq1")
                        fin.done(e.tensor_tensor(hw[:, u, :, :], hh[:, u, :, :],
                                                 wn2[:, :].unsqueeze(1).broadcast_to([TN, 2, D]), ALU.mult), "hw")
                        fin.wait(e, i, "hw")
                        fin.done(e.tensor_tensor(hh[:, u, :, :], hh[:, u, :, :], xr0[:, u, :, :], ALU.add), "hx")
                        fin.wait(e, i, "hx")
                        roots2.wait(e, i, "root")
                        for t in range(2):
                            fin.done(e.scalar_tensor_tensor(hh[:, u, t, :], hw[:, u, t, :], rr[:, u, t:t + 1],
                                                            hh[:, u, t, :], ALU.mult, ALU.add), f"y{t}")
                    pipeline(e, NB, [(stage_fin, 3), (stage_ms, 2), (stage_h, 1), (stage_z, 0)])

                @block.scalar
                def _(e):
                    def squares(i, u, h):
                        hsum.wait(e, i, "h")
                        fin.wait(e, i - 2, "y1")
                        for t in range(2):
                            if t:
                                sqs.wait(e, i, "sq0")
                            else:
                                sqs.wait(e, i - 1, "sq1")
                            sqs.done(e.activation(sq[:, :], hh[:, u, t, :], ACT.Square,
                                                  accum_out=ss[:, u, t:t + 1]), f"sq{t}")
                    pipeline(e, NB, [(squares, 0)])

                @block.tensor
                def _(e):
                    e.wait_ge(s_w, 48)
                    e.wait_ge(s_p, 2 * DC)
                    for c in range(DC):
                        mm = e.matmul(ps[:, 0, c * D:(c + 1) * D], kvd[:, c, :], wout[:, c, :], start=True, stop=True)
                    mm.then_inc(s_m, 1)
                    e.wait_ge(s_p, 2 * DC + 1)

                    def stage_den(i, u, h):
                        zs.wait(e, i - 1, "eps")
                        for c in range(DC):
                            mm = e.matmul(ps[:, 1, c * BN:(c + 1) * BN], ksd[:, c, :],
                                          qT[:, c, ds(i * BN, BN)], start=True, stop=True)
                        dens.done(mm, "den")

                    def stage_out(i, u, h):
                        zs.wait(e, i, "qz")
                        hsum.wait(e, i - 1, "h")
                        for t in range(2):
                            for c in range(DC):
                                mm = e.matmul(ps[0:TN, 2, t * D:(t + 1) * D], qz[:, u, c, t * TN:(t + 1) * TN],
                                              mix[:, c, :], start=(c == 0), stop=(c == DC - 1))
                        outs.done(mm, "out")
                    pipeline(e, NB, [(stage_den, 0), (stage_out, 1)])
            inner.__exit__(None)

        def sum_edges(name, rows_d, weighted, add):
            UG = 4
            width = WIN if weighted else P
            parts = 4 if weighted else 1
            with Phase(name) as ph:
                idx = ph.sb("idx", [TN, RR, ST], I32)
                rel = ph.sb("rel", [TN, NG, 2])
                base = ph.sb("base", [1, NG], I32)
                flag = ph.sb("flag", [1, 1], I32)
                now = ph.sb("now", [TN, 2, 4], I32)
                got = ph.sb("got", [TN, 2 * UG, D])
                hot = ph.sb("hot", [TN, 2, 2, width])
                if weighted:
                    wt = ph.sb("wt", [TN, NG, 2, 4])
                    hotw = ph.sb("hotw", [TN, 2, 2, 4, WIN])
                start = ph.sb("start", [TN, 1])
                off = ph.sb("off", [TN, 2])
                s_in, s_z = ph.sem("in"), ph.sem("z")
                landed = ph.landing("got", 2 * UG)
                put = ph.steps("put", "idx")
                ready = ph.steps("ready", *(("hot", "hotw") if weighted else ("hot",)))
                summed = ph.steps("summed", "sums")
                added = ph.steps("added", "add")

                def make_hot(e, pair, u):
                    return e.tensor_tensor(hot[:, u, :, :],
                                           iota[0:TN, 0:width].unsqueeze(1).broadcast_to([TN, 2, width]),
                                           pair.unsqueeze(2).broadcast_to([TN, 2, width]), ALU.is_equal)

                def make_weighted(e, w_pair, u):
                    return [e.tensor_tensor(hotw[:, u, j, :, :],
                                            hot[:, u, j, :].unsqueeze(1).broadcast_to([TN, 4, WIN]),
                                            w_pair[:, j, :].unsqueeze(2).broadcast_to([TN, 4, WIN]), ALU.mult)
                            for j in range(2)]

                def sums(e, b, u, slot):
                    for c in range(DC):
                        for j in range(2):
                            lhs = got[:, slot + j, c * P:(c + 1) * P]
                            if weighted:
                                at, n = (0, 4 * WIN) if c == 0 else (4 * WIN, 3 * WIN)
                                rhs = hotw[:, u, j, :, :].rearrange("p k w -> p (k w)")[:, c * WIN:4 * WIN]
                            else:
                                at, n, rhs = c * P, P, hot[:, u, j, :]
                            mm = e.matmul(ps[:, b, at:at + n], lhs, rhs, start=(j == 0), stop=(j == 1))
                    return mm

                with nc.Block() as block:
                    @block.sync
                    def _(e):
                        loads = [(idx[:, :, :].rearrange("p r s -> p (r s)"), idx_d[0:TN, :]),
                                 (rel[:, :, :].rearrange("p g j -> p (g j)"), rel_d[0:TN, :]),
                                 (base[:, :], base_d), (flag[:, :], flag_d)]
                        if weighted:
                            loads.append((wt[:, :, :, :].rearrange("p g j k -> p (g j k)"), w_d[0:TN, :]))
                        for dst, src in loads:
                            e.dma_start(dst, src).then_inc(s_in, 16)
                        e.wait_ge(s_in, 16 * len(loads))

                    @block.gpsimd
                    def _(e):
                        e.wait_ge(s_in, 16 * (4 + weighted))

                        def gather(i, u, h):
                            summed.wait(e, i - UG, "sums")
                            if u % 2 == 0:
                                for s in range(4):
                                    landed.wait(e, 2 * u + s, h - 1)
                                half = (h * (UG // 2) + u // 2)
                                flat = idx[:, :, :].rearrange("p r s -> p (r s)")
                                put.done(e.tensor_copy(now[:, u // 2, :], flat[:, ds(half * 4, 4)]), "idx")
                                put.wait(e, half, "idx")
                            e.sem_inc(s_held["Pool"], 1)
                            for j in range(2):
                                slot = 2 * u + j
                                landed.start(e.indirect_dma_start(
                                    got[:, slot, :], None, rows_d,
                                    bass.IndirectOffsetOnAxis(ap=now[:, u // 2, slot % 4:slot % 4 + 1], axis=0)), slot)
                        pipeline(e, NG, [(gather, 0)], unroll=UG)

                    @block.vector
                    def _(e):
                        e.wait_ge(s_in, 16 * (4 + weighted))

                        def prepare(i, u, h):
                            summed.wait(e, i - 2, "sums")
                            ready.done(make_hot(e, rel[:, ds(i, 1), :].rearrange("p g j -> p (g j)"), u % 2), "hot")
                            if weighted:
                                ready.wait(e, i, "hot")
                                both = make_weighted(e, wt[:, ds(i, 1), :, :].rearrange("p g j k -> p (g j) k"), u % 2)
                                ready.done(both[1], "hotw")

                        def accumulate(i, u, h):
                            at = e.value_load(base[0:1, ds(i, 1)], min_val=0, max_val=N)
                            summed.wait(e, i, "sums")
                            added.wait(e, i - 1, "add")
                            added.done(add(e, at, u % 2), "add")
                        pipeline(e, NG, [(prepare, 0), (accumulate, 1)], unroll=UG)

                    @block.tensor
                    def _(e):
                        def group(i, u, h):
                            landed.wait(e, 2 * u, h)
                            landed.wait(e, 2 * u + 1, h)
                            ready.wait(e, i, "hotw" if weighted else "hot")
                            added.wait(e, i - 2, "add")
                            summed.done(sums(e, u % 2, u % 2, 2 * u), "sums")
                        pipeline(e, NG, [(group, 0)], unroll=UG)

                NW = (N + WIN - 1) // WIN
                s_l, s_rows, s_hot, s_sum, s_add = (ph.sem(n) for n in ("l", "rows", "hot", "sum", "add"))
                s_idx, s_pe, s_dve, s_chain = (ph.sem(n) for n in ("idx", "go_pe", "go_dve", "chain"))
                with nc.Block() as block:
                    @block.sync
                    def _(e):
                        e.dma_start(rel[:, :, :].rearrange("p g j -> p (g j)"), left_d[0:TN, :]).then_inc(s_l, 16)
                        e.wait_ge(s_l, 16)

                    @block.gpsimd
                    def _(e):
                        some = e.value_load(flag[0:1, 0:1], min_val=0, max_val=E)
                        with e.If(some > 0):
                            with e.Fori(0, NG) as g:
                                flat = idx[:, :, :].rearrange("p r s -> p (r s)")
                                e.tensor_copy(now[:, 0, 0:2], flat[:, ds(g * 2, 2)]).then_inc(s_idx, 1)
                                e.wait_ge(s_idx, 1)
                                for j in range(2):
                                    e.indirect_dma_start(got[:, j, :], None, rows_d, bass.IndirectOffsetOnAxis(
                                        ap=now[:, 0, j:j + 1], axis=0)).then_inc(s_rows, 16)
                                e.sem_inc(s_add, 1)
                                e.wait_ge(s_add, NW + 1)
                                for s in (s_idx, s_hot, s_sum, s_add, s_chain):
                                    e.sem_clear(s)
                                e.sem_inc(s_pe, 1)
                                e.sem_inc(s_dve, 1)

                    @block.tensor
                    def _(e):
                        some = e.value_load(flag[0:1, 0:1], min_val=0, max_val=E)
                        with e.If(some > 0):
                            with e.Fori(0, NG) as g:
                                e.wait_ge(s_rows, g * 32 + 32)
                                e.sem_inc(s_held["PE"], 1)
                                with e.Fori(0, NW) as w:
                                    e.wait_ge(s_add, w + 1)
                                    e.wait_ge(s_hot, w + 1)
                                    sums(e, 0, 0, 0).then_inc(s_sum, 1)
                                e.wait_ge(s_pe, 1)
                                e.sem_clear(s_pe)

                    @block.vector
                    def _(e):
                        e.wait_ge(s_l, 16)
                        some = e.value_load(flag[0:1, 0:1], min_val=0, max_val=E)
                        links = 3 if weighted else 2
                        with e.If(some > 0):
                            with e.Fori(0, NG) as g:
                                e.memset(start[:, :], -float(WIN)).then_inc(s_chain, 1)
                                with e.Fori(0, NW) as w:
                                    e.wait_ge(s_chain, w * links + 1)
                                    e.tensor_scalar(start[:, :], start[:, :], float(WIN), None, ALU.add)\
                                     .then_inc(s_chain, 1)
                                    e.wait_ge(s_chain, w * links + 2)
                                    e.tensor_scalar(off[:, :], rel[:, ds(g, 1), :].rearrange("p g j -> p (g j)"),
                                                    start[:, 0:1], None, ALU.subtract).then_inc(s_chain, 1)
                                    e.wait_ge(s_chain, w * links + 3)
                                    ins = make_hot(e, off[:, :], 0)
                                    if weighted:
                                        ins.then_inc(s_chain, 1)
                                        e.wait_ge(s_chain, w * links + 4)
                                        ins = make_weighted(
                                            e, wt[:, ds(g, 1), :, :].rearrange("p g j k -> p (g j) k"), 0)[1]
                                    ins.then_inc(s_hot, 1)
                                    e.wait_ge(s_sum, w + 1)
                                    add(e, w * WIN, 0).then_inc(s_add, 1)
                                e.wait_ge(s_dve, 1)
                                e.sem_clear(s_dve)


        def add_columns(e, at, bank):
            w = cols[:, :, ds(at, WIN)]
            return e.tensor_tensor(w, w, ps[:, bank, 0:DC * P].rearrange("p (c n) -> p c n", c=DC)[:, :, 0:WIN],
                                   ALU.add)
        sum_edges("p3", xn_d, False, add_columns)

        HC = HID // P
        gin_scale = layer0.enter_context(nc.sbuf_tensor("gin_scale", [P, HC], F32))
        gin_bias = layer0.enter_context(nc.sbuf_tensor("gin_bias", [P, HC], F32))
        with Phase("p4") as ph:
            w1 = ph.sb("w1", [P, DC, HID])
            hid = ph.sb("hid", [P, 2, HC, BN])
            st = ph.sb("st", [P, HC, NB, 6])
            vecs = ph.sb("vecs", [P, 3, HC])
            mv = ph.sb("mv", [P, HC, 2])
            tmp = ph.sb("tmp", [P, 2, HC])
            s_w, s_v, s_p = ph.sem("w"), ph.sem("v"), ph.sem("p")
            up = ph.steps("up", "0", "1", "2", "3")
            outp = ph.steps("copied", "0", "1", "2", "3")
            stat = ph.steps("stat", "stats")
            h_out = ph.landing("h", 2)
            with nc.Block() as block:
                @block.sync
                def _(e):
                    e.dma_start(w1[:, :, :], chunked(A["L0_gnn_W1"])).then_inc(s_w, 16)
                    for k, name in enumerate(("L0_gnn_b1", "L0_gnn_gamma", "L0_gnn_beta")):
                        e.dma_start(vecs[:, k, :], A[name].rearrange("(c p) -> p c", p=P),
                                    allow_slow_non_contiguous=True).then_inc(s_w, 16)

                    def store(i, u, h):
                        outp.wait(e, i, "3")
                        h_out.start(e.dma_start(h1_d[ds(i, 1), :, :].rearrange("b p n -> (b p) n"),
                                                hid[:, u, :, :].rearrange("p c n -> p (c n)")), u)
                    pipeline(e, NB, [(store, 0)])
                    for u in range(2):
                        h_out.wait(e, u, (NB - 1 - u) // 2)

                @block.tensor
                def _(e):
                    e.wait_ge(s_w, 64)

                    def project(i, u, h):
                        for q in range(4):
                            outp.wait(e, i - 2, str(q))
                            for k in range(2):
                                f = (2 * q + k) * P
                                for c in range(DC):
                                    mm = e.matmul(ps[:, 4 * u + q, k * BN:(k + 1) * BN], w1[:, c, f:f + P],
                                                  cols[:, c, ds(i * BN, BN)], start=(c == 0), stop=(c == DC - 1))
                            up.done(mm, str(q))
                    pipeline(e, NB, [(project, 0)])

                @block.scalar
                def _(e):
                    def copy(i, u, h):
                        stat.wait(e, i - 2, "stats")
                        h_out.wait(e, u, h - 1)
                        for q in range(4):
                            up.wait(e, i, str(q))
                            outp.done(e.activation(hid[:, u, 2 * q:2 * q + 2, :],
                                                   ps[:, 4 * u + q, 0:2 * BN].rearrange("p (k n) -> p k n", k=2),
                                                   ACT.Copy), str(q))
                    pipeline(e, NB, [(copy, 0)])

                @block.vector
                def _(e):
                    def stats(i, u, h):
                        for c in range(HC):
                            outp.wait(e, i, str(c // 2))
                            ins = e.bn_stats(st[:, c, ds(i, 1), :].rearrange("p a k -> p (a k)"), hid[:, u, c, :])
                        stat.done(ins, "stats")
                    pipeline(e, NB, [(stats, 0)])
                    stat.wait(e, NB - 1, "stats")
                    box = [0]

                    def step(ins):
                        chained(e, ins, s_v, box)
                    for c in range(HC):
                        step(e.bn_aggr(mv[:, c, :], st[:, c, :, :].rearrange("p b k -> p (b k)")))
                    b1, gamma, beta = (vecs[:, k, :] for k in range(3))
                    step(e.tensor_scalar(tmp[:, 0, :], mv[:, :, 1], 1.0, 1e-5, ALU.mult, ALU.add))
                    e.sem_inc(s_p, 1)
                    e.wait_ge(s_w, 64)
                    step(e.tensor_tensor(mv[:, :, 0], mv[:, :, 0], b1, ALU.add))
                    step(e.tensor_tensor(mv[:, :, 0], b1, mv[:, :, 0], ALU.subtract))
                    e.wait_ge(s_p, 2)
                    step(e.tensor_tensor(gin_scale[:, :], tmp[:, 1, :], gamma, ALU.mult))
                    step(e.tensor_tensor(mv[:, :, 0], mv[:, :, 0], gin_scale[:, :], ALU.mult))
                    step(e.tensor_tensor(gin_bias[:, :], mv[:, :, 0], beta, ALU.add))

                @block.gpsimd
                def _(e):
                    e.wait_ge(s_p, 1)
                    e.tensor_tensor(tmp[:, 1, :], tmp[:, 0, :], neg_half[:, 0:HC], ALU.pow).then_inc(s_p, 1)

        def pick_two(e, step, prob, rank, best, first, keys, picks):
            shape = list(prob.shape)
            ranks = rank.unsqueeze(1).broadcast_to(shape)
            for k in range(2):
                step(e.tensor_reduce(best[:, k, :], prob, AX, ALU.max))
                step(e.tensor_tensor(keys, prob, best[:, k, :].unsqueeze(2).broadcast_to(shape), ALU.is_equal))
                step(e.tensor_tensor(keys, keys, ranks, ALU.mult))
                step(e.tensor_reduce(first[:, k, :], keys, AX, ALU.max))
                step(e.tensor_tensor(picks[:, k, :, :], ranks, first[:, k, :].unsqueeze(2).broadcast_to(shape),
                                     ALU.is_equal))
                if k == 0:
                    step(e.scalar_tensor_tensor(prob, picks[:, k, :, :], -2.0, prob, ALU.mult, ALU.add))

        class RowNorm:

            def __init__(self, ph, name, writes, tiles=2):
                self.tiles = tiles
                self.st = ph.sb(f"{name}_st", [TN, 2, tiles, 6])
                self.mv = ph.sb(f"{name}_mv", [TN, 2, tiles, 2])
                self.pre = ph.sb(f"{name}_pre", [TN, 2, tiles])
                self.rs = ph.sb(f"{name}_rs", [TN, 2, tiles])
                self.stats = ph.steps(f"{name}_stats", *(f"stats{t}" for t in range(tiles)), *(f"aggr{t}" for t in range(tiles)),
                                      "pre")
                self.root = ph.steps(f"{name}_root", "root")
                self.norm = ph.steps(f"{name}_norm", *writes)
                self.last = writes[-1]

            def row_stats(self, e, i, u, x):
                self.norm.wait(e, i - 2, self.last)
                for t in range(self.tiles):
                    self.stats.done(e.bn_stats(self.st[:, u, t, :], x[:, t, :]), f"stats{t}")
                self.stats.wait(e, i, f"stats{self.tiles - 1}")
                e.sem_inc(s_held["DVE"], 1)
                for t in range(self.tiles):
                    self.stats.done(e.bn_aggr(self.mv[:, u, t, :], self.st[:, u, t, :]), f"aggr{t}")
                self.stats.wait(e, i, f"aggr{self.tiles - 1}")
                self.stats.done(e.tensor_scalar(self.pre[:, u, :], self.mv[:, u, :, 1], 1.0, LN_EPS,
                                                ALU.mult, ALU.add), "pre")

            def roots(self, e, i, u):
                self.stats.wait(e, i, "pre")
                self.root.done(e.tensor_tensor(self.rs[:, u, :], self.pre[:, u, :], neg_half[0:TN, 0:self.tiles],
                                               ALU.pow), "root")

            def scaled(self, e, u, t, dst, src):
                return e.tensor_scalar(dst, src, self.mv[:, u, t, 0:1], self.rs[:, u, t:t + 1],
                                       ALU.subtract, ALU.mult)

        routes = layer0.enter_context(nc.sbuf_tensor("routes", [TN, 2 * NB, 8], F32))
        with Phase("p5") as ph:
            hid = ph.sb("hid", [P, 2, HC, BN])
            w2 = ph.sb("w2", [P, HC, D])
            b2 = ph.sb("b2", [TN, D])
            xp = ph.sb("xp", [TN, 2, 2, D])
            gb = ph.sb("gb", [TN, 2, 2, D])
            x1 = ph.sb("x1", [TN, 2, 2, D])
            f1 = ph.sb("f1", [TN, 2, 2, D])
            rw1 = ph.sb("rw1", [P, DC, RH0])
            rb1 = ph.sb("rb1", [P, 1])
            rw2 = ph.sb("rw2", [P, NE0])
            rb2 = ph.sb("rb2", [TN, NE0])
            rh = ph.sb("rh", [P, 2, BN])
            s_w, s_z = ph.sem("w"), ph.sem("z")
            h_in, xp_in, x1_out = ph.landing("h", 2), ph.landing("xp", 2), ph.landing("x1", 2)
            relu = ph.steps("relu", *(str(c) for c in range(HC)))
            down = ph.steps("down", "rows")
            sums1 = ph.steps("sums", "b2", "x1")
            ln = RowNorm(ph, "ln", ("f0", "f1"))
            turn = ph.steps("turn", "turn")
            copied = ph.steps("copied", "cols")
            rhid = ph.steps("rhid", "rh")
            ract = ph.steps("ract", "relu")
            logit = ph.steps("logit", "logits")
            kept = ph.steps("kept", "logits")
            with nc.Block() as block:
                @block.sync
                def _(e):
                    loads = [(w2[:, :, :], chunked(A["L0_gnn_W2"])),
                             (b2[:, :], A["L0_gnn_b2"].partition_broadcast(TN)),
                             (rw1[:, :, :], chunked(A["L0_ffn_router_w1"])),
                             (rb1[:, :], A["L0_ffn_router_b1"].rearrange("(p a) -> p a", a=1)),
                             (rw2[:, :], A["L0_ffn_router_w2"]),
                             (rb2[:, :], A["L0_ffn_router_b2"].partition_broadcast(TN))]
                    for dst, src in loads:
                        e.dma_start(dst, src).then_inc(s_w, 16)

                    def load(i, u, h):
                        down.wait(e, i - 2, "rows")
                        h_in.start(e.dma_start(hid[:, u, :, :].rearrange("p c n -> p (c n)"),
                                               h1_d[ds(i, 1), :, :].rearrange("b p n -> (b p) n")), u)
                        sums1.wait(e, i - 2, "x1")
                        xp_in.start(e.dma_start(xp[:, u, :, :], rows_of(xp_d, i)), u)

                    def store(i, u, h):
                        sums1.wait(e, i, "x1")
                        x1_out.start(e.dma_start(rows_of(x1_d, i), x1[:, u, :, :]), u)
                    pipeline(e, NB, [(load, 0), (store, 3)])
                    for u in range(2):
                        x1_out.wait(e, u, (NB - 1 - u) // 2)

                @block.scalar
                def _(e):
                    def bn_relu(i, u, h):
                        h_in.wait(e, u, h)
                        for c in range(HC):
                            relu.done(e.activation(hid[:, u, c, :], hid[:, u, c, :], ACT.Relu,
                                                   bias=gin_bias[:, c:c + 1], scale=gin_scale[:, c:c + 1]), str(c))

                    def copy(i, u, h):
                        turn.wait(e, i, "turn")
                        copied.done(e.activation(cols[:, :, ds(i * BN, BN)],
                                                 ps[:, 2, 0:2 * BN].rearrange("p (c n) -> p c n", c=DC),
                                                 ACT.Copy), "cols")

                    def router_relu(i, u, h):
                        rhid.wait(e, i, "rh")
                        logit.wait(e, i - 2, "logits")
                        ract.done(e.activation(rh[:, u, :], ps[:, 3, 0:BN], ACT.Relu, bias=rb1[:, 0:1]), "relu")
                    e.wait_ge(s_w, 96)
                    pipeline(e, NB, [(router_relu, 4), (copy, 3), (bn_relu, 0)])

                @block.tensor
                def _(e):
                    e.wait_ge(s_w, 96)

                    def rows(i, u, h):
                        sums1.wait(e, i - 2, "b2")
                        for t in range(2):
                            for c in range(HC):
                                if t == 0:
                                    relu.wait(e, i, str(c))
                                mm = e.matmul(ps[0:TN, u, t * D:(t + 1) * D], hid[:, u, c, t * TN:(t + 1) * TN],
                                              w2[:, c, :], start=(c == 0), stop=(c == HC - 1))
                        down.done(mm, "rows")

                    def turned(i, u, h):
                        ln.norm.wait(e, i, "f1")
                        copied.wait(e, i - 1, "cols")
                        for c in range(DC):
                            for t in range(2):
                                at = c * BN + t * TN
                                mm = e.transpose(ps[:, 2, at:at + TN], f1[:, u, t, c * P:(c + 1) * P],
                                                 ident[0:TN, 0:TN])
                        turn.done(mm, "turn")

                    def router(i, u, h):
                        copied.wait(e, i, "cols")
                        ract.wait(e, i - 1, "relu")
                        for c in range(DC):
                            mm = e.matmul(ps[:, 3, 0:BN], rw1[:, c, :], cols[:, c, ds(i * BN, BN)],
                                          start=(c == 0), stop=(c == DC - 1))
                        rhid.done(mm, "rh")

                    def logits(i, u, h):
                        ract.wait(e, i, "relu")
                        kept.wait(e, i - 1, "logits")
                        for t in range(2):
                            mm = e.matmul(ps[0:TN, 4, t * 8:t * 8 + NE0], rh[:, u, t * TN:(t + 1) * TN], rw2[:, :],
                                          start=True, stop=True)
                        logit.done(mm, "logits")
                    pipeline(e, NB, [(logits, 5), (router, 4), (turned, 3), (rows, 1)])

                @block.gpsimd
                def _(e):
                    pipeline(e, NB, [(lambda i, u, h: ln.roots(e, i, u), 0)])

                @block.vector
                def _(e):
                    e.memset(routes[:, :, :], 0.0).then_inc(s_z, 1)
                    e.wait_ge(s_z, 1)
                    e.wait_ge(s_w, 96)

                    def x1_of(i, u, h):
                        down.wait(e, i, "rows")
                        sums1.done(e.tensor_tensor(gb[:, u, :, :], ps[0:TN, u, :].rearrange("p (t f) -> p t f", t=2),
                                                   b2[:, :].unsqueeze(1).broadcast_to([TN, 2, D]), ALU.add), "b2")
                        sums1.wait(e, i, "b2")
                        xp_in.wait(e, u, h)
                        x1_out.wait(e, u, h - 1)
                        sums1.done(e.scalar_tensor_tensor(x1[:, u, :, :], gb[:, u, :, :], 0.0, xp[:, u, :, :],
                                                          ALU.max, ALU.add), "x1")
                        sums1.wait(e, i, "x1")
                        ln.row_stats(e, i, u, x1[:, u, :, :])

                    def f1_of(i, u, h):
                        ln.root.wait(e, i, "root")
                        turn.wait(e, i - 2, "turn")
                        for t in range(2):
                            ln.norm.done(ln.scaled(e, u, t, f1[:, u, t, :], x1[:, u, t, :]), f"f{t}")

                    def keep(i, u, h):
                        logit.wait(e, i, "logits")
                        kept.done(e.tensor_tensor(routes[:, ds(i * 2, 2), 0:NE0],
                                                  ps[0:TN, 4, 0:16].rearrange("p (t k) -> p t k", t=2)[:, :, 0:NE0],
                                                  rb2[:, :].unsqueeze(1).broadcast_to([TN, 2, NE0]), ALU.add),
                                  "logits")
                    pipeline(e, NB, [(keep, 5), (f1_of, 2), (x1_of, 1)])

        with Phase("p5r") as ph:
            NT = 2 * NB
            big = ph.sb("big", [TN, NT])
            ex = ph.sb("ex", [TN, NT, NE0])
            prob = ph.sb("prob", [TN, NT, NE0])
            best = ph.sb("best", [TN, 2, NT])
            first = ph.sb("first", [TN, 2, NT])
            gate = ph.sb("gate", [TN, NT, 2])
            rank = ph.sb("rank", [TN, NE0])
            picks = ph.sb("picks", [TN, 2, NT, NE0])
            keys = ph.sb("keys", [TN, NT, NE0])
            one = ph.sb("one", [TN, NT])
            s_v, s_e = ph.sem("v"), ph.sem("e")
            with nc.Block() as block:
                @block.vector
                def _(e):
                    box = [0]

                    def step(ins):
                        chained(e, ins, s_v, box)

                    def per_expert(x):
                        return x.unsqueeze(2).broadcast_to([TN, NT, NE0])
                    step(e.tensor_scalar(rank[:, :], iota[0:TN, 0:NE0], -1.0, 8.0, ALU.mult, ALU.add))
                    step(e.tensor_reduce(big[:, :], routes[:, :, 0:NE0], AX, ALU.max))
                    step(e.tensor_tensor(ex[:, :, :], routes[:, :, 0:NE0], per_expert(big[:, :]), ALU.subtract))
                    e.sem_inc(s_e, 1)
                    e.wait_ge(s_e, 2)
                    step(e.tensor_reduce(big[:, :], ex[:, :, :], AX, ALU.add))
                    step(e.reciprocal(big[:, :], big[:, :]))
                    step(e.tensor_tensor(prob[:, :, :], ex[:, :, :], per_expert(big[:, :]), ALU.mult))
                    pick_two(e, step, prob[:, :, :], rank[:, :], best[:, :, :], first[:, :, :], keys[:, :, :],
                             picks[:, :, :, :])
                    step(e.tensor_tensor(one[:, :], best[:, 1, :], best[:, 0, :], ALU.subtract))
                    e.sem_inc(s_e, 1)
                    e.wait_ge(s_e, 4)
                    step(e.tensor_scalar(big[:, :], gate[:, :, 1], 1.0, None, ALU.add))
                    step(e.reciprocal(gate[:, :, 0], big[:, :]))
                    step(e.tensor_tensor(gate[:, :, 1], gate[:, :, 1], gate[:, :, 0], ALU.mult))
                    for k in range(2):
                        step(e.tensor_tensor(picks[:, k, :, :], picks[:, k, :, :], per_expert(gate[:, :, k]), ALU.mult))
                    step(e.tensor_tensor(routes[:, :, 0:NE0], picks[:, 0, :, :], picks[:, 1, :, :], ALU.add))

                @block.scalar
                def _(e):
                    e.wait_ge(s_e, 1)
                    e.activation(ex[:, :, :], ex[:, :, :], ACT.Exp).then_inc(s_e, 1)
                    e.wait_ge(s_e, 3)
                    e.activation(gate[:, :, 1], one[:, :], ACT.Exp).then_inc(s_e, 1)

        with Phase("p6") as ph:
            LA, LB, LC = 2, 3, 4
            NE = NE0
            ws = [ph.sb(f"w{k}", [P, NE, DC, D]) for k in range(3)]
            b3 = ph.sb("b3", [NE, D])
            bs = ph.sb("bs", [P, 2, NE, DC])
            x1 = ph.sb("x1", [TN, 2, 2, D])
            acc = ph.sb("acc", [TN, 2, 2, D])
            wcur = ph.sb("wcur", [TN, 2, 2, 8])
            wT = ph.sb("wT", [NE, 2, BN])
            h1 = ph.sb("h1", [P, 2, DC, BN])
            h2 = ph.sb("h2", [P, 2, DC, BN])
            xm = ph.sb("xm", [TN, 2, 2, D])
            xmT = ph.sb("xmT", [P, 2, DC * BN])
            s_w = ph.sem("w")
            x_in, x_out, m_out, t_out = (ph.landing(n, 2) for n in ("xi", "xo", "mo", "to"))
            cur = ph.steps("cur", "w")
            wturn = ph.steps("wturn", "t")
            wcopy = ph.steps("wcopy", "c")
            bias3 = ph.steps("bias3", "b3")
            init = ph.steps("init", "x1")
            up = [ph.steps(n, "mm") for n in ("a", "b", "c")]
            act = [ph.steps(n, "c0", "c1") for n in ("ra", "rb")]
            mixed = ph.steps("mixed", "t0", "t1")
            ln = RowNorm(ph, "ln", ("s0", "v0", "s1", "v1"))
            turn = ph.steps("turn", "turn")
            copied = ph.steps("copied", "T")
            NLOAD = 3 + 1 + 2 * NE * DC
            with nc.Block() as block:
                @block.sync
                def _(e):
                    for k in range(3):
                        e.dma_start(ws[k][:, :, :, :].rearrange("p e c n -> p (e c) n"),
                                    A[f"L0_ffn_expert_w{k + 1}"].rearrange("e (c p) n -> p (e c) n", p=P))\
                         .then_inc(s_w, 16)
                    e.dma_start(b3[:, :], A["L0_ffn_expert_b3"]).then_inc(s_w, 16)
                    for k in range(2):
                        for x in range(NE):
                            for c in range(DC):
                                e.dma_start(bs[:, k, x, c:c + 1],
                                            A[f"L0_ffn_expert_b{k + 1}"][x:x + 1, c * P:(c + 1) * P]
                                            .rearrange("a p -> p a")).then_inc(s_w, 16)

                    def load(i, u, h):
                        init.wait(e, i - 2, "x1")
                        x_in.start(e.dma_start(x1[:, u, :, :], rows_of(x1_d, i)), u)

                    def store(i, u, h):
                        mixed.wait(e, i * NE + NE - 1, "t1")
                        x_out.start(e.dma_start(rows_of(x2_d, i), acc[:, u, :, :]), u)
                        ln.norm.wait(e, i, "v1")
                        m_out.start(e.dma_start(rows_of(xm_d, i), xm[:, u, :, :]), u)
                        copied.wait(e, i, "T")
                        t_out.start(e.dma_start(xmT_d[ds(i, 1), :, :].rearrange("b p n -> (b p) n"),
                                                xmT[:, u, :]), u)
                    pipeline(e, NB, [(load, 0), (store, 1)])
                    for u in range(2):
                        for s in (x_out, m_out, t_out):
                            s.wait(e, u, (NB - 1 - u) // 2)

                def at_block(when, fn):
                    def stage(m, u, h):
                        if u % NE == when:
                            fn(h * 2 + u // NE, u // NE, h)
                    return stage

                def experts(e, stages):
                    pipeline(e, NB * NE, stages, unroll=2 * NE)

                @block.scalar
                def _(e):
                    e.wait_ge(s_w, 16 * NLOAD)

                    def wt_copy(i, u, h):
                        wturn.wait(e, i, "t")
                        bias3.wait(e, i - 2, "b3")
                        wcopy.done(e.activation(wT[:, u, :], ps[0:NE, 6, 0:BN], ACT.Copy), "c")

                    def relu(k, hk):
                        def stage(m, u, h):
                            up[k].wait(e, m, "mm")
                            up[k + 1].wait(e, m - 2, "mm")
                            for c in range(DC):
                                act[k].done(e.activation(hk[:, u % 2, c, :],
                                                         ps[:, 2 * k + u % 2, c * BN:(c + 1) * BN], ACT.Relu,
                                                         bias=bs[:, k, u % NE, c:c + 1]), f"c{c}")
                        return stage

                    def copy(i, u, h):
                        turn.wait(e, i, "turn")
                        t_out.wait(e, u, h - 1)
                        copied.done(e.activation(xmT[:, u, :], ps[:, 6, 0:2 * BN], ACT.Copy), "T")
                    experts(e, [(at_block(NE - 1, copy), 6), (relu(1, h2), LB), (relu(0, h1), LA),
                                (at_block(0, wt_copy), 0)])

                @block.tensor
                def _(e):
                    e.wait_ge(s_w, 16 * NLOAD)

                    def w_turn(i, u, h):
                        cur.wait(e, i, "w")
                        copied.wait(e, i - 2, "T")
                        for t in range(2):
                            mm = e.transpose(ps[0:NE, 6, t * TN:(t + 1) * TN], wcur[:, u, t, 0:NE],
                                             ident[0:TN, 0:TN])
                        wturn.done(mm, "t")

                    def w_bias(i, u, h):
                        wcopy.wait(e, i, "c")
                        init.wait(e, i - 1, "x1")
                        for t in range(2):
                            mm = e.matmul(ps[0:TN, 7, t * D:(t + 1) * D], wT[:, u, t * TN:(t + 1) * TN], b3[:, :],
                                          start=True, stop=True)
                        bias3.done(mm, "b3")

                    def layer_a(m, u, h):
                        act[0].wait(e, m - 2, "c1")
                        i = h * 2 + u // NE
                        for o in range(DC):
                            for c in range(DC):
                                mm = e.matmul(ps[:, u % 2, o * BN:(o + 1) * BN],
                                              ws[0][:, u % NE, c, o * P:(o + 1) * P], cols[:, c, ds(i * BN, BN)],
                                              start=(c == 0), stop=(c == DC - 1))
                        up[0].done(mm, "mm")

                    def layer_b(m, u, h):
                        act[1].wait(e, m - 2, "c1")
                        act[0].wait(e, m, "c1")
                        for o in range(DC):
                            for c in range(DC):
                                mm = e.matmul(ps[:, 2 + u % 2, o * BN:(o + 1) * BN],
                                              ws[1][:, u % NE, c, o * P:(o + 1) * P], h1[:, u % 2, c, :],
                                              start=(c == 0), stop=(c == DC - 1))
                        up[1].done(mm, "mm")

                    def layer_c(m, u, h):
                        mixed.wait(e, m - 2, "t1")
                        act[1].wait(e, m, "c1")
                        for t in range(2):
                            for c in range(DC):
                                mm = e.matmul(ps[0:TN, 4 + u % 2, t * D:(t + 1) * D],
                                              h2[:, u % 2, c, t * TN:(t + 1) * TN], ws[2][:, u % NE, c, :],
                                              start=(c == 0), stop=(c == DC - 1))
                        up[2].done(mm, "mm")

                    def turned(i, u, h):
                        ln.norm.wait(e, i, "v1")
                        wcopy.wait(e, i + 1 if not isinstance(i, int) or i + 1 < NB else i, "c")
                        for c in range(DC):
                            for t in range(2):
                                at = c * BN + t * TN
                                mm = e.transpose(ps[:, 6, at:at + TN], xm[:, u, t, c * P:(c + 1) * P],
                                                 ident[0:TN, 0:TN])
                        turn.done(mm, "turn")
                    experts(e, [(at_block(NE - 1, turned), 6), (layer_c, LC), (layer_b, LB), (layer_a, LA),
                                (at_block(0, w_bias), 1), (at_block(0, w_turn), 0)])

                @block.gpsimd
                def _(e):
                    pipeline(e, NB, [(lambda i, u, h: ln.roots(e, i, u), 0)])

                @block.vector
                def _(e):
                    def current(i, u, h):
                        mixed.wait(e, i * NE - NE - 1, "t1")
                        wturn.wait(e, i - 2, "t")
                        cur.done(e.tensor_copy(wcur[:, u, :, :], routes[:, ds(i * 2, 2), :]), "w")

                    def begin(i, u, h):
                        bias3.wait(e, i, "b3")
                        x_in.wait(e, u, h)
                        x_out.wait(e, u, h - 1)
                        init.done(e.tensor_tensor(acc[:, u, :, :], ps[0:TN, 7, :].rearrange("p (t f) -> p t f", t=2),
                                                  x1[:, u, :, :], ALU.add), "x1")

                    def weigh(m, u, h):
                        b = u // NE
                        if u % NE == 0:
                            init.wait(e, h * 2 + b, "x1")
                        else:
                            mixed.wait(e, m - 1, "t1")
                        up[2].wait(e, m, "mm")
                        for t in range(2):
                            mixed.done(e.scalar_tensor_tensor(acc[:, b, t, :], ps[0:TN, 4 + u % 2, t * D:(t + 1) * D],
                                                              wcur[:, b, t, u % NE:u % NE + 1], acc[:, b, t, :],
                                                              ALU.mult, ALU.add), f"t{t}")

                    def row_stats(i, u, h):
                        mixed.wait(e, i * NE + NE - 1, "t1")
                        ln.row_stats(e, i, u, acc[:, u, :, :])

                    def normed(i, u, h):
                        ln.root.wait(e, i, "root")
                        turn.wait(e, i - 2, "turn")
                        m_out.wait(e, u, h - 1)
                        for t in range(2):
                            ln.norm.done(ln.scaled(e, u, t, xm[:, u, t, 0:MUL], acc[:, u, t, 0:MUL]), f"s{t}")
                            ln.norm.done(ln.scaled(e, u, t, xm[:, u, t, MUL:D].rearrange("p (m i) -> p i m", m=3),
                                                   acc[:, u, t, MUL:D].rearrange("p (i m) -> p i m", m=3)), f"v{t}")
                    experts(e, [(at_block(NE - 1, normed), 5), (weigh, LC), (at_block(NE - 1, row_stats), LC),
                                (at_block(0, begin), 2), (at_block(0, current), 0)])
        layer0.close()

        INNER = H1 * HD1
        IC = INNER // P
        with Phase("p7") as ph:
            wkv = ph.sb("wkv", [P, DC, 2 * INNER])
            wq = ph.sb("wq", [P, IC, D])
            wo = ph.sb("wo", [P, IC, D])
            means = ph.sb("means", [P, DC * 2 * H1])
            same = ph.sb("same", [P, P])
            xmT = ph.sb("xmT", [P, 2, DC * BN])
            sq = ph.sb("sq", [TN, 2, 2 * H1, HD1])
            v1 = ph.sb("v1", [TN, 2, INNER])
            k1 = ph.sb("k1", [TN, 2, INNER])
            ms = ph.sb("ms", [TN, 2, 2 * H1])
            pr = ph.sb("pr", [TN, 2, H1])
            rs = ph.sb("rs", [TN, 2, H1])
            acc = ph.sb("acc", [P, IC, P])
            a1 = ph.sb("a1", [P, IC, D])
            mix1 = ph.sb("mix1", [P, DC, D])
            s_w, s_p, s_z, s_f, s_m, s_o = (ph.sem(n) for n in ("w", "p", "z", "f", "m", "o"))
            x_in = ph.landing("x", 2)
            proj = ph.steps("proj", "k", "v")
            squares = ph.steps("sq", "k", "v", "copy")
            sizes = ph.steps("sizes", "sum", "mean", "prod")
            root = ph.steps("root", "root")
            kn = ph.steps("kn", "k")
            dots = ph.steps("dots", "dots")
            accd = ph.steps("accd", "acc")
            with nc.Block() as block:
                @block.sync
                def _(e):
                    for dst, src in ((wkv[:, :, :], chunked(A["L1_mix_WkvT"])), (wq[:, :, :], chunked(A["L1_mix_Wq"])),
                                     (wo[:, :, :], chunked(A["L1_mix_WoutT"]))):
                        e.dma_start(dst, src).then_inc(s_w, 16)

                    def load(i, u, h):
                        proj.wait(e, 2 * (i - 2) + 1, "v")
                        x_in.start(e.dma_start(xmT[:, u, :], xmT_d[ds(i, 1), :, :].rearrange("b p n -> (b p) n")), u)
                    pipeline(e, NB, [(load, 0)])
                    e.wait_ge(s_f, 3)
                    e.dma_start(mix1_d, mix1[:, :, :].rearrange("p c n -> p (c n)")).then_inc(s_o, 16)
                    e.wait_ge(s_o, 16)

                @block.gpsimd
                def _(e):
                    e.memset(same[:, :], 0.0).then_inc(s_z, 1)
                    e.wait_ge(s_z, 1)
                    for q in range(2):
                        qs = slice(q * HD1, (q + 1) * HD1)
                        e.memset(same[qs, qs], 1.0 / N).then_inc(s_z, 1)
                    e.wait_ge(s_z, 3)

                    def roots(i, u, h):
                        sizes.wait(e, i, "prod")
                        kn.wait(e, i - 2, "k")
                        root.done(e.tensor_tensor(rs[:, u % 2, :], pr[:, u % 2, :], neg_half[0:TN, 0:H1], ALU.pow),
                                  "root")
                    pipeline(e, 2 * NB, [(roots, 0)], unroll=4)

                @block.tensor
                def _(e):
                    e.wait_ge(s_p, 3)

                    def project(i, u, h):
                        if u % 2 == 0:
                            x_in.wait(e, u // 2, h)
                        t = (u // 2, u % 2)
                        for k, name in enumerate("kv"):
                            if k == 0:
                                kn.wait(e, i - 2, "k")
                            else:
                                squares.wait(e, i - 2, "copy")
                            for c in range(DC):
                                at = c * BN + t[1] * TN
                                mm = e.matmul(ps[0:TN, 2 * k + u % 2, :], xmT[:, t[0], at:at + TN],
                                              wkv[:, c, k * INNER:(k + 1) * INNER], start=(c == 0), stop=(c == DC - 1))
                            proj.done(mm, name)

                    def products(i, u, h):
                        kn.wait(e, i, "k")
                        squares.wait(e, i, "copy")
                        accd.wait(e, i - 2, "acc")
                        for j in range(IC):
                            js = slice(j * P, (j + 1) * P)
                            mm = e.matmul(ps[:, 4 + u % 2, js], v1[:, u % 2, js], k1[:, u % 2, js],
                                          start=True, stop=True)
                        dots.done(mm, "dots")
                    pipeline(e, 2 * NB, [(products, 2), (project, 0)], unroll=4)
                    e.wait_ge(s_f, 1)
                    for j in range(IC):
                        mm = e.matmul(ps[:, 6 + j // 2, (j % 2) * D:(j % 2 + 1) * D], acc[:, j, :], wo[:, j, :],
                                      start=True, stop=True)
                    mm.then_inc(s_m, 1)
                    e.wait_ge(s_f, 2)
                    for c in range(DC):
                        for j in range(IC):
                            mm = e.matmul(ps[:, 0, c * D:(c + 1) * D], wq[:, j, c * P:(c + 1) * P], a1[:, j, :],
                                          start=(j == 0), stop=(j == IC - 1))
                    mm.then_inc(s_m, 1)

                @block.scalar
                def _(e):
                    def stage(i, u, h):
                        p = u % 2
                        sizes.wait(e, i - 2, "sum")
                        dots.wait(e, i - 2, "dots")
                        proj.wait(e, i, "k")
                        squares.done(e.activation(sq[:, p, 0:H1, :].rearrange("p h d -> p (h d)"), ps[0:TN, p, :],
                                                  ACT.Square), "k")
                        proj.wait(e, i, "v")
                        squares.done(e.activation(sq[:, p, H1:2 * H1, :].rearrange("p h d -> p (h d)"),
                                                  ps[0:TN, 2 + p, :], ACT.Square), "v")
                        squares.done(e.activation(v1[:, p, :], ps[0:TN, 2 + p, :], ACT.Copy), "copy")
                    pipeline(e, 2 * NB, [(stage, 0)], unroll=4)

                @block.vector
                def _(e):
                    e.memset(acc[:, :, :], 0.0).then_inc(s_p, 1)
                    e.wait_ge(s_w, 48)
                    heads = wkv[:, :, :].rearrange("p c (h d) -> p (c h) d", d=HD1)
                    e.tensor_reduce(means[:, :], heads, AX, ALU.add).then_inc(s_p, 1)
                    e.wait_ge(s_p, 2)
                    e.scalar_tensor_tensor(heads, means[:, :].unsqueeze(2).broadcast_to([P, DC * 2 * H1, HD1]),
                                           -1.0 / HD1, heads, ALU.mult, ALU.add).then_inc(s_p, 1)

                    def size(i, u, h):
                        p = u % 2
                        squares.wait(e, i, "v")
                        root.wait(e, i - 2, "root")
                        sizes.done(e.tensor_reduce(ms[:, p, :], sq[:, p, :, :], AX, ALU.add), "sum")
                        sizes.wait(e, i, "sum")
                        sizes.done(e.tensor_scalar(ms[:, p, :], ms[:, p, :], 1.0 / HD1, 1e-5, ALU.mult, ALU.add),
                                   "mean")
                        sizes.wait(e, i, "mean")
                        sizes.done(e.tensor_tensor(pr[:, p, :], ms[:, p, 0:H1], ms[:, p, H1:2 * H1], ALU.mult),
                                   "prod")

                    def scale_k(i, u, h):
                        p = u % 2
                        root.wait(e, i, "root")
                        squares.wait(e, i, "k")
                        dots.wait(e, i - 2, "dots")
                        kn.done(e.tensor_tensor(k1[:, p, :].rearrange("p (h d) -> p h d", h=H1),
                                                ps[0:TN, p, :].rearrange("p (h d) -> p h d", h=H1),
                                                rs[:, p, :].unsqueeze(2).broadcast_to([TN, H1, HD1]), ALU.mult), "k")

                    def accumulate(i, u, h):
                        dots.wait(e, i, "dots")
                        accd.wait(e, i - 1, "acc")
                        flat = acc[:, :, :].rearrange("p j d -> p (j d)")
                        accd.done(e.tensor_tensor(flat, flat, ps[:, 4 + u % 2, :], ALU.add), "acc")
                    pipeline(e, 2 * NB, [(accumulate, 2), (scale_k, 1), (size, 0)], unroll=4)
                    accd.wait(e, 2 * NB - 1, "acc")
                    e.wait_ge(s_z, 3)
                    e.tensor_tensor(acc[:, :, :], acc[:, :, :],
                                    same[:, :].unsqueeze(1).broadcast_to([P, IC, P]), ALU.mult).then_inc(s_f, 1)
                    e.wait_ge(s_m, 1)
                    e.tensor_copy(a1[:, :, :], ps[:, 6:8, :].rearrange("p b (k n) -> p (b k) n", k=2)).then_inc(s_f, 1)
                    e.wait_ge(s_m, 2)
                    e.tensor_copy(mix1[:, :, :], ps[:, 0, :].rearrange("p (c n) -> p c n", c=DC)).then_inc(s_f, 1)

        layer1 = ExitStack()
        SL = 7
        msg = layer1.enter_context(nc.sbuf_tensor("msg", [P, SL, NPAD], F32))
        s_mz = sem("msg_zero")
        with nc.Block() as block:
            @block.vector
            def _(e):
                e.memset(msg[:, 0:4, :], 0.0).then_inc(s_mz, 1)

            @block.gpsimd
            def _(e):
                e.memset(msg[:, 4:SL, :], 0.0).then_inc(s_mz, 1)
                e.wait_ge(s_mz, 2)

        def add_messages(e, at, bank):
            w = msg[:, :, ds(at, WIN)]
            return e.tensor_tensor(w, w, ps[:, bank, 0:SL * WIN].rearrange("p (k n) -> p k n", k=SL), ALU.add)
        sum_edges("p8", xm_d, True, add_messages)

        with Phase("p9") as ph:
            wm = ph.sb("wm", [P, SL, D])
            mix1 = ph.sb("mix1", [P, DC, D])
            parts = ph.sb("parts", [P, 4, MUL])
            bout = ph.sb("bout", [TN, D])
            mt = ph.sb("mt", [P, 2, SL, TN])
            xmT = ph.sb("xmT", [P, 2, DC, TN])
            x2 = ph.sb("x2", [TN, 2, D])
            xb = ph.sb("xb", [TN, 2, D])
            x3 = ph.sb("x3", [TN, 2, D])
            f3 = ph.sb("f3", [TN, 2, D])
            f3T = ph.sb("f3T", [P, 2, DC, TN])
            fsum = ph.sb("fsum", [P, DC, 2 * NB])
            s_w, s_z, s_p, s_o = (ph.sem(n) for n in ("w", "z", "p", "o"))
            x_in = ph.landing("xi", 2, 2)
            x_out, f_out, t_out = (ph.landing(n, 2) for n in ("xo", "fo", "to"))
            fixed = ph.steps("fixed", "msg")
            rows = ph.steps("rows", "rows")
            sums3 = ph.steps("sums", "xb", "x3")
            ln = RowNorm(ph, "ln", ("f",), tiles=1)
            turn = ph.steps("turn", "turn")
            copied = ph.steps("copied", "c0", "c1")
            ALPHA = (2.0 * MUL) ** -0.5 / 4.0
            LO, HI = slice(0, MUL), slice(MUL, 2 * MUL)
            W00, W11, W01, W10 = range(4)
            MAPS = [(0, LO, W01, 1.0, 1), (0, HI, W11, 3.0 ** -0.5, 0),
                    (1, LO, W00, 1.0, 0), (1, HI, W10, 1.0, 1),
                    (2, LO, W01, 1.0, 2), (3, LO, W01, 1.0, 3),
                    (4, LO, W10, 1.0, 2), (4, HI, W10, 1.0, 3),
                    (5, LO, W11, 3.0 ** -0.5, 0), (6, HI, W11, 3.0 ** -0.5, 0)]

            def tile_of(dram, i):
                return dram[ds(i * TN, TN), :]
            with nc.Block() as block:
                @block.sync
                def _(e):
                    for k, name in enumerate(("00_0", "11_0", "01_1", "10_1")):
                        for half in (LO, HI):
                            e.dma_start(parts[half, k, :], A[f"L1_gnn_w_{name}"]).then_inc(s_w, 16)
                    e.dma_start(bout[:, :], A["L1_mix_bout"].partition_broadcast(TN)).then_inc(s_w, 16)
                    e.dma_start(mix1[:, :, :].rearrange("p c n -> p (c n)"), mix1_d).then_inc(s_w, 16)

                    def load(i, u, h):
                        rows.wait(e, i - 2, "rows")
                        x_in.start(e.dma_start(xmT[:, u, :, :],
                                               xmT_d[ds(h, 1), :, :].rearrange("b p (c t n) -> (b p) c t n", c=DC, t=2)
                                               [:, :, u, :]), u)
                        sums3.wait(e, i - 2, "xb")
                        x_in.start(e.dma_start(x2[:, u, :], tile_of(x2_d, i)), u)

                    def store(i, u, h):
                        sums3.wait(e, i, "x3")
                        x_out.start(e.dma_start(tile_of(x3_d, i), x3[:, u, :]), u)
                        ln.norm.wait(e, i, "f")
                        f_out.start(e.dma_start(tile_of(f3_d, i), f3[:, u, :]), u)
                        copied.wait(e, i, "c1")
                        t_out.start(e.dma_start(f3T_d[ds(i, 1), :, :].rearrange("b p n -> (b p) n"),
                                                f3T[:, u, :, :].rearrange("p c n -> p (c n)")), u)
                    pipeline(e, 2 * NB, [(load, 0), (store, 3)])
                    for u in range(2):
                        for s in (x_out, f_out, t_out):
                            s.wait(e, u, NB - 1)
                    e.dma_start(fsum_d, fsum[:, :, :].rearrange("p c n -> p (c n)")).then_inc(s_o, 16)
                    e.wait_ge(s_o, 16)

                @block.gpsimd
                def _(e):
                    e.memset(wm[:, :, :], 0.0).then_inc(s_z, 1)
                    e.wait_ge(s_z, 1)
                    pipeline(e, 2 * NB, [(lambda i, u, h: ln.roots(e, i, u), 0)])

                @block.scalar
                def _(e):
                    def fix(i, u, h):
                        rows.wait(e, i - 2, "rows")
                        fixed.done(e.activation(mt[:, u, :, :], msg[:, :, ds(i * TN, TN)], ACT.Copy), "msg")

                    def copy(i, u, h):
                        turn.wait(e, i, "turn")
                        t_out.wait(e, u, h - 1)
                        for c in range(DC):
                            copied.done(e.activation(f3T[:, u, c, :], ps[:, 2 + u, c * TN:(c + 1) * TN], ACT.Copy,
                                                     accum_out=fsum[:, c, ds(i, 1)]), f"c{c}")
                    pipeline(e, 2 * NB, [(copy, 2), (fix, 0)])

                @block.tensor
                def _(e):
                    e.wait_ge(s_p, len(MAPS))

                    def product(i, u, h):
                        x_in.wait(e, u, h)
                        fixed.wait(e, i, "msg")
                        sums3.wait(e, i - 2, "x3")
                        for c in range(DC):
                            e.matmul(ps[0:TN, u, 0:D], xmT[:, u, c, :], mix1[:, c, :], start=(c == 0), stop=False)
                        for k in range(SL):
                            mm = e.matmul(ps[0:TN, u, 0:D], mt[:, u, k, :], wm[:, k, :],
                                          start=False, stop=(k == SL - 1))
                        rows.done(mm, "rows")

                    def turned(i, u, h):
                        ln.norm.wait(e, i, "f")
                        copied.wait(e, i - 2, "c1")
                        for c in range(DC):
                            mm = e.transpose(ps[:, 2 + u, c * TN:(c + 1) * TN], f3[:, u, c * P:(c + 1) * P],
                                             ident[0:TN, 0:TN])
                        turn.done(mm, "turn")
                    pipeline(e, 2 * NB, [(turned, 2), (product, 0)])

                @block.vector
                def _(e):
                    e.wait_ge(s_z, 1)
                    e.wait_ge(s_w, 10 * 16)
                    for slot, half, k, factor, m in MAPS:
                        to = wm[half, slot, 0:MUL] if m == 0 else wm[half, slot, MUL + m - 1:D:3]
                        e.tensor_scalar(to, parts[half, k, :], ALPHA * factor, None, ALU.mult).then_inc(s_p, 1)

                    def x3_of(i, u, h):
                        x_in.wait(e, u, h)
                        sums3.done(e.tensor_tensor(xb[:, u, :], x2[:, u, :], bout[:, :], ALU.add), "xb")
                        rows.wait(e, i, "rows")
                        sums3.wait(e, i, "xb")
                        x_out.wait(e, u, h - 1)
                        sums3.done(e.tensor_tensor(x3[:, u, :], ps[0:TN, u, 0:D], xb[:, u, :], ALU.add), "x3")
                        sums3.wait(e, i, "x3")
                        ln.row_stats(e, i, u, x3[:, u:u + 1, :])

                    def f3_of(i, u, h):
                        ln.root.wait(e, i, "root")
                        turn.wait(e, i - 2, "turn")
                        f_out.wait(e, u, h - 1)
                        ln.norm.done(ln.scaled(e, u, 0, f3[:, u, :], x3[:, u, :]), "f")
                    pipeline(e, 2 * NB, [(f3_of, 1), (x3_of, 0)])
        layer1.close()

        with Phase("p11") as ph:
            FC = F1 // P
            w1 = ph.sb("w1", [P, 2, DC, F1])
            w2 = ph.sb("w2", [P, 2, FC, D])
            b1 = ph.sb("b1", [P, 2, FC])
            bias = ph.sb("bias", [TN, D])
            gamma = ph.sb("gamma", [TN, D])
            beta = ph.sb("beta", [TN, D])
            gates = ph.sb("gates", [P, 2])
            router = Phase("p10")
            fsum = router.sb("fsum", [P, DC, 2 * NB])
            mean = router.sb("mean", [P, DC])
            wr = router.sb("wr", [P, DC, NE1])
            br = router.sb("br", [1, NE1])
            lg = router.sb("lg", [1, NE1])
            ex = router.sb("ex", [1, NE1])
            rw = router.sb("rw", [1, NE1])
            one = router.sb("one", [1, 1])
            best = router.sb("best", [1, 2, 1])
            first = router.sb("first", [1, 2, 1])
            keys = router.sb("keys", [1, 1, NE1])
            rank = router.sb("rank", [1, NE1])
            picks = router.sb("picks", [1, 2, 1, NE1])
            gate = router.sb("gate", [1, 2])
            chosen = router.sb("chosen", [1, 2], I32)
            b2 = router.sb("b2", [1, 2, D])
            s_in, s_w, s_v, s_e, s_pe, s_sel = (router.sem(n) for n in ("in", "w", "v", "e", "pe", "sel"))
            CAPACITY = -(-N * 5 // (4 * NE1))
            with nc.Block() as block:
                @block.sync
                def _(e):
                    for dst, src in ((fsum[:, :, :].rearrange("p c n -> p (c n)"), fsum_d),
                                     (wr[:, :, :], chunked(A["L1_ffn_Wr"])),
                                     (br[:, :], A["L1_ffn_br"].rearrange("(a n) -> a n", a=1)),
                                     (gamma[:, :], A["L1_ffn_gamma"].partition_broadcast(TN)),
                                     (beta[:, :], A["L1_ffn_beta"].partition_broadcast(TN))):
                        e.dma_start(dst, src).then_inc(s_in, 16)
                    e.wait_ge(s_sel, 1)
                    for k in range(2):
                        x = e.value_load(chosen[0:1, k:k + 1], min_val=0, max_val=NE1 - 1)
                        for dst, src in ((w1[:, k, :, :], A["L1_ffn_W1"][ds(x, 1), :, :]
                                          .rearrange("e (c p) n -> p (e c) n", p=P)),
                                         (w2[:, k, :, :], A["L1_ffn_W2"][ds(x, 1), :, :]
                                          .rearrange("e (c p) n -> p (e c) n", p=P)),
                                         (b2[:, k, :], A["L1_ffn_b2"][ds(x, 1), :])):
                            e.dma_start(dst, src).then_inc(s_w, 16)
                        e.dma_start(b1[:, k, :], A["L1_ffn_b1"][ds(x, 1), :].rearrange("e (c p) -> p (e c)", p=P),
                                    allow_slow_non_contiguous=True).then_inc(s_w, 16)
                    e.wait_ge(s_w, 8 * 16)

                @block.tensor
                def _(e):
                    e.wait_ge(s_in, 5 * 16)
                    e.wait_ge(s_pe, 1)
                    for c in range(DC):
                        mm = e.matmul(ps[0:1, 0, 0:NE1], mean[:, c:c + 1], wr[:, c, :],
                                      start=(c == 0), stop=(c == DC - 1))
                    mm.then_inc(s_pe, 1)
                    e.wait_ge(s_pe, 3)
                    e.matmul(ps[:, 1, 0:2], ones[0:1, :], gate[:, :], start=True, stop=True).then_inc(s_pe, 1)
                    e.wait_ge(s_pe, 5)
                    for k in range(2):
                        mm = e.matmul(ps[0:TN, 2, 0:D], ones[0:1, 0:TN], b2[:, k, :], start=(k == 0), stop=(k == 1))
                    mm.then_inc(s_pe, 1)

                @block.scalar
                def _(e):
                    for k in range(2):
                        e.wait_ge(s_e, 2 * k + 1)
                        e.activation(ex[:, :], lg[:, :], ACT.Exp).then_inc(s_e, 1)
                    e.wait_ge(s_e, 5)
                    e.activation(gate[:, 1:2], one[:, :], ACT.Exp).then_inc(s_e, 1)

                @block.vector
                def _(e):
                    box = [0]

                    def step(ins):
                        chained(e, ins, s_v, box)

                    def softmax(k):
                        step(e.tensor_reduce(one[:, :], lg[:, :], AX, ALU.max))
                        step(e.tensor_scalar(lg[:, :], lg[:, :], one[:, 0:1], None, ALU.subtract))
                        e.sem_inc(s_e, 1)
                        e.wait_ge(s_e, 2 * k + 2)
                        step(e.tensor_reduce(one[:, :], ex[:, :], AX, ALU.add))
                        step(e.reciprocal(one[:, :], one[:, :]))
                        step(e.tensor_scalar(rw[:, :], ex[:, :], one[:, 0:1], None, ALU.mult))
                    e.wait_ge(s_in, 5 * 16)
                    step(e.tensor_reduce(mean[:, :], fsum[:, :, :], AX, ALU.add))
                    step(e.tensor_scalar(mean[:, :], mean[:, :], 1.0 / N, None, ALU.mult))
                    e.sem_inc(s_pe, 1)
                    step(e.tensor_scalar(rank[:, :], iota[0:1, 0:NE1], -1.0, 8.0, ALU.mult, ALU.add))
                    e.wait_ge(s_pe, 2)
                    step(e.tensor_tensor(lg[:, :], ps[0:1, 0, 0:NE1], br[:, :], ALU.add))
                    softmax(0)
                    step(e.tensor_scalar(lg[:, :], rw[:, :], float(N), None, ALU.mult))
                    step(e.reciprocal(lg[:, :], lg[:, :]))
                    step(e.tensor_scalar(lg[:, :], lg[:, :], float(CAPACITY), 1.0, ALU.mult, ALU.min))
                    step(e.tensor_tensor(lg[:, :], lg[:, :], rw[:, :], ALU.mult))
                    softmax(1)
                    pick_two(e, step, rw[:, :].unsqueeze(1), rank[:, :], best[:, :, :], first[:, :, :],
                             keys[:, :, :], picks[:, :, :, :])
                    step(e.tensor_scalar(chosen[:, :], first[:, :, 0], -1.0, 8.0, ALU.mult, ALU.add))
                    e.sem_inc(s_sel, 1)
                    step(e.tensor_tensor(one[:, :], best[:, 1, :], best[:, 0, :], ALU.subtract))
                    e.sem_inc(s_e, 1)
                    e.wait_ge(s_e, 6)
                    step(e.tensor_scalar(one[:, :], gate[:, 1:2], 1.0, None, ALU.add))
                    step(e.reciprocal(gate[:, 0:1], one[:, :]))
                    step(e.tensor_tensor(gate[:, 1:2], gate[:, 1:2], gate[:, 0:1], ALU.mult))
                    e.sem_inc(s_pe, 1)
                    e.wait_ge(s_pe, 4)
                    step(e.tensor_copy(gates[:, :], ps[:, 1, 0:2]))
                    e.wait_ge(s_w, 8 * 16)
                    for k in range(2):
                        step(e.tensor_scalar(b2[:, k, :], b2[:, k, :], gate[:, k:k + 1], None, ALU.mult))
                    e.sem_inc(s_pe, 1)
                    for k in range(2):
                        step(e.tensor_scalar(w2[:, k, :, :], w2[:, k, :, :], gates[:, k:k + 1], None, ALU.mult))
                    e.wait_ge(s_pe, 6)
                    step(e.tensor_copy(bias[:, :], ps[0:TN, 2, 0:D]))
            router.__exit__(None)

            f3T = ph.sb("f3T", [P, 2, 2, DC * TN])
            hid = ph.sb("hid", [P, 2, 2, FC, BN])
            f3 = ph.sb("f3", [TN, 2, 2, D])
            x3 = ph.sb("x3", [TN, 2, 2, D])
            z = ph.sb("z", [TN, 2, 2, D])
            y = ph.sb("y", [TN, 2, 2, D])
            c_in, f_in, x_in, y_out = (ph.landing(n, 2) for n in ("ci", "fi", "xi", "yo"))
            BANKS = [f"{q}" for q in range(FC)]
            up = ph.steps("up", *BANKS)
            act = ph.steps("act", *BANKS)
            down = ph.steps("down", "rows")
            sums = ph.steps("sums", "bias", "z")
            ln = RowNorm(ph, "ln", ("n0", "n1"))
            fin = ph.steps("fin", "beta", "gamma", "out")
            with nc.Block() as block:
                @block.sync
                def _(e):
                    def load_columns(i, u, h):
                        up.wait(e, i - 2, BANKS[-1])
                        c_in.start(e.dma_start(f3T[:, u, :, :], f3T_d[ds(i * 2, 2), :, :].rearrange("t p n -> p t n")), u)

                    def load_rows(i, u, h):
                        sums.wait(e, i - 2, "bias")
                        f_in.start(e.dma_start(f3[:, u, :, :], rows_of(f3_d, i)), u)
                        fin.wait(e, i - 2, "beta")
                        x_in.start(e.dma_start(x3[:, u, :, :], rows_of(x3_d, i)), u)

                    def store(i, u, h):
                        fin.wait(e, i, "out")
                        y_out.start(e.dma_start(rows_of(out, i), y[:, u, :, :]), u)
                    pipeline(e, NB, [(load_columns, 0), (store, 2), (load_rows, 0)])
                    for u in range(2):
                        y_out.wait(e, u, (NB - 1 - u) // 2)

                @block.tensor
                def _(e):
                    def layer_up(i, u, h):
                        c_in.wait(e, u, h)
                        for q in range(FC):
                            act.wait(e, i - 1, BANKS[q])
                            for m in range(2):
                                k, f = divmod(2 * q + m, FC)
                                for c in range(DC):
                                    mm = e.matmul(ps[:, q, m * BN:(m + 1) * BN], w1[:, k, c, f * P:(f + 1) * P],
                                                  f3T[:, u, :, c * TN:(c + 1) * TN],
                                                  start=(c == 0), stop=(c == DC - 1))
                            up.done(mm, BANKS[q])

                    def layer_down(i, u, h):
                        sums.wait(e, i - 2, "z")
                        act.wait(e, i, BANKS[-1])
                        for t in range(2):
                            for j in range(2 * FC):
                                k, f = divmod(j, FC)
                                mm = e.matmul(ps[0:TN, 4 + u, t * D:(t + 1) * D], hid[:, u, k, f, t * TN:(t + 1) * TN],
                                              w2[:, k, f, :], start=(j == 0), stop=(j == 2 * FC - 1))
                        down.done(mm, "rows")
                    pipeline(e, NB, [(layer_down, 1), (layer_up, 0)])

                @block.scalar
                def _(e):
                    def gelu(i, u, h):
                        down.wait(e, i - 2, "rows")
                        for q in range(FC):
                            up.wait(e, i, BANKS[q])
                            for m in range(2):
                                k, f = divmod(2 * q + m, FC)
                                ins = e.activation(hid[:, u, k, f, :], ps[:, q, m * BN:(m + 1) * BN], ACT.Gelu,
                                                   bias=b1[:, k, f:f + 1])
                            act.done(ins, BANKS[q])
                    pipeline(e, NB, [(gelu, 0)])

                @block.gpsimd
                def _(e):
                    pipeline(e, NB, [(lambda i, u, h: ln.roots(e, i, u), 0)])

                @block.vector
                def _(e):
                    def both(x):
                        return x[:, :].unsqueeze(1).broadcast_to([TN, 2, D])

                    def residual(i, u, h):
                        f_in.wait(e, u, h)
                        ln.norm.wait(e, i - 2, "n1")
                        sums.done(e.tensor_tensor(z[:, u, :, :], f3[:, u, :, :], both(bias), ALU.add), "bias")
                        down.wait(e, i, "rows")
                        sums.wait(e, i, "bias")
                        sums.done(e.tensor_tensor(z[:, u, :, :], ps[0:TN, 4 + u, :].rearrange("p (t f) -> p t f", t=2),
                                                  z[:, u, :, :], ALU.add), "z")
                        sums.wait(e, i, "z")
                        ln.row_stats(e, i, u, z[:, u, :, :])

                    def finish(i, u, h):
                        x_in.wait(e, u, h)
                        y_out.wait(e, u, h - 1)
                        ln.root.wait(e, i, "root")
                        for t in range(2):
                            ln.norm.done(ln.scaled(e, u, t, z[:, u, t, :], z[:, u, t, :]), f"n{t}")
                        fin.done(e.tensor_tensor(y[:, u, :, :], x3[:, u, :, :], both(beta), ALU.add), "beta")
                        ln.norm.wait(e, i, "n1")
                        fin.done(e.tensor_tensor(z[:, u, :, :], z[:, u, :, :], both(gamma), ALU.mult), "gamma")
                        fin.wait(e, i, "gamma")
                        fin.done(e.tensor_tensor(y[:, u, :, :], y[:, u, :, :], z[:, u, :, :], ALU.add), "out")
                    pipeline(e, NB, [(finish, 1), (residual, 0)])


_ORDER = [*range(MUL), *(MUL + 3 * i + m for m in range(3) for i in range(MUL))]


def lay_out(inputs):
    import numpy as _np
    arrays = {name: _np.asarray(a) for name, a in inputs.items()}
    wqkv = arrays.pop("L1_mix_Wqkv")
    inner = wqkv.shape[0] // 3
    arrays["L1_mix_Wq"] = wqkv[:inner][:, _ORDER]
    arrays["L1_mix_WkvT"] = wqkv[inner:].T[_ORDER]
    arrays["L1_mix_WoutT"] = arrays.pop("L1_mix_Wout").T
    return arrays


def kernel(**inputs):
    import numpy as _np
    import concourse.bacc as _bacc
    from concourse.bass_utils import run_bass_kernel_spmd as _run

    nc = _bacc.Bacc("TRN2", target_bir_lowering=False, num_devices=1)
    arrays, args = {}, {}
    for name, a in lay_out(inputs).items():
        a = _np.ascontiguousarray(a)
        arrays[f"in_{name}"] = a
        args[name] = nc.dram_tensor(f"in_{name}", a.shape, mybir.dt.from_np(a.dtype), kind="ExternalInput").ap()
    out = nc.dram_tensor("out_0", (N, D), F32, kind="ExternalOutput").ap()
    gps_kernel(nc, args, out)
    r = _run(nc, [arrays], core_ids=[0])
    return r.results[0]["out_0"]
```

```python
from contextlib import ExitStack

import concourse.bass as bass
from concourse import mybir

F32 = mybir.dt.float32
I32 = mybir.dt.int32
U32 = mybir.dt.uint32
ALU = mybir.AluOpType
ACT = mybir.ActivationFunctionType
AX = mybir.AxisListType.X
ds = bass.ds

N, D, E = 6250, 256, 100000
P = 128
TN = 125
BN = 2 * TN
NB = N // BN
DC = D // P
WIN = 48
NPAD = N + WIN
GE = 2 * TN
NG = E // GE
RR = 100
RU = E // RR
ST = RU // TN
HID = 1024
LN_EPS = 1e-5
H0, HD0 = 8, 32
NE0, RH0 = 6, 128
H1, HD1 = 8, 64
NE1, F1 = 8, 512
MUL = 64
NEG = -1.0


class Steps:

    def __init__(self, sem, *names):
        self.sem, self.names, self.at = sem, names, 0

    def done(self, ins, name):
        assert self.names[self.at % len(self.names)] == name, (self.names, self.at, name)
        self.at += 1
        ins.then_inc(self.sem, 1)

    def wait(self, eng, i, name):
        value = i * len(self.names) + self.names.index(name) + 1
        if not isinstance(value, int) or value > 0:
            eng.wait_ge(self.sem, value)


class Landing:

    def __init__(self, sems, per=1):
        self.sems, self.per = sems, per

    def start(self, ins, u):
        ins.then_inc(self.sems[u], 16)

    def wait(self, eng, u, h):
        value = 16 * self.per * (h + 1)
        if not isinstance(value, int) or value > 0:
            eng.wait_ge(self.sems[u], value)


def pipeline(eng, n, stages, unroll=2):
    deepest = max(lag for _, lag in stages)
    steps = n + deepest
    first = deepest + unroll

    def one(s, k=None):
        for fn, lag in stages:
            i = s - lag
            if k is not None:
                fn(k * unroll + i, i % unroll, k + i // unroll)
            elif 0 <= i < n:
                fn(i, i % unroll, i // unroll)

    turns = max(0, (n - first) // unroll)
    if turns < 2:
        first, turns = steps, 0
    for s in range(min(first, steps)):
        one(s)
    if turns:
        with eng.Fori(0, turns) as k:
            for u in range(unroll):
                one(first + u, k)
    for s in range(first + turns * unroll, steps):
        one(s)


def gps_kernel(nc, A, out):
    top = ExitStack()
    sem_names = iter(range(10000))

    def sem(name):
        return top.enter_context(nc.semaphore(f"{name}_{next(sem_names)}"))

    def recycle(sems):
        nc.clear_and_free_semaphores(sems)
        nc.all_engine_barrier()

    class Phase:

        def __init__(self, name):
            self.name, self.ctx, self.sems = name, ExitStack(), []

        def __enter__(self):
            return self

        def __exit__(self, *a):
            self.ctx.close()
            if a[0] is None:
                recycle(self.sems)

        def sb(self, name, shape, dt=F32):
            return self.ctx.enter_context(nc.sbuf_tensor(f"{self.name}_{name}", shape, dt))

        def sem(self, name):
            self.sems.append(nc.alloc_semaphore(name=f"{self.name}_{name}"))
            return self.sems[-1]

        def steps(self, name, *names):
            return Steps(self.sem(name), *names)

        def landing(self, name, slots, per=1):
            return Landing([self.sem(f"{name}{u}") for u in range(slots)], per)

    def sb(name, shape, dt=F32):
        return top.enter_context(nc.sbuf_tensor(name, shape, dt))

    def scratch(name, shape, dt=F32):
        return nc.dram_tensor(name, shape, dt).ap()

    def rows_of(dram, i):
        return dram[ds(i * BN, BN), :].rearrange("(t p) f -> p t f", t=2)

    def chunked(dram):
        return dram.rearrange("(c p) n -> p c n", p=P)

    with top:
        ps = top.enter_context(nc.psum_tensor("ps", [P, 8, 512], F32))

        ident = sb("ident", [P, P])
        ones = sb("ones", [P, P])
        iota = sb("iota", [P, P])
        neg_half = sb("neg_half", [P, 16])
        layer0 = top.enter_context(ExitStack())
        cols = layer0.enter_context(nc.sbuf_tensor("cols", [P, DC, NPAD], F32))

        w1 = layer0.enter_context(nc.sbuf_tensor("gin_w1", [P, DC, HID], F32))
        s_w1 = sem("gin_w1")

        xn_d = scratch("xn_d", (N, D))
        xp_d = scratch("xp_d", (N, D))
        h1_d = scratch("h1_d", (NB, P, 8 * BN))
        x1_d = scratch("x1_d", (N, D))
        f1_d = scratch("f1_d", (N, D))
        x2_d = scratch("x2_d", (N, D))
        xm_d = scratch("xm_d", (N, D))
        xmT_d = scratch("xmT_d", (NB, P, DC * BN))
        x3_d = scratch("x3_d", (N, D))
        f3T_d = scratch("f3T_d", (2 * NB, P, DC * TN))
        f3_d = scratch("f3_d", (N, D))
        idx_d = scratch("idx_d", (P, RR * ST), I32)
        rel_d = scratch("rel_d", (P, RR * ST))
        left_d = scratch("left_d", (P, RR * ST))
        w_d = scratch("w_d", (P, RR * ST * 4))
        base_d = scratch("base_d", (1, NG), I32)
        flag_d = scratch("flag_d", (1, 1), I32)
        fsum_d = scratch("fsum_d", (P, DC * 2 * NB))
        mix1_d = scratch("mix1_d", (P, DC * D))

        s_const = sem("const")
        s_held = {engine: sem(f"held_{engine}") for engine in ("DVE", "PE", "Pool")}
        with nc.Block() as block:
            @block.gpsimd
            def _(e):
                e.memset(ident[:, :], 0.0).then_inc(s_const, 1)
                e.iota(iota[:, :], pattern=[[1, P]], base=0, channel_multiplier=0,
                       allow_small_or_imprecise_dtypes=True).then_inc(s_const, 1)
                e.memset(ones[:, :], 1.0).then_inc(s_const, 1)
                e.memset(neg_half[:, :], -0.5).then_inc(s_const, 1)
                e.memset(cols[:, :, N:NPAD], 0.0).then_inc(s_const, 1)
                e.wait_ge(s_const, 1)
                e.affine_select(out=ident[:, :], in_=ident[:, :], compare_op=ALU.not_equal, fill=1.0, base=0,
                                pattern=[[-1, P]], channel_multiplier=1).then_inc(s_const, 1)
                e.wait_ge(s_const, 6)

        def chained(e, ins, s, box):
            box[0] += 1
            ins.then_inc(s, 1)
            e.wait_ge(s, box[0])

        with Phase("p0") as ph:
            raw_i = ph.sb("raw_i", [RR, 2, RU], I32)
            raw_f = ph.sb("raw_f", [RR, 2, RU])
            idx = ph.sb("idx", [TN, RR, ST], I32)
            dst = ph.sb("dst", [TN, NG, 2])
            base = ph.sb("base", [TN, NG])
            base_i = ph.sb("base_i", [1, NG], I32)
            rel = ph.sb("rel", [TN, NG, 2])
            ok = ph.sb("ok", [TN, NG, 2])
            left = ph.sb("left", [TN, NG, 2])
            bad = ph.sb("bad", [TN, 1])
            flag = ph.sb("flag", [1, 1], I32)
            s_in, s_f, s_t, s_c, s_b, s_x, s_g, s_out = (ph.sem(n) for n in
                                                         ("in", "f", "t", "c", "b", "x", "g", "out"))
            with nc.Block() as block:
                @block.sync
                def _(e):
                    for k, name in enumerate(("src", "dst")):
                        e.dma_start(raw_i[:, k, :], A[name].rearrange("(r u) -> r u", u=RU)).then_inc(s_in, 16)
                    e.wait_ge(s_x, 1)
                    e.dma_start(idx_d[0:TN, :], idx[:, :, :].rearrange("p r s -> p (r s)")).then_inc(s_out, 16)
                    e.dma_start(rel_d[0:TN, :], rel[:, :, :].rearrange("p g j -> p (g j)")).then_inc(s_out, 16)
                    e.dma_start(left_d[0:TN, :], left[:, :, :].rearrange("p g j -> p (g j)")).then_inc(s_out, 16)
                    e.dma_start(base_d[:, :], base_i[:, :]).then_inc(s_out, 16)
                    e.dma_start(flag_d[:, :], flag[:, :]).then_inc(s_out, 16)
                    e.wait_ge(s_out, 5 * 16)

                @block.tensor
                def _(e):
                    e.wait_ge(s_f, 2)
                    for k in range(2):
                        for s in range(ST):
                            at = (s % 4) * RR
                            mm = e.transpose(ps[0:TN, 2 * k + s // 4, at:at + RR],
                                             raw_f[:, k, s * TN:(s + 1) * TN], ident[0:RR, 0:RR])
                    mm.then_inc(s_t, 1)
                    e.wait_ge(s_c, 4)
                    e.matmul(ps[0:TN, 4, 0:NG], ones[0:1, 0:TN], dst[0:1, :, 0],
                             start=True, stop=True).then_inc(s_b, 1)
                    e.wait_ge(s_g, 1)
                    e.matmul(ps[0:1, 5, 0:1], bad[:, :], ones[0:TN, 0:1], start=True, stop=True).then_inc(s_b, 1)

                @block.vector
                def _(e):
                    e.wait_ge(s_in, 32)
                    for k in range(2):
                        e.tensor_copy(raw_f[:, k, :], raw_i[:, k, :]).then_inc(s_f, 1)
                    e.wait_ge(s_t, 1)
                    for k, to in enumerate((idx[:, :, :], dst[:, :, :].rearrange("p (r q) j -> p r (q j)", r=RR))):
                        for b in range(2):
                            e.tensor_copy(to[:, :, 4 * b:4 * b + 4],
                                          ps[0:TN, 2 * k + b, 0:4 * RR].rearrange("p (s r) -> p r s", s=4))\
                             .then_inc(s_c, 1)
                    box = [0]
                    s_v = ph.sem("v")

                    def step(ins):
                        chained(e, ins, s_v, box)
                    e.wait_ge(s_b, 1)
                    step(e.tensor_scalar(base[:, :], ps[0:TN, 4, 0:NG], 0.0, float(N), ALU.max, ALU.min))
                    step(e.tensor_copy(base_i[:, :], base[0:1, :]))
                    e.wait_ge(s_c, 4)
                    wide = base[:, :].unsqueeze(2).broadcast_to([TN, NG, 2])
                    step(e.tensor_tensor(rel[:, :, :], dst[:, :, :], wide, ALU.subtract))
                    step(e.tensor_scalar(left[:, :, :], rel[:, :, :], 0.0, None, ALU.is_ge))
                    step(e.scalar_tensor_tensor(ok[:, :, :], rel[:, :, :], float(WIN), left[:, :, :],
                                                ALU.is_lt, ALU.mult))
                    step(e.scalar_tensor_tensor(rel[:, :, :], rel[:, :, :], 1.0, ok[:, :, :], ALU.add, ALU.mult))
                    step(e.tensor_scalar(rel[:, :, :], rel[:, :, :], -1.0, None, ALU.add))
                    step(e.tensor_scalar(ok[:, :, :], ok[:, :, :], -1.0, 1.0, ALU.mult, ALU.add))
                    e.tensor_reduce(bad[:, :], ok[:, :, :].rearrange("p g j -> p (g j)"), AX, ALU.add).then_inc(s_g, 1)
                    step(e.scalar_tensor_tensor(left[:, :, :], dst[:, :, :], 1.0, ok[:, :, :], ALU.add, ALU.mult))
                    step(e.tensor_scalar(left[:, :, :], left[:, :, :], -1.0, None, ALU.add))
                    e.wait_ge(s_b, 2)
                    step(e.tensor_copy(flag[:, :], ps[0:1, 5, 0:1]))
                    e.sem_inc(s_x, 1)

        class Rider:

            def __init__(self, period, end=None, **stages):
                self.period, self.end, self.stages = period, end, stages

            def on(self, e, engine, turn):
                def every(fn):
                    def stage(i, u, h):
                        if u % self.period == 0:
                            fn(e, h * (turn // self.period) + u // self.period, u // self.period, h)
                    return stage
                return [(every(fn), lag) for fn, lag in self.stages.get(engine, ())]

        def sum_edges(name, rows_d, weighted, add, riders=()):
            UG = 4
            TURN = 4 * UG if riders else 2 * UG

            def groups(e, engine, stages):
                own = [(lambda i, u, h, fn=fn: fn(i, u % (2 * UG), h * (TURN // UG) + u // UG), lag)
                       for fn, lag in stages]
                beside = [stage for rider in riders for stage in rider.on(e, engine, TURN)]
                if own or beside:
                    pipeline(e, NG, own + beside, unroll=TURN)
            HS = 4
            BANKS = 4
            width = WIN if weighted else P
            parts = 4 if weighted else 1
            with Phase(name) as ph:
                idx = ph.sb("idx", [TN, RR, ST], I32)
                rel = ph.sb("rel", [TN, NG, 2])
                base = ph.sb("base", [1, NG], I32)
                flag = ph.sb("flag", [1, 1], I32)
                now = ph.sb("now", [TN, 2, 2 * UG], I32)
                got = ph.sb("got", [TN, 2 * UG, D])
                hot = ph.sb("hot", [TN, HS, 2, width])
                if weighted:
                    wt = ph.sb("wt", [TN, NG, 2, 4])
                    hotw = ph.sb("hotw", [TN, HS, 2, 4, WIN])
                start = ph.sb("start", [TN, 1])
                off = ph.sb("off", [TN, 2])
                s_in, s_z = ph.sem("in"), ph.sem("z")
                landed = ph.landing("got", 2 * UG)
                put = ph.steps("put", "idx")
                ready = ph.steps("ready", *(("hot", "hotw") if weighted else ("hot",)))
                summed = ph.steps("summed", "sums")
                added = ph.steps("added", "add")

                def make_hot(e, pair, u):
                    return e.tensor_tensor(hot[:, u, :, :],
                                           iota[0:TN, 0:width].unsqueeze(1).broadcast_to([TN, 2, width]),
                                           pair.unsqueeze(2).broadcast_to([TN, 2, width]), ALU.is_equal)

                def make_weighted(e, w_pair, u):
                    return [e.tensor_tensor(hotw[:, u, j, :, :],
                                            hot[:, u, j, :].unsqueeze(1).broadcast_to([TN, 4, WIN]),
                                            w_pair[:, j, :].unsqueeze(2).broadcast_to([TN, 4, WIN]), ALU.mult)
                            for j in range(2)]

                def sums(e, b, u, slot):
                    for c in range(DC):
                        for j in range(2):
                            lhs = got[:, slot + j, c * P:(c + 1) * P]
                            if weighted:
                                at, n = (0, 4 * WIN) if c == 0 else (4 * WIN, 3 * WIN)
                                rhs = hotw[:, u, j, :, :].rearrange("p k w -> p (k w)")[:, c * WIN:4 * WIN]
                            else:
                                at, n, rhs = c * P, P, hot[:, u, j, :]
                            mm = e.matmul(ps[:, b, at:at + n], lhs, rhs, start=(j == 0), stop=(j == 1))
                    return mm

                with nc.Block() as block:
                    @block.sync
                    def _(e):
                        loads = [(idx[:, :, :].rearrange("p r s -> p (r s)"), idx_d[0:TN, :]),
                                 (rel[:, :, :].rearrange("p g j -> p (g j)"), rel_d[0:TN, :]),
                                 (base[:, :], base_d), (flag[:, :], flag_d)]
                        if weighted:
                            loads.append((wt[:, :, :, :].rearrange("p g j k -> p (g j k)"), w_d[0:TN, :]))
                        for dst, src in loads:
                            e.dma_start(dst, src).then_inc(s_in, 16)
                        e.wait_ge(s_in, 16 * len(loads))
                        groups(e, "sync", [])
                        for rider in riders:
                            if rider.end:
                                rider.end(e)
                        if not weighted:
                            e.dma_start(w1[:, :, :], chunked(A["L0_gnn_W1"])).then_inc(s_w1, 16)

                    @block.scalar
                    def _(e):
                        groups(e, "scalar", [])

                    @block.gpsimd
                    def _(e):
                        e.wait_ge(s_in, 16 * (4 + weighted))

                        def gather(i, u, h):
                            summed.wait(e, i - UG, "sums")
                            half = u // UG
                            if u % UG == 0:
                                flat = idx[:, :, :].rearrange("p r s -> p (r s)")
                                put.done(e.tensor_copy(now[:, half, :], flat[:, ds(h * 2 * UG, 2 * UG)]), "idx")
                                put.wait(e, h, "idx")
                            e.sem_inc(s_held["Pool"], 1)
                            for j in range(2):
                                slot = 2 * (u % UG) + j
                                landed.start(e.indirect_dma_start(
                                    got[:, slot, :], None, rows_d,
                                    bass.IndirectOffsetOnAxis(ap=now[:, half, slot:slot + 1], axis=0)), slot)
                        groups(e, "gpsimd", [(gather, 0)])

                    @block.vector
                    def _(e):
                        e.wait_ge(s_in, 16 * (4 + weighted))

                        def prepare(i, u, h):
                            summed.wait(e, i - HS, "sums")
                            ready.done(make_hot(e, rel[:, ds(i, 1), :].rearrange("p g j -> p (g j)"), u % HS), "hot")
                            if weighted:
                                ready.wait(e, i, "hot")
                                both = make_weighted(e, wt[:, ds(i, 1), :, :].rearrange("p g j k -> p (g j) k"), u % HS)
                                ready.done(both[1], "hotw")

                        def accumulate(i, u, h):
                            at = e.value_load(base[0:1, ds(i, 1)], min_val=0, max_val=N)
                            summed.wait(e, i, "sums")
                            added.wait(e, i - 1, "add")
                            added.done(add(e, at, u % BANKS), "add")
                        groups(e, "vector", [(prepare, 0), (accumulate, HS - 1)])

                    @block.tensor
                    def _(e):
                        def group(i, u, h):
                            slot = 2 * (u % UG)
                            landed.wait(e, slot, h)
                            landed.wait(e, slot + 1, h)
                            ready.wait(e, i, "hotw" if weighted else "hot")
                            added.wait(e, i - BANKS, "add")
                            summed.done(sums(e, u % BANKS, u % HS, slot), "sums")
                        groups(e, "tensor", [(group, 0)])

                NW = (N + WIN - 1) // WIN
                s_l, s_rows, s_hot, s_sum, s_add = (ph.sem(n) for n in ("l", "rows", "hot", "sum", "add"))
                s_idx, s_pe, s_dve, s_chain = (ph.sem(n) for n in ("idx", "go_pe", "go_dve", "chain"))
                with nc.Block() as block:
                    @block.sync
                    def _(e):
                        e.dma_start(rel[:, :, :].rearrange("p g j -> p (g j)"), left_d[0:TN, :]).then_inc(s_l, 16)
                        e.wait_ge(s_l, 16)

                    @block.gpsimd
                    def _(e):
                        some = e.value_load(flag[0:1, 0:1], min_val=0, max_val=E)
                        with e.If(some > 0):
                            with e.Fori(0, NG) as g:
                                flat = idx[:, :, :].rearrange("p r s -> p (r s)")
                                e.tensor_copy(now[:, 0, 0:2], flat[:, ds(g * 2, 2)]).then_inc(s_idx, 1)
                                e.wait_ge(s_idx, 1)
                                for j in range(2):
                                    e.indirect_dma_start(got[:, j, :], None, rows_d, bass.IndirectOffsetOnAxis(
                                        ap=now[:, 0, j:j + 1], axis=0)).then_inc(s_rows, 16)
                                e.sem_inc(s_add, 1)
                                e.wait_ge(s_add, NW + 1)
                                for s in (s_idx, s_hot, s_sum, s_add, s_chain):
                                    e.sem_clear(s)
                                e.sem_inc(s_pe, 1)
                                e.sem_inc(s_dve, 1)

                    @block.tensor
                    def _(e):
                        some = e.value_load(flag[0:1, 0:1], min_val=0, max_val=E)
                        with e.If(some > 0):
                            with e.Fori(0, NG) as g:
                                e.wait_ge(s_rows, g * 32 + 32)
                                e.sem_inc(s_held["PE"], 1)
                                with e.Fori(0, NW) as w:
                                    e.wait_ge(s_add, w + 1)
                                    e.wait_ge(s_hot, w + 1)
                                    sums(e, 0, 0, 0).then_inc(s_sum, 1)
                                e.wait_ge(s_pe, 1)
                                e.sem_clear(s_pe)

                    @block.vector
                    def _(e):
                        e.wait_ge(s_l, 16)
                        some = e.value_load(flag[0:1, 0:1], min_val=0, max_val=E)
                        links = 3 if weighted else 2
                        with e.If(some > 0):
                            with e.Fori(0, NG) as g:
                                e.memset(start[:, :], -float(WIN)).then_inc(s_chain, 1)
                                with e.Fori(0, NW) as w:
                                    e.wait_ge(s_chain, w * links + 1)
                                    e.tensor_scalar(start[:, :], start[:, :], float(WIN), None, ALU.add)\
                                     .then_inc(s_chain, 1)
                                    e.wait_ge(s_chain, w * links + 2)
                                    e.tensor_scalar(off[:, :], rel[:, ds(g, 1), :].rearrange("p g j -> p (g j)"),
                                                    start[:, 0:1], None, ALU.subtract).then_inc(s_chain, 1)
                                    e.wait_ge(s_chain, w * links + 3)
                                    ins = make_hot(e, off[:, :], 0)
                                    if weighted:
                                        ins.then_inc(s_chain, 1)
                                        e.wait_ge(s_chain, w * links + 4)
                                        ins = make_weighted(
                                            e, wt[:, ds(g, 1), :, :].rearrange("p g j k -> p (g j) k"), 0)[1]
                                    ins.then_inc(s_hot, 1)
                                    e.wait_ge(s_sum, w + 1)
                                    add(e, w * WIN, 0).then_inc(s_add, 1)
                                e.wait_ge(s_dve, 1)
                                e.sem_clear(s_dve)

        with Phase("p1") as ph:
            qT = ph.sb("qT", [P, DC, N])
            kv_acc = ph.sb("kv_acc", [P, DC * P + DC * HD0])
            inner = Phase("p1a")
            xin = inner.sb("xin", [TN, 2, 2, D])
            st = inner.sb("st", [TN, 2, 2, 6])
            mv = inner.sb("mv", [TN, 2, 2, 2])
            pre = inner.sb("pre", [TN, 2, 2, 2])
            rs = inner.sb("rs", [TN, 2, 2, 2])
            xn = inner.sb("xn", [TN, 2, 2, D])
            xr = inner.sb("xr", [TN, 2, 2, D])
            xrT = inner.sb("xrT", [P, 2, DC, BN])
            wqkv = inner.sb("wqkv", [P, DC, 3 * D])
            wn1 = inner.sb("wn1", [P, DC])
            ek = inner.sb("ek", [TN, 2, D])
            rk = inner.sb("rk", [TN, 2, D])
            k1 = inner.sb("k1", [TN, 2, 2, D])
            v1 = inner.sb("v1", [TN, 2, 2, D])
            eq = inner.sb("eq", [P, DC, BN])
            rq = inner.sb("rq", [P, DC, BN])
            s_w = inner.sem("w")
            s_ws = inner.sem("ws")
            x_in = inner.landing("x", 2)
            xn_out = inner.landing("xn", 2)
            stats = inner.steps("stats", "stats0", "stats1", "aggr0", "aggr1", "pre0", "pre1")
            root = inner.steps("root", "root")
            norm = inner.steps("norm", "xn0", "xn1", "xr0", "xr1")
            turn = inner.steps("turn", "xnT", "xrT")
            copied = inner.steps("copied", "cols", "xrT")
            proj = inner.steps("proj", "k", "q")
            acts = inner.steps("acts", "ek", "rk", "v", "eq", "rq")
            feat = inner.steps("feat", "k", "q")
            kvs = inner.steps("kvs", "kv")
            accd = inner.steps("accd", "acc")
            s_z = inner.sem("z")

            with nc.Block() as block:
                @block.sync
                def _(e):
                    e.dma_start(wqkv[:, :, :], chunked(A["L0_mix_w_qkv"])).then_inc(s_w, 16)
                    e.dma_start(wn1[:, :], A["L0_mix_w_norm1"].rearrange("(c p) -> p c", p=P),
                                allow_slow_non_contiguous=True).then_inc(s_w, 16)

                    def load(i, u, h):
                        norm.wait(e, i - 2, "xr1")
                        x_in.start(e.dma_start(xin[:, u, :, :], rows_of(A["x"], i)), u)

                    def store(i, u, h):
                        norm.wait(e, i, "xn1")
                        xn_out.start(e.dma_start(rows_of(xn_d, i), xn[:, u, :, :]), u)
                    pipeline(e, NB, [(load, 0), (store, 2)])
                    for u in range(2):
                        xn_out.wait(e, u, (NB - 1 - u) // 2)

                @block.gpsimd
                def _(e):
                    def roots(i, u, h):
                        stats.wait(e, i, "pre1")
                        norm.wait(e, i - 2, "xr1")
                        root.done(e.tensor_tensor(rs[:, u, :, :], pre[:, u, :, :],
                                                  neg_half[0:TN, 0:4].rearrange("p (a b) -> p a b", a=2),
                                                  ALU.pow), "root")
                    pipeline(e, NB, [(roots, 0)])

                @block.vector
                def _(e):
                    e.memset(kv_acc[:, :], 0.0).then_inc(s_z, 1)
                    e.wait_ge(s_w, 32)
                    for c in range(DC):
                        e.tensor_scalar(wqkv[:, c, :], wqkv[:, c, :], wn1[:, c:c + 1], None,
                                        ALU.mult).then_inc(s_ws, 1)

                    def stage_stats(i, u, h):
                        x_in.wait(e, u, h)
                        for t in range(2):
                            stats.done(e.bn_stats(st[:, u, t, :], xin[:, u, t, :]), f"stats{t}")
                        stats.wait(e, i, "stats1")
                        e.sem_inc(s_held["DVE"], 1)
                        for t in range(2):
                            stats.done(e.bn_aggr(mv[:, u, t, :], st[:, u, t, :]), f"aggr{t}")
                        stats.wait(e, i, "aggr1")
                        root.wait(e, i - 2, "root")
                        stats.done(e.tensor_scalar(pre[:, u, :, 0], mv[:, u, :, 1], 1.0, LN_EPS,
                                                   ALU.mult, ALU.add), "pre0")
                        stats.done(e.tensor_scalar(pre[:, u, :, 1], mv[:, u, :, 1], 1.0 + 1e-6, 1e-6 * LN_EPS,
                                                   ALU.mult, ALU.add), "pre1")

                    def stage_norm(i, u, h):
                        root.wait(e, i, "root")
                        turn.wait(e, i - 2, "xrT")
                        xn_out.wait(e, u, h - 1)
                        for k, dst in enumerate((xn, xr)):
                            for t in range(2):
                                norm.done(e.tensor_scalar(dst[:, u, t, :], xin[:, u, t, :],
                                                          mv[:, u, t, 0:1], rs[:, u, t, k:k + 1],
                                                          ALU.subtract, ALU.mult), f"{('xn', 'xr')[k]}{t}")

                    def stage_feat(i, u, h):
                        kvs.wait(e, i - 2, "kv")
                        acts.wait(e, i, "rk")
                        feat.done(e.scalar_tensor_tensor(k1[:, u, :, :], ek[:, :, :], 1.0, rk[:, :, :],
                                                         ALU.min, ALU.add), "k")
                        acts.wait(e, i, "rq")
                        feat.done(e.scalar_tensor_tensor(qT[:, :, ds(i * BN, BN)], eq[:, :, :], 1.0,
                                                         rq[:, :, :], ALU.min, ALU.add), "q")

                    def stage_acc(i, u, h):
                        kvs.wait(e, i, "kv")
                        if isinstance(i, int) and i == 0:
                            e.wait_ge(s_z, 1)
                        accd.wait(e, i - 1, "acc")
                        accd.done(e.tensor_tensor(kv_acc[:, :], kv_acc[:, :], ps[:, 5, 0:320], ALU.add), "acc")
                    pipeline(e, NB, [(stage_acc, 4), (stage_feat, 3), (stage_norm, 1), (stage_stats, 0)])

                @block.tensor
                def _(e):
                    e.wait_ge(s_ws, DC)

                    def stage_turn(i, u, h):
                        norm.wait(e, i, "xr1")
                        for k, (src, name) in enumerate(((xn, "xnT"), (xr, "xrT"))):
                            copied.wait(e, i - 1, ("cols", "xrT")[k])
                            for c in range(DC):
                                for t in range(2):
                                    at = c * BN + t * TN
                                    mm = e.transpose(ps[:, k, at:at + TN], src[:, u, t, c * P:(c + 1) * P],
                                                     ident[0:TN, 0:TN])
                            turn.done(mm, name)

                    def stage_proj(i, u, h):
                        copied.wait(e, i, "xrT")
                        acts.wait(e, i - 1, "v")
                        for t in range(2):
                            for c in range(DC):
                                mm = e.matmul(ps[0:TN, 2 + t, :], xrT[:, u, c, t * TN:(t + 1) * TN],
                                              wqkv[:, c, D:3 * D], start=(c == 0), stop=(c == DC - 1))
                        proj.done(mm, "k")
                        acts.wait(e, i - 1, "rq")
                        for o in range(DC):
                            for c in range(DC):
                                mm = e.matmul(ps[:, 4, o * BN:(o + 1) * BN], wqkv[:, c, o * P:(o + 1) * P],
                                              xrT[:, u, c, :], start=(c == 0), stop=(c == DC - 1))
                        proj.done(mm, "q")

                    def stage_kv(i, u, h):
                        feat.wait(e, i, "k")
                        acts.wait(e, i, "v")
                        accd.wait(e, i - 1, "acc")
                        for c in range(DC):
                            cs = slice(c * P, (c + 1) * P)
                            for t in range(2):
                                e.matmul(ps[:, 5, cs], v1[:, u, t, cs], k1[:, u, t, cs],
                                         start=(t == 0), stop=(t == 1))
                            for t in range(2):
                                at = DC * P + c * HD0
                                mm = e.matmul(ps[:, 5, at:at + HD0], k1[:, u, t, cs], ones[0:TN, 0:HD0],
                                              start=(t == 0), stop=(t == 1))
                        kvs.done(mm, "kv")
                    pipeline(e, NB, [(stage_kv, 4), (stage_proj, 2), (stage_turn, 1)])

                @block.scalar
                def _(e):
                    def stage_copy(i, u, h):
                        turn.wait(e, i, "xnT")
                        copied.done(e.activation(cols[:, :, ds(i * BN, BN)],
                                                 ps[:, 0, 0:2 * BN].rearrange("p (c n) -> p c n", c=DC),
                                                 ACT.Copy), "cols")
                        turn.wait(e, i, "xrT")
                        proj.wait(e, i - 2, "q")
                        copied.done(e.activation(xrT[:, u, :, :],
                                                 ps[:, 1, 0:2 * BN].rearrange("p (c n) -> p c n", c=DC),
                                                 ACT.Copy), "xrT")

                    def stage_acts(i, u, h):
                        proj.wait(e, i, "k")
                        feat.wait(e, i - 1, "k")
                        acts.done(e.activation(ek[:, :, :], ps[0:TN, 2:4, 0:D], ACT.Exp), "ek")
                        acts.done(e.activation(rk[:, :, :], ps[0:TN, 2:4, 0:D], ACT.Relu), "rk")
                        kvs.wait(e, i - 2, "kv")
                        acts.done(e.activation(v1[:, u, :, :], ps[0:TN, 2:4, D:2 * D], ACT.Copy), "v")
                        proj.wait(e, i, "q")
                        feat.wait(e, i - 1, "q")
                        bank = ps[:, 4, 0:2 * BN].rearrange("p (c n) -> p c n", c=DC)
                        acts.done(e.activation(eq[:, :, :], bank, ACT.Exp), "eq")
                        acts.done(e.activation(rq[:, :, :], bank, ACT.Relu), "rq")
                    pipeline(e, NB, [(stage_acts, 2), (stage_copy, 1)])
            inner.__exit__(None)

            inner = Phase("p2")
            wout = inner.sb("wout", [P, DC, D])
            bout = inner.sb("bout", [TN, D])
            wn2 = inner.sb("wn2", [TN, D])
            diag = inner.sb("diag", [P, P])
            kvd = inner.sb("kvd", [P, DC, P])
            ksd = inner.sb("ksd", [P, DC, P])
            mix = inner.sb("mix", [P, DC, D])
            den = inner.sb("den", [P, 2, DC, TN])
            qz = inner.sb("qz", [P, 2, DC, TN])
            xnr = inner.sb("xnr", [TN, 2, D])
            xr0 = inner.sb("xr0", [TN, 2, D])
            hh = inner.sb("hh", [TN, 2, D])
            sq = inner.sb("sq", [TN, D])
            ss = inner.sb("ss", [TN, 2])
            rr = inner.sb("rr", [TN, 2])
            hw = inner.sb("hw", [TN, 2, D])
            UU, K1, C1 = 10, 10, 64
            NU = RU // UU
            emb = inner.sb("emb", [RR, 4, UU * K1])
            embT = inner.sb("embT", [UU * K1, 2, RR])
            w1b = inner.sb("w1b", [UU * K1, UU, C1])
            w2r = inner.sb("w2r", [RR, C1])
            hs = inner.sb("hs", [RR, 2, UU, C1])
            hwr = inner.sb("hwr", [RR, 2, UU, C1])
            rad = inner.sb("rad", [RR, RU])
            attr = inner.sb("attr", [RR, RU, 4])
            s_w, s_d, s_p, s_m, s_z = (inner.sem(n) for n in ("w", "d", "p", "m", "z"))
            with nc.Block() as block:
                @block.sync
                def _(e):
                    e.dma_start(wout[:, :, :], chunked(A["L0_mix_w_out"])).then_inc(s_w, 16)
                    e.dma_start(bout[:, :], A["L0_mix_b_out"].partition_broadcast(TN)).then_inc(s_w, 16)
                    e.dma_start(wn2[:, :], A["L0_mix_w_norm2"].partition_broadcast(TN)).then_inc(s_w, 16)
                    e.dma_start(w2r[:, :], A["L1_gnn_fc_w2"].rearrange("c a -> (a c)").partition_broadcast(RR))\
                     .then_inc(s_w, 16)
                    e.dma_start(attr[:, :, :], A["edge_attr_4"].rearrange("(r u) k -> r u k", r=RR)).then_inc(s_w, 16)
                    e.wait_ge(s_z, 1)
                    for u in range(UU):
                        e.dma_start(w1b[u * K1:(u + 1) * K1, u, :], A["L1_gnn_fc_w1"]).then_inc(s_w, 16)
                    e.wait_ge(s_w, 16 * (5 + UU))

                @block.gpsimd
                def _(e):
                    e.memset(w1b[:, :, :], 0.0).then_inc(s_z, 1)
                    e.memset(diag[:, :], 0.0).then_inc(s_d, 1)
                    e.wait_ge(s_d, 1)
                    for q in range(4):
                        qs = slice(q * HD0, (q + 1) * HD0)
                        e.memset(diag[qs, qs], 1.0).then_inc(s_d, 1)

                @block.vector
                def _(e):
                    e.wait_ge(s_d, 5)
                    for c in range(DC):
                        e.tensor_tensor(kvd[:, c, :], kv_acc[:, c * P:(c + 1) * P], diag[:, :],
                                        ALU.mult).then_inc(s_p, 1)
                        at = DC * P + c * HD0
                        e.tensor_tensor(ksd[:, c, :].rearrange("p (a b) -> p a b", a=4),
                                        diag[:, :].rearrange("p (a b) -> p a b", a=4),
                                        kv_acc[:, at:at + HD0].unsqueeze(1).broadcast_to([P, 4, HD0]),
                                        ALU.mult).then_inc(s_p, 1)
                    e.wait_ge(s_w, 16 * (5 + UU))
                    e.tensor_scalar(w2r[:, :], w2r[:, :], 1.679177 / 8.0, None, ALU.mult).then_inc(s_p, 1)
                    e.wait_ge(s_m, 1)
                    e.tensor_copy(mix[:, :, :], ps[:, 7, :].rearrange("p (c n) -> p c n", c=DC)).then_inc(s_p, 1)
                    e.wait_ge(s_p, 2 * DC + 2)

                @block.tensor
                def _(e):
                    e.wait_ge(s_w, 16 * (5 + UU))
                    e.wait_ge(s_p, 2 * DC)
                    for c in range(DC):
                        mm = e.matmul(ps[:, 7, c * D:(c + 1) * D], kvd[:, c, :], wout[:, c, :], start=True, stop=True)
                    mm.then_inc(s_m, 1)

            def attention():
                xn_in = inner.landing("xn", 2, 2)
                xp_out = inner.landing("xp", 2)
                dens = inner.steps("dens", "den")
                zs = inner.steps("zs", "eps", "inv", "qz")
                outs = inner.steps("outs", "out")
                hsum = inner.steps("hsum", "xb", "h")
                sqs = inner.steps("sqs", "sq")
                msq = inner.steps("msq", "ms")
                roots2 = inner.steps("roots", "root")
                fin = inner.steps("fin", "hw", "hx", "y")

                def tile_of(dram, i):
                    return dram[ds(i * TN, TN), :]

                def load(e, i, u, h):
                    fin.wait(e, i - 2, "y")
                    xn_in.start(e.dma_start(xnr[:, u, :], tile_of(xn_d, i)), u)
                    xn_in.start(e.dma_start(xr0[:, u, :], tile_of(A["x"], i)), u)

                def store(e, i, u, h):
                    fin.wait(e, i, "y")
                    xp_out.start(e.dma_start(tile_of(xp_d, i), hh[:, u, :]), u)

                def stored(e):
                    for u in range(2):
                        xp_out.wait(e, u, NB - 1)

                def denominators(e, i, u, h):
                    hsum.wait(e, i - 1, "h")
                    for c in range(DC):
                        mm = e.matmul(ps[:, 7, c * TN:(c + 1) * TN], ksd[:, c, :], qT[:, c, ds(i * TN, TN)],
                                      start=True, stop=True)
                    dens.done(mm, "den")

                def divide(e, i, u, h):
                    dens.wait(e, i, "den")
                    outs.wait(e, i - 2, "out")
                    bank = ps[:, 7, 0:2 * TN].rearrange("p (c n) -> p c n", c=DC)
                    zs.done(e.tensor_scalar(den[:, u, :, :], bank, 1e-6, None, ALU.add), "eps")
                    zs.wait(e, i, "eps")
                    zs.done(e.reciprocal(den[:, u, :, :], den[:, u, :, :]), "inv")
                    zs.wait(e, i, "inv")
                    zs.done(e.tensor_tensor(qz[:, u, :, :], qT[:, :, ds(i * TN, TN)], den[:, u, :, :], ALU.mult), "qz")

                def product(e, i, u, h):
                    zs.wait(e, i, "qz")
                    for c in range(DC):
                        mm = e.matmul(ps[0:TN, 7, D:2 * D], qz[:, u, c, :], mix[:, c, :], start=(c == 0), stop=(c == DC - 1))
                    outs.done(mm, "out")

                def add_xn(e, i, u, h):
                    xn_in.wait(e, u, h)
                    xp_out.wait(e, u, h - 1)
                    hsum.done(e.tensor_tensor(xnr[:, u, :], xnr[:, u, :], bout[:, :], ALU.add), "xb")
                    outs.wait(e, i, "out")
                    hsum.wait(e, i, "xb")
                    hsum.done(e.tensor_tensor(hh[:, u, :], xnr[:, u, :], ps[0:TN, 7, D:2 * D], ALU.add), "h")

                def square(e, i, u, h):
                    hsum.wait(e, i, "h")
                    fin.wait(e, i - 2, "y")
                    sqs.wait(e, i - 1, "sq")
                    sqs.done(e.activation(sq[:, :], hh[:, u, :], ACT.Square, accum_out=ss[:, u:u + 1]), "sq")

                def mean_square(e, i, u, h):
                    sqs.wait(e, i, "sq")
                    msq.done(e.tensor_scalar(ss[:, u:u + 1], ss[:, u:u + 1], 1.0 / D, 1e-6, ALU.mult, ALU.add), "ms")

                def root(e, i, u, h):
                    msq.wait(e, i, "ms")
                    roots2.done(e.tensor_tensor(rr[:, u:u + 1], ss[:, u:u + 1], neg_half[0:TN, 0:1], ALU.pow), "root")

                def finish(e, i, u, h):
                    fin.done(e.tensor_tensor(hw[:, u, :], hh[:, u, :], wn2[:, :], ALU.mult), "hw")
                    fin.wait(e, i, "hw")
                    fin.done(e.tensor_tensor(hh[:, u, :], hh[:, u, :], xr0[:, u, :], ALU.add), "hx")
                    fin.wait(e, i, "hx")
                    roots2.wait(e, i, "root")
                    fin.done(e.scalar_tensor_tensor(hh[:, u, :], hw[:, u, :], rr[:, u:u + 1], hh[:, u, :],
                                                    ALU.mult, ALU.add), "y")
                return dict(sync=[(load, 4), (store, 17)], tensor=[(denominators, 2), (product, 6)],
                            vector=[(divide, 5), (add_xn, 8), (mean_square, 10), (finish, 16)],
                            scalar=[(square, 8)], gpsimd=[(root, 15)]), stored

            def radial_network():
                e_in = inner.landing("emb", 4)
                turn = inner.steps("turn", "turn")
                copied = inner.steps("copied", "embT")
                hid = inner.steps("hid", "hid")
                act = inner.steps("act", "silu")
                rads = inner.steps("rads", "mul", "sum")
                raw = A["edge_attr_10"].rearrange("(r v u) k -> v r (u k)", r=RR, u=UU)

                def load(e, i, u, h):
                    turn.wait(e, i - 4, "turn")
                    e_in.start(e.dma_start(emb[:, u, :], raw[ds(i, 1), :, :].rearrange("v r k -> (v r) k")), u)

                def turned(e, i, u, h):
                    e_in.wait(e, u, h)
                    copied.wait(e, i - 1, "embT")
                    turn.done(e.transpose(ps[0:UU * K1, 6, 0:RR], emb[:, u, :], ident[0:RR, 0:RR]), "turn")

                def copy(e, i, u, h):
                    turn.wait(e, i, "turn")
                    hid.wait(e, i - 2, "hid")
                    copied.done(e.activation(embT[:, u % 2, :], ps[0:UU * K1, 6, 0:RR], ACT.Copy), "embT")

                def hidden(e, i, u, h):
                    copied.wait(e, i, "embT")
                    act.wait(e, i - 1, "silu")
                    for k in range(2):
                        half = slice(k * UU // 2, (k + 1) * UU // 2)
                        mm = e.matmul(ps[0:RR, 4 + k, 0:UU * C1 // 2], embT[:, u % 2, :],
                                      w1b[:, half, :].rearrange("p u c -> p (u c)"), start=True, stop=True)
                    hid.done(mm, "hid")

                def silu(e, i, u, h):
                    hid.wait(e, i, "hid")
                    rads.wait(e, i - 2, "mul")
                    act.done(e.activation(hs[:, u % 2, :, :], ps[0:RR, 4:6, 0:UU * C1 // 2], ACT.Silu,
                                          scale=K1 ** -0.5), "silu")

                def reduce(e, i, u, h):
                    act.wait(e, i, "silu")
                    rads.done(e.tensor_tensor(hwr[:, u % 2, :, :], hs[:, u % 2, :, :],
                                              w2r[:, :].unsqueeze(1).broadcast_to([RR, UU, C1]), ALU.mult), "mul")
                    rads.wait(e, i, "mul")
                    rads.done(e.tensor_reduce(rad[:, ds(i * UU, UU)], hwr[:, u % 2, :, :], AX, ALU.add), "sum")
                return dict(sync=[(load, 0)], tensor=[(turned, 2), (hidden, 3)], scalar=[(copy, 2), (silu, 3)],
                            vector=[(reduce, 6)]), None

            def rider(period, parts):
                stages, end = parts
                return Rider(period, end, **stages)

            def add_columns(e, at, bank):
                w = cols[:, :, ds(at, WIN)]
                return e.tensor_tensor(w, w, ps[:, bank, 0:DC * P].rearrange("p (c n) -> p c n", c=DC)[:, :, 0:WIN],
                                       ALU.add)
            sum_edges("p3", xn_d, False, add_columns,
                      riders=[rider(NG // NU, radial_network()), rider(NG // (2 * NB), attention())])

            ORDER = (1, 0, 2, 3)
            with Phase("p3w") as ph:
                wr = ph.sb("wr", [RR, 4, RU])
                wt = ph.sb("wt", [TN, RR, ST, 4])
                s_wr, s_t, s_e, s_o = (ph.sem(n) for n in ("wr", "t", "e", "o"))
                with nc.Block() as block:
                    @block.sync
                    def _(e):
                        e.wait_ge(s_e, ST)
                        e.dma_start(w_d[0:TN, :], wt[:, :, :, :].rearrange("p r s k -> p (r s k)")).then_inc(s_o, 16)
                        e.wait_ge(s_o, 16)

                    @block.vector
                    def _(e):
                        for k, m in enumerate(ORDER):
                            e.tensor_tensor(wr[:, k, :], attr[:, :, m], rad[:, :], ALU.mult).then_inc(s_wr, 1)
                        for s in range(ST):
                            e.wait_ge(s_t, s + 1)
                            e.tensor_copy(wt[:, :, s, :],
                                          ps[0:TN, 4 + s % 2, 0:4 * RR].rearrange("p (k r) -> p r k", k=4))\
                             .then_inc(s_e, 1)

                    @block.tensor
                    def _(e):
                        e.wait_ge(s_wr, 4)
                        for s in range(ST):
                            if s >= 2:
                                e.wait_ge(s_e, s - 1)
                            for k in range(4):
                                mm = e.transpose(ps[0:TN, 4 + s % 2, k * RR:(k + 1) * RR],
                                                 wr[:, k, s * TN:(s + 1) * TN], ident[0:RR, 0:RR])
                            mm.then_inc(s_t, 1)
            inner.__exit__(None)

        w2 = layer0.enter_context(nc.sbuf_tensor("gin_w2", [P, HID // P, D], F32))
        s_w2 = sem("gin_w2")

        HC = HID // P
        gin_scale = layer0.enter_context(nc.sbuf_tensor("gin_scale", [P, HC], F32))
        gin_bias = layer0.enter_context(nc.sbuf_tensor("gin_bias", [P, HC], F32))
        with Phase("p4") as ph:
            hid = ph.sb("hid", [P, 2, HC, BN])
            st = ph.sb("st", [P, HC, NB, 6])
            vecs = ph.sb("vecs", [P, 3, HC])
            mv = ph.sb("mv", [P, HC, 2])
            tmp = ph.sb("tmp", [P, 2, HC])
            s_w, s_v, s_p = ph.sem("w"), ph.sem("v"), ph.sem("p")
            up = ph.steps("up", "0", "1", "2", "3")
            outp = ph.steps("copied", "0", "1", "2", "3")
            stat = ph.steps("stat", "stats")
            h_out = ph.landing("h", 2)
            with nc.Block() as block:
                @block.sync
                def _(e):
                    for k, name in enumerate(("L0_gnn_b1", "L0_gnn_gamma", "L0_gnn_beta")):
                        e.dma_start(vecs[:, k, :], A[name].rearrange("(c p) -> p c", p=P),
                                    allow_slow_non_contiguous=True).then_inc(s_w, 16)

                    def store(i, u, h):
                        outp.wait(e, i, "3")
                        h_out.start(e.dma_start(h1_d[ds(i, 1), :, :].rearrange("b p n -> (b p) n"),
                                                hid[:, u, :, :].rearrange("p c n -> p (c n)")), u)
                    pipeline(e, NB, [(store, 0)])
                    e.dma_start(w2[:, :, :], chunked(A["L0_gnn_W2"])).then_inc(s_w2, 16)
                    for u in range(2):
                        h_out.wait(e, u, (NB - 1 - u) // 2)

                @block.tensor
                def _(e):
                    e.wait_ge(s_w1, 16)

                    def project(i, u, h):
                        for q in range(4):
                            outp.wait(e, i - 2, str(q))
                            for k in range(2):
                                f = (2 * q + k) * P
                                for c in range(DC):
                                    mm = e.matmul(ps[:, 4 * u + q, k * BN:(k + 1) * BN], w1[:, c, f:f + P],
                                                  cols[:, c, ds(i * BN, BN)], start=(c == 0), stop=(c == DC - 1))
                            up.done(mm, str(q))
                    pipeline(e, NB, [(project, 0)])

                @block.scalar
                def _(e):
                    def copy(i, u, h):
                        stat.wait(e, i - 2, "stats")
                        h_out.wait(e, u, h - 1)
                        for q in range(4):
                            up.wait(e, i, str(q))
                            outp.done(e.activation(hid[:, u, 2 * q:2 * q + 2, :],
                                                   ps[:, 4 * u + q, 0:2 * BN].rearrange("p (k n) -> p k n", k=2),
                                                   ACT.Copy), str(q))
                    pipeline(e, NB, [(copy, 0)])

                @block.vector
                def _(e):
                    def stats(i, u, h):
                        for c in range(HC):
                            outp.wait(e, i, str(c // 2))
                            ins = e.bn_stats(st[:, c, ds(i, 1), :].rearrange("p a k -> p (a k)"), hid[:, u, c, :])
                        stat.done(ins, "stats")
                    pipeline(e, NB, [(stats, 0)])
                    stat.wait(e, NB - 1, "stats")
                    box = [0]

                    def step(ins):
                        chained(e, ins, s_v, box)
                    for c in range(HC):
                        step(e.bn_aggr(mv[:, c, :], st[:, c, :, :].rearrange("p b k -> p (b k)")))
                    b1, gamma, beta = (vecs[:, k, :] for k in range(3))
                    step(e.tensor_scalar(tmp[:, 0, :], mv[:, :, 1], 1.0, 1e-5, ALU.mult, ALU.add))
                    e.sem_inc(s_p, 1)
                    e.wait_ge(s_w, 48)
                    step(e.tensor_tensor(mv[:, :, 0], mv[:, :, 0], b1, ALU.add))
                    step(e.tensor_tensor(mv[:, :, 0], b1, mv[:, :, 0], ALU.subtract))
                    e.wait_ge(s_p, 2)
                    step(e.tensor_tensor(gin_scale[:, :], tmp[:, 1, :], gamma, ALU.mult))
                    step(e.tensor_tensor(mv[:, :, 0], mv[:, :, 0], gin_scale[:, :], ALU.mult))
                    step(e.tensor_tensor(gin_bias[:, :], mv[:, :, 0], beta, ALU.add))

                @block.gpsimd
                def _(e):
                    e.wait_ge(s_p, 1)
                    e.tensor_tensor(tmp[:, 1, :], tmp[:, 0, :], neg_half[:, 0:HC], ALU.pow).then_inc(s_p, 1)

        def pick_two(e, step, prob, rank, best, first, keys, picks):
            shape = list(prob.shape)
            ranks = rank.unsqueeze(1).broadcast_to(shape)
            for k in range(2):
                step(e.tensor_reduce(best[:, k, :], prob, AX, ALU.max))
                step(e.tensor_tensor(keys, prob, best[:, k, :].unsqueeze(2).broadcast_to(shape), ALU.is_equal))
                step(e.tensor_tensor(keys, keys, ranks, ALU.mult))
                step(e.tensor_reduce(first[:, k, :], keys, AX, ALU.max))
                step(e.tensor_tensor(picks[:, k, :, :], ranks, first[:, k, :].unsqueeze(2).broadcast_to(shape),
                                     ALU.is_equal))
                if k == 0:
                    step(e.scalar_tensor_tensor(prob, picks[:, k, :, :], -2.0, prob, ALU.mult, ALU.add))

        class RowNorm:

            def __init__(self, ph, name, writes, tiles=2):
                self.tiles = tiles
                self.st = ph.sb(f"{name}_st", [TN, 2, tiles, 6])
                self.mv = ph.sb(f"{name}_mv", [TN, 2, tiles, 2])
                self.pre = ph.sb(f"{name}_pre", [TN, 2, tiles])
                self.rs = ph.sb(f"{name}_rs", [TN, 2, tiles])
                self.stats = ph.steps(f"{name}_stats", *(f"stats{t}" for t in range(tiles)), *(f"aggr{t}" for t in range(tiles)),
                                      "pre")
                self.root = ph.steps(f"{name}_root", "root")
                self.norm = ph.steps(f"{name}_norm", *writes)
                self.last = writes[-1]

            def row_stats(self, e, i, u, x):
                self.norm.wait(e, i - 2, self.last)
                for t in range(self.tiles):
                    self.stats.done(e.bn_stats(self.st[:, u, t, :], x[:, t, :]), f"stats{t}")
                self.stats.wait(e, i, f"stats{self.tiles - 1}")
                e.sem_inc(s_held["DVE"], 1)
                for t in range(self.tiles):
                    self.stats.done(e.bn_aggr(self.mv[:, u, t, :], self.st[:, u, t, :]), f"aggr{t}")
                self.stats.wait(e, i, f"aggr{self.tiles - 1}")
                self.stats.done(e.tensor_scalar(self.pre[:, u, :], self.mv[:, u, :, 1], 1.0, LN_EPS,
                                                ALU.mult, ALU.add), "pre")

            def roots(self, e, i, u):
                self.stats.wait(e, i, "pre")
                self.root.done(e.tensor_tensor(self.rs[:, u, :], self.pre[:, u, :], neg_half[0:TN, 0:self.tiles],
                                               ALU.pow), "root")

            def scaled(self, e, u, t, dst, src):
                return e.tensor_scalar(dst, src, self.mv[:, u, t, 0:1], self.rs[:, u, t:t + 1],
                                       ALU.subtract, ALU.mult)

        routes = layer0.enter_context(nc.sbuf_tensor("routes", [TN, 2 * NB, 8], F32))
        p6w = Phase("p6w")
        ws = [p6w.sb(f"w{k}", [P, NE0, DC, D]) for k in range(3)]
        b3 = p6w.sb("b3", [NE0, D])
        bs = p6w.sb("bs", [P, 2, NE0, DC])
        s_w6 = p6w.sem("w")
        NLOAD6 = 3 + 1 + 2 * NE0 * DC

        def load_weights6(e):
            for k in range(3):
                e.dma_start(ws[k][:, :, :, :].rearrange("p e c n -> p (e c) n"),
                            A[f"L0_ffn_expert_w{k + 1}"].rearrange("e (c p) n -> p (e c) n", p=P)).then_inc(s_w6, 16)
            e.dma_start(b3[:, :], A["L0_ffn_expert_b3"]).then_inc(s_w6, 16)
            for k in range(2):
                for x in range(NE0):
                    for c in range(DC):
                        e.dma_start(bs[:, k, x, c:c + 1], A[f"L0_ffn_expert_b{k + 1}"][x:x + 1, c * P:(c + 1) * P]
                                    .rearrange("a p -> p a")).then_inc(s_w6, 16)
        with Phase("p5") as ph:
            hid = ph.sb("hid", [P, 2, HC, BN])
            b2 = ph.sb("b2", [TN, D])
            xp = ph.sb("xp", [TN, 2, 2, D])
            gb = ph.sb("gb", [TN, 2, 2, D])
            x1 = ph.sb("x1", [TN, 2, 2, D])
            f1 = ph.sb("f1", [TN, 2, 2, D])
            rw1 = ph.sb("rw1", [P, DC, RH0])
            rb1 = ph.sb("rb1", [P, 1])
            rw2 = ph.sb("rw2", [P, NE0])
            rb2 = ph.sb("rb2", [TN, NE0])
            rh = ph.sb("rh", [P, 2, BN])
            s_w, s_z = ph.sem("w"), ph.sem("z")
            h_in, xp_in, x1_out = ph.landing("h", 2), ph.landing("xp", 2), ph.landing("x1", 2)
            relu = ph.steps("relu", *(str(c) for c in range(HC)))
            down = ph.steps("down", "rows")
            sums1 = ph.steps("sums", "b2", "x1")
            ln = RowNorm(ph, "ln", ("f0", "f1"))
            turn = ph.steps("turn", "turn")
            copied = ph.steps("copied", "cols")
            rhid = ph.steps("rhid", "rh")
            ract = ph.steps("ract", "relu")
            logit = ph.steps("logit", "logits")
            kept = ph.steps("kept", "logits")
            with nc.Block() as block:
                @block.sync
                def _(e):
                    loads = [(b2[:, :], A["L0_gnn_b2"].partition_broadcast(TN)),
                             (rw1[:, :, :], chunked(A["L0_ffn_router_w1"])),
                             (rb1[:, :], A["L0_ffn_router_b1"].rearrange("(p a) -> p a", a=1)),
                             (rw2[:, :], A["L0_ffn_router_w2"]),
                             (rb2[:, :], A["L0_ffn_router_b2"].partition_broadcast(TN))]
                    for dst, src in loads:
                        e.dma_start(dst, src).then_inc(s_w, 16)

                    def load(i, u, h):
                        down.wait(e, i - 2, "rows")
                        h_in.start(e.dma_start(hid[:, u, :, :].rearrange("p c n -> p (c n)"),
                                               h1_d[ds(i, 1), :, :].rearrange("b p n -> (b p) n")), u)
                        sums1.wait(e, i - 2, "x1")
                        xp_in.start(e.dma_start(xp[:, u, :, :], rows_of(xp_d, i)), u)

                    def store(i, u, h):
                        sums1.wait(e, i, "x1")
                        x1_out.start(e.dma_start(rows_of(x1_d, i), x1[:, u, :, :]), u)
                    pipeline(e, NB, [(load, 0), (store, 3)])
                    load_weights6(e)
                    for u in range(2):
                        x1_out.wait(e, u, (NB - 1 - u) // 2)

                @block.scalar
                def _(e):
                    def bn_relu(i, u, h):
                        h_in.wait(e, u, h)
                        for c in range(HC):
                            relu.done(e.activation(hid[:, u, c, :], hid[:, u, c, :], ACT.Relu,
                                                   bias=gin_bias[:, c:c + 1], scale=gin_scale[:, c:c + 1]), str(c))

                    def copy(i, u, h):
                        turn.wait(e, i, "turn")
                        copied.done(e.activation(cols[:, :, ds(i * BN, BN)],
                                                 ps[:, 2, 0:2 * BN].rearrange("p (c n) -> p c n", c=DC),
                                                 ACT.Copy), "cols")

                    def router_relu(i, u, h):
                        rhid.wait(e, i, "rh")
                        logit.wait(e, i - 2, "logits")
                        ract.done(e.activation(rh[:, u, :], ps[:, 3, 0:BN], ACT.Relu, bias=rb1[:, 0:1]), "relu")
                    e.wait_ge(s_w, 80)
                    pipeline(e, NB, [(router_relu, 4), (copy, 3), (bn_relu, 0)])

                @block.tensor
                def _(e):
                    e.wait_ge(s_w, 80)
                    e.wait_ge(s_w2, 16)

                    def rows(i, u, h):
                        sums1.wait(e, i - 2, "b2")
                        for t in range(2):
                            for c in range(HC):
                                if t == 0:
                                    relu.wait(e, i, str(c))
                                mm = e.matmul(ps[0:TN, u, t * D:(t + 1) * D], hid[:, u, c, t * TN:(t + 1) * TN],
                                              w2[:, c, :], start=(c == 0), stop=(c == HC - 1))
                        down.done(mm, "rows")

                    def turned(i, u, h):
                        ln.norm.wait(e, i, "f1")
                        copied.wait(e, i - 1, "cols")
                        for c in range(DC):
                            for t in range(2):
                                at = c * BN + t * TN
                                mm = e.transpose(ps[:, 2, at:at + TN], f1[:, u, t, c * P:(c + 1) * P],
                                                 ident[0:TN, 0:TN])
                        turn.done(mm, "turn")

                    def router(i, u, h):
                        copied.wait(e, i, "cols")
                        ract.wait(e, i - 1, "relu")
                        for c in range(DC):
                            mm = e.matmul(ps[:, 3, 0:BN], rw1[:, c, :], cols[:, c, ds(i * BN, BN)],
                                          start=(c == 0), stop=(c == DC - 1))
                        rhid.done(mm, "rh")

                    def logits(i, u, h):
                        ract.wait(e, i, "relu")
                        kept.wait(e, i - 1, "logits")
                        for t in range(2):
                            mm = e.matmul(ps[0:TN, 4, t * 8:t * 8 + NE0], rh[:, u, t * TN:(t + 1) * TN], rw2[:, :],
                                          start=True, stop=True)
                        logit.done(mm, "logits")
                    pipeline(e, NB, [(logits, 5), (router, 4), (turned, 3), (rows, 1)])

                @block.gpsimd
                def _(e):
                    pipeline(e, NB, [(lambda i, u, h: ln.roots(e, i, u), 0)])

                @block.vector
                def _(e):
                    e.memset(routes[:, :, :], 0.0).then_inc(s_z, 1)
                    e.wait_ge(s_z, 1)
                    e.wait_ge(s_w, 80)

                    def x1_of(i, u, h):
                        down.wait(e, i, "rows")
                        sums1.done(e.tensor_tensor(gb[:, u, :, :], ps[0:TN, u, :].rearrange("p (t f) -> p t f", t=2),
                                                   b2[:, :].unsqueeze(1).broadcast_to([TN, 2, D]), ALU.add), "b2")
                        sums1.wait(e, i, "b2")
                        xp_in.wait(e, u, h)
                        x1_out.wait(e, u, h - 1)
                        sums1.done(e.scalar_tensor_tensor(x1[:, u, :, :], gb[:, u, :, :], 0.0, xp[:, u, :, :],
                                                          ALU.max, ALU.add), "x1")
                        sums1.wait(e, i, "x1")
                        ln.row_stats(e, i, u, x1[:, u, :, :])

                    def f1_of(i, u, h):
                        ln.root.wait(e, i, "root")
                        turn.wait(e, i - 2, "turn")
                        for t in range(2):
                            ln.norm.done(ln.scaled(e, u, t, f1[:, u, t, :], x1[:, u, t, :]), f"f{t}")

                    def keep(i, u, h):
                        logit.wait(e, i, "logits")
                        kept.done(e.tensor_tensor(routes[:, ds(i * 2, 2), 0:NE0],
                                                  ps[0:TN, 4, 0:16].rearrange("p (t k) -> p t k", t=2)[:, :, 0:NE0],
                                                  rb2[:, :].unsqueeze(1).broadcast_to([TN, 2, NE0]), ALU.add),
                                  "logits")
                    pipeline(e, NB, [(keep, 5), (f1_of, 2), (x1_of, 1)])

        with Phase("p5r") as ph:
            NT = 2 * NB
            big = ph.sb("big", [TN, NT])
            ex = ph.sb("ex", [TN, NT, NE0])
            prob = ph.sb("prob", [TN, NT, NE0])
            best = ph.sb("best", [TN, 2, NT])
            first = ph.sb("first", [TN, 2, NT])
            gate = ph.sb("gate", [TN, NT, 2])
            rank = ph.sb("rank", [TN, NE0])
            picks = ph.sb("picks", [TN, 2, NT, NE0])
            keys = ph.sb("keys", [TN, NT, NE0])
            one = ph.sb("one", [TN, NT])
            s_v, s_e = ph.sem("v"), ph.sem("e")
            with nc.Block() as block:
                @block.vector
                def _(e):
                    box = [0]

                    def step(ins):
                        chained(e, ins, s_v, box)

                    def per_expert(x):
                        return x.unsqueeze(2).broadcast_to([TN, NT, NE0])
                    step(e.tensor_scalar(rank[:, :], iota[0:TN, 0:NE0], -1.0, 8.0, ALU.mult, ALU.add))
                    step(e.tensor_reduce(big[:, :], routes[:, :, 0:NE0], AX, ALU.max))
                    step(e.tensor_tensor(ex[:, :, :], routes[:, :, 0:NE0], per_expert(big[:, :]), ALU.subtract))
                    e.sem_inc(s_e, 1)
                    e.wait_ge(s_e, 2)
                    step(e.tensor_reduce(big[:, :], ex[:, :, :], AX, ALU.add))
                    step(e.reciprocal(big[:, :], big[:, :]))
                    step(e.tensor_tensor(prob[:, :, :], ex[:, :, :], per_expert(big[:, :]), ALU.mult))
                    pick_two(e, step, prob[:, :, :], rank[:, :], best[:, :, :], first[:, :, :], keys[:, :, :],
                             picks[:, :, :, :])
                    step(e.tensor_tensor(one[:, :], best[:, 1, :], best[:, 0, :], ALU.subtract))
                    e.sem_inc(s_e, 1)
                    e.wait_ge(s_e, 4)
                    step(e.tensor_scalar(big[:, :], gate[:, :, 1], 1.0, None, ALU.add))
                    step(e.reciprocal(gate[:, :, 0], big[:, :]))
                    step(e.tensor_tensor(gate[:, :, 1], gate[:, :, 1], gate[:, :, 0], ALU.mult))
                    for k in range(2):
                        step(e.tensor_tensor(picks[:, k, :, :], picks[:, k, :, :], per_expert(gate[:, :, k]), ALU.mult))
                    step(e.tensor_tensor(routes[:, :, 0:NE0], picks[:, 0, :, :], picks[:, 1, :, :], ALU.add))

                @block.scalar
                def _(e):
                    e.wait_ge(s_e, 1)
                    e.activation(ex[:, :, :], ex[:, :, :], ACT.Exp).then_inc(s_e, 1)
                    e.wait_ge(s_e, 3)
                    e.activation(gate[:, :, 1], one[:, :], ACT.Exp).then_inc(s_e, 1)

        with Phase("p6") as ph:
            LA, LB, LC = 2, 3, 4
            NE = NE0
            x1 = ph.sb("x1", [TN, 2, 2, D])
            acc = ph.sb("acc", [TN, 2, 2, D])
            wcur = ph.sb("wcur", [TN, 2, 2, 8])
            wT = ph.sb("wT", [NE, 2, BN])
            h1 = ph.sb("h1", [P, 2, DC, BN])
            h2 = ph.sb("h2", [P, 2, DC, BN])
            xm = ph.sb("xm", [TN, 2, 2, D])
            xmT = ph.sb("xmT", [P, 2, DC * BN])
            x_in, x_out, m_out, t_out = (ph.landing(n, 2) for n in ("xi", "xo", "mo", "to"))
            cur = ph.steps("cur", "w")
            wturn = ph.steps("wturn", "t")
            wcopy = ph.steps("wcopy", "c")
            bias3 = ph.steps("bias3", "b3")
            init = ph.steps("init", "x1")
            up = [ph.steps(n, "mm") for n in ("a", "b", "c")]
            act = [ph.steps(n, "c0", "c1") for n in ("ra", "rb")]
            mixed = ph.steps("mixed", "t0", "t1")
            ln = RowNorm(ph, "ln", ("s0", "v0", "s1", "v1"))
            turn = ph.steps("turn", "turn")
            copied = ph.steps("copied", "T")
            with nc.Block() as block:
                @block.sync
                def _(e):
                    def load(i, u, h):
                        init.wait(e, i - 2, "x1")
                        x_in.start(e.dma_start(x1[:, u, :, :], rows_of(x1_d, i)), u)

                    def store(i, u, h):
                        mixed.wait(e, i * NE + NE - 1, "t1")
                        x_out.start(e.dma_start(rows_of(x2_d, i), acc[:, u, :, :]), u)
                        ln.norm.wait(e, i, "v1")
                        m_out.start(e.dma_start(rows_of(xm_d, i), xm[:, u, :, :]), u)
                        copied.wait(e, i, "T")
                        t_out.start(e.dma_start(xmT_d[ds(i, 1), :, :].rearrange("b p n -> (b p) n"),
                                                xmT[:, u, :]), u)
                    pipeline(e, NB, [(load, 0), (store, 1)])
                    for u in range(2):
                        for s in (x_out, m_out, t_out):
                            s.wait(e, u, (NB - 1 - u) // 2)

                def at_block(when, fn):
                    def stage(m, u, h):
                        if u % NE == when:
                            fn(h * 2 + u // NE, u // NE, h)
                    return stage

                def experts(e, stages):
                    pipeline(e, NB * NE, stages, unroll=2 * NE)

                @block.scalar
                def _(e):
                    e.wait_ge(s_w6, 16 * NLOAD6)

                    def wt_copy(i, u, h):
                        wturn.wait(e, i, "t")
                        bias3.wait(e, i - 2, "b3")
                        wcopy.done(e.activation(wT[:, u, :], ps[0:NE, 6, 0:BN], ACT.Copy), "c")

                    def relu(k, hk):
                        def stage(m, u, h):
                            up[k].wait(e, m, "mm")
                            up[k + 1].wait(e, m - 2, "mm")
                            for c in range(DC):
                                act[k].done(e.activation(hk[:, u % 2, c, :],
                                                         ps[:, 2 * k + u % 2, c * BN:(c + 1) * BN], ACT.Relu,
                                                         bias=bs[:, k, u % NE, c:c + 1]), f"c{c}")
                        return stage

                    def copy(i, u, h):
                        turn.wait(e, i, "turn")
                        t_out.wait(e, u, h - 1)
                        copied.done(e.activation(xmT[:, u, :], ps[:, 6, 0:2 * BN], ACT.Copy), "T")
                    experts(e, [(at_block(NE - 1, copy), 6), (relu(1, h2), LB), (relu(0, h1), LA),
                                (at_block(0, wt_copy), 0)])

                @block.tensor
                def _(e):
                    e.wait_ge(s_w6, 16 * NLOAD6)

                    def w_turn(i, u, h):
                        cur.wait(e, i, "w")
                        copied.wait(e, i - 2, "T")
                        for t in range(2):
                            mm = e.transpose(ps[0:NE, 6, t * TN:(t + 1) * TN], wcur[:, u, t, 0:NE],
                                             ident[0:TN, 0:TN])
                        wturn.done(mm, "t")

                    def w_bias(i, u, h):
                        wcopy.wait(e, i, "c")
                        init.wait(e, i - 1, "x1")
                        for t in range(2):
                            mm = e.matmul(ps[0:TN, 7, t * D:(t + 1) * D], wT[:, u, t * TN:(t + 1) * TN], b3[:, :],
                                          start=True, stop=True)
                        bias3.done(mm, "b3")

                    def layer_a(m, u, h):
                        act[0].wait(e, m - 2, "c1")
                        i = h * 2 + u // NE
                        for o in range(DC):
                            for c in range(DC):
                                mm = e.matmul(ps[:, u % 2, o * BN:(o + 1) * BN],
                                              ws[0][:, u % NE, c, o * P:(o + 1) * P], cols[:, c, ds(i * BN, BN)],
                                              start=(c == 0), stop=(c == DC - 1))
                        up[0].done(mm, "mm")

                    def layer_b(m, u, h):
                        act[1].wait(e, m - 2, "c1")
                        act[0].wait(e, m, "c1")
                        for o in range(DC):
                            for c in range(DC):
                                mm = e.matmul(ps[:, 2 + u % 2, o * BN:(o + 1) * BN],
                                              ws[1][:, u % NE, c, o * P:(o + 1) * P], h1[:, u % 2, c, :],
                                              start=(c == 0), stop=(c == DC - 1))
                        up[1].done(mm, "mm")

                    def layer_c(m, u, h):
                        mixed.wait(e, m - 2, "t1")
                        act[1].wait(e, m, "c1")
                        for t in range(2):
                            for c in range(DC):
                                mm = e.matmul(ps[0:TN, 4 + u % 2, t * D:(t + 1) * D],
                                              h2[:, u % 2, c, t * TN:(t + 1) * TN], ws[2][:, u % NE, c, :],
                                              start=(c == 0), stop=(c == DC - 1))
                        up[2].done(mm, "mm")

                    def turned(i, u, h):
                        ln.norm.wait(e, i, "v1")
                        wcopy.wait(e, i + 1 if not isinstance(i, int) or i + 1 < NB else i, "c")
                        for c in range(DC):
                            for t in range(2):
                                at = c * BN + t * TN
                                mm = e.transpose(ps[:, 6, at:at + TN], xm[:, u, t, c * P:(c + 1) * P],
                                                 ident[0:TN, 0:TN])
                        turn.done(mm, "turn")
                    experts(e, [(at_block(NE - 1, turned), 6), (layer_c, LC), (layer_b, LB), (layer_a, LA),
                                (at_block(0, w_bias), 1), (at_block(0, w_turn), 0)])

                @block.gpsimd
                def _(e):
                    pipeline(e, NB, [(lambda i, u, h: ln.roots(e, i, u), 0)])

                @block.vector
                def _(e):
                    def current(i, u, h):
                        mixed.wait(e, i * NE - NE - 1, "t1")
                        wturn.wait(e, i - 2, "t")
                        cur.done(e.tensor_copy(wcur[:, u, :, :], routes[:, ds(i * 2, 2), :]), "w")

                    def begin(i, u, h):
                        bias3.wait(e, i, "b3")
                        x_in.wait(e, u, h)
                        x_out.wait(e, u, h - 1)
                        init.done(e.tensor_tensor(acc[:, u, :, :], ps[0:TN, 7, :].rearrange("p (t f) -> p t f", t=2),
                                                  x1[:, u, :, :], ALU.add), "x1")

                    def weigh(m, u, h):
                        b = u // NE
                        if u % NE == 0:
                            init.wait(e, h * 2 + b, "x1")
                        else:
                            mixed.wait(e, m - 1, "t1")
                        up[2].wait(e, m, "mm")
                        for t in range(2):
                            mixed.done(e.scalar_tensor_tensor(acc[:, b, t, :], ps[0:TN, 4 + u % 2, t * D:(t + 1) * D],
                                                              wcur[:, b, t, u % NE:u % NE + 1], acc[:, b, t, :],
                                                              ALU.mult, ALU.add), f"t{t}")

                    def row_stats(i, u, h):
                        mixed.wait(e, i * NE + NE - 1, "t1")
                        ln.row_stats(e, i, u, acc[:, u, :, :])

                    def normed(i, u, h):
                        ln.root.wait(e, i, "root")
                        turn.wait(e, i - 2, "turn")
                        m_out.wait(e, u, h - 1)
                        for t in range(2):
                            ln.norm.done(ln.scaled(e, u, t, xm[:, u, t, 0:MUL], acc[:, u, t, 0:MUL]), f"s{t}")
                            ln.norm.done(ln.scaled(e, u, t, xm[:, u, t, MUL:D].rearrange("p (m i) -> p i m", m=3),
                                                   acc[:, u, t, MUL:D].rearrange("p (i m) -> p i m", m=3)), f"v{t}")
                    experts(e, [(at_block(NE - 1, normed), 5), (weigh, LC), (at_block(NE - 1, row_stats), LC),
                                (at_block(0, begin), 2), (at_block(0, current), 0)])
        p6w.__exit__(None)

        layer0.close()

        SL = 6
        layer1 = ExitStack()
        msg = layer1.enter_context(nc.sbuf_tensor("msg", [P, SL, NPAD], F32))
        INNER = H1 * HD1
        IC = INNER // P
        acc = layer1.enter_context(nc.sbuf_tensor("acc", [P, IC, P], F32))
        p7 = Phase("p7")
        wkv = p7.sb("wkv", [P, DC, 2 * INNER])
        means = p7.sb("means", [P, DC * 2 * H1])
        xmT = p7.sb("xmT", [P, DC, TN])
        sq = p7.sb("sq", [TN, 2 * H1, HD1])
        v1 = p7.sb("v1", [TN, INNER])
        k1 = p7.sb("k1", [TN, INNER])
        ms = p7.sb("ms", [TN, 2, 2 * H1])
        pr = p7.sb("pr", [TN, 2, H1])
        rs = p7.sb("rs", [TN, 2, H1])
        s_w, s_p, s_mz = (p7.sem(n) for n in ("w", "p", "msg_zero"))
        with nc.Block() as block:
            @block.sync
            def _(e):
                e.dma_start(wkv[:, :, :], chunked(A["L1_mix_WkvT"])).then_inc(s_w, 16)
                e.wait_ge(s_w, 16)

            @block.vector
            def _(e):
                e.memset(msg[:, 0:1, :], 0.0).then_inc(s_mz, 1)
                e.memset(acc[:, :, :], 0.0).then_inc(s_p, 1)
                e.wait_ge(s_w, 16)
                heads = wkv[:, :, :].rearrange("p c (h d) -> p (c h) d", d=HD1)
                e.tensor_reduce(means[:, :], heads, AX, ALU.add).then_inc(s_p, 1)
                e.wait_ge(s_p, 2)
                e.scalar_tensor_tensor(heads, means[:, :].unsqueeze(2).broadcast_to([P, DC * 2 * H1, HD1]),
                                       -1.0 / HD1, heads, ALU.mult, ALU.add).then_inc(s_p, 1)

            @block.gpsimd
            def _(e):
                e.memset(msg[:, 1:3, :], 0.0).then_inc(s_mz, 1)
                e.wait_ge(s_mz, 2 + SL - 3)
                e.wait_ge(s_p, 3)

            @block.scalar
            def _(e):
                for k in range(3, SL):
                    e.activation(msg[:, k, :], iota[:, 0:1].broadcast_to([P, NPAD]), ACT.Copy).then_inc(s_mz, 1)

        def kv_products():
            K, V, DOTS = (4, 7), 5, 6
            x_in = p7.landing("x", 1)
            proj = p7.steps("proj", "k", "v")
            squares = p7.steps("sq", "k", "v", "copy")
            sizes = p7.steps("sizes", "sum", "mean", "prod")
            root = p7.steps("root", "root")
            kn = p7.steps("kn", "k")
            dots = p7.steps("dots", "dots")
            accd = p7.steps("accd", "acc")

            def load(e, i, u, h):
                proj.wait(e, i - 1, "v")
                x_in.start(e.dma_start(xmT[:, :, :],
                                       xmT_d[ds(h, 1), :, :].rearrange("b p (c t n) -> (b p) c t n", c=DC, t=2)
                                       [:, :, u, :]), 0)

            def project(e, i, u, h):
                x_in.wait(e, 0, i)
                for bank, name, at in ((K[u], "k", 0), (V, "v", INNER)):
                    if name == "k":
                        kn.wait(e, i - 2, "k")
                    else:
                        squares.wait(e, i - 1, "copy")
                    for c in range(DC):
                        mm = e.matmul(ps[0:TN, bank, :], xmT[:, c, :], wkv[:, c, at:at + INNER],
                                      start=(c == 0), stop=(c == DC - 1))
                    proj.done(mm, name)

            def square(e, i, u, h):
                sizes.wait(e, i - 1, "sum")
                dots.wait(e, i - 1, "dots")
                for q, bank, name in ((0, K[u], "k"), (H1, V, "v")):
                    proj.wait(e, i, name)
                    squares.done(e.activation(sq[:, q:q + H1, :].rearrange("p h d -> p (h d)"), ps[0:TN, bank, :],
                                              ACT.Square), name)
                squares.done(e.activation(v1[:, :], ps[0:TN, V, :], ACT.Copy), "copy")

            def size(e, i, u, h):
                squares.wait(e, i, "v")
                root.wait(e, i - 2, "root")
                sizes.done(e.tensor_reduce(ms[:, u, :], sq[:, :, :], AX, ALU.add), "sum")
                sizes.wait(e, i, "sum")
                sizes.done(e.tensor_scalar(ms[:, u, :], ms[:, u, :], 1.0 / HD1, 1e-5, ALU.mult, ALU.add), "mean")
                sizes.wait(e, i, "mean")
                sizes.done(e.tensor_tensor(pr[:, u, :], ms[:, u, 0:H1], ms[:, u, H1:2 * H1], ALU.mult), "prod")

            def roots(e, i, u, h):
                sizes.wait(e, i, "prod")
                kn.wait(e, i - 2, "k")
                root.done(e.tensor_tensor(rs[:, u, :], pr[:, u, :], neg_half[0:TN, 0:H1], ALU.pow), "root")

            def scale_k(e, i, u, h):
                root.wait(e, i, "root")
                squares.wait(e, i, "k")
                dots.wait(e, i - 1, "dots")
                kn.done(e.tensor_tensor(k1[:, :].rearrange("p (h d) -> p h d", h=H1),
                                        ps[0:TN, K[u], :].rearrange("p (h d) -> p h d", h=H1),
                                        rs[:, u, :].unsqueeze(2).broadcast_to([TN, H1, HD1]), ALU.mult), "k")

            def products(e, i, u, h):
                kn.wait(e, i, "k")
                squares.wait(e, i, "copy")
                accd.wait(e, i - 1, "acc")
                for j in range(IC):
                    js = slice(j * P, (j + 1) * P)
                    mm = e.matmul(ps[:, DOTS, js], v1[:, js], k1[:, js], start=True, stop=True)
                dots.done(mm, "dots")

            def accumulate(e, i, u, h):
                dots.wait(e, i, "dots")
                accd.wait(e, i - 1, "acc")
                flat = acc[:, :, :].rearrange("p j d -> p (j d)")
                accd.done(e.tensor_tensor(flat, flat, ps[:, DOTS, :], ALU.add), "acc")
            return Rider(NG // (2 * NB), None, sync=[(load, 0)], tensor=[(project, 5), (products, 13)],
                         scalar=[(square, 5)], gpsimd=[(roots, 14)],
                         vector=[(size, 9), (scale_k, 15), (accumulate, 16)])

        def add_messages(e, at, bank):
            def add(to, source):
                return e.tensor_tensor(to, to, source, ALU.add)
            sums = ps[:, bank, 0:7 * WIN].rearrange("p (k n) -> p k n", k=7)
            add(msg[:, 0:5, ds(at, WIN)], sums[:, 0:5, :])
            add(msg[0:MUL, 5:6, ds(at, WIN)], sums[0:MUL, 5:6, :])
            return add(msg[MUL:P, 5:6, ds(at, WIN)], sums[MUL:P, 6:7, :])
        sum_edges("p8", xm_d, True, add_messages, riders=[kv_products()])
        p7.__exit__(None)

        p7f = Phase("p7f")
        mix1 = p7f.sb("mix1", [P, DC, D])
        wq = p7f.sb("wq", [P, IC, D])
        wo = p7f.sb("wo", [P, IC, D])
        a1 = p7f.sb("a1", [P, IC, D])
        same = p7f.sb("same", [P, P])
        s_w, s_z, s_f, s_m = (p7f.sem(n) for n in ("w", "z", "f", "m"))
        with nc.Block() as block:
            @block.sync
            def _(e):
                e.dma_start(wq[:, :, :], chunked(A["L1_mix_Wq"])).then_inc(s_w, 16)
                e.dma_start(wo[:, :, :], chunked(A["L1_mix_WoutT"])).then_inc(s_w, 16)
                e.wait_ge(s_w, 32)

            @block.gpsimd
            def _(e):
                e.memset(same[:, :], 0.0).then_inc(s_z, 1)
                e.wait_ge(s_z, 1)
                for q in range(2):
                    qs = slice(q * HD1, (q + 1) * HD1)
                    e.memset(same[qs, qs], 1.0 / N).then_inc(s_z, 1)

            @block.tensor
            def _(e):
                e.wait_ge(s_w, 32)
                e.wait_ge(s_f, 1)
                for j in range(IC):
                    mm = e.matmul(ps[:, 6 + j // 2, (j % 2) * D:(j % 2 + 1) * D], acc[:, j, :], wo[:, j, :],
                                  start=True, stop=True)
                mm.then_inc(s_m, 1)
                e.wait_ge(s_f, 2)
                for c in range(DC):
                    for j in range(IC):
                        mm = e.matmul(ps[:, 0, c * D:(c + 1) * D], wq[:, j, c * P:(c + 1) * P], a1[:, j, :],
                                      start=(j == 0), stop=(j == IC - 1))
                mm.then_inc(s_m, 1)

            @block.vector
            def _(e):
                e.wait_ge(s_z, 3)
                e.tensor_tensor(acc[:, :, :], acc[:, :, :], same[:, :].unsqueeze(1).broadcast_to([P, IC, P]),
                                ALU.mult).then_inc(s_f, 1)
                e.wait_ge(s_m, 1)
                e.tensor_copy(a1[:, :, :], ps[:, 6:8, :].rearrange("p b (k n) -> p (b k) n", k=2)).then_inc(s_f, 1)
                e.wait_ge(s_m, 2)
                e.tensor_copy(mix1[:, :, :], ps[:, 0, :].rearrange("p (c n) -> p c n", c=DC)).then_inc(s_f, 1)
                e.wait_ge(s_f, 3)

        with Phase("p9") as ph:
            wm = ph.sb("wm", [P, SL, D])
            parts = ph.sb("parts", [P, 4, MUL])
            bout = ph.sb("bout", [TN, D])
            mt = ph.sb("mt", [P, 2, SL, TN])
            xmT = ph.sb("xmT", [P, 2, DC, TN])
            x2 = ph.sb("x2", [TN, 2, D])
            xb = ph.sb("xb", [TN, 2, D])
            x3 = ph.sb("x3", [TN, 2, D])
            f3 = ph.sb("f3", [TN, 2, D])
            f3T = ph.sb("f3T", [P, 2, DC, TN])
            fsum = ph.sb("fsum", [P, DC, 2 * NB])
            s_w, s_z, s_p, s_o = (ph.sem(n) for n in ("w", "z", "p", "o"))
            x_in = ph.landing("xi", 2, 2)
            x_out, f_out, t_out = (ph.landing(n, 2) for n in ("xo", "fo", "to"))
            fixed = ph.steps("fixed", "msg")
            rows = ph.steps("rows", "rows")
            sums3 = ph.steps("sums", "xb", "x3")
            ln = RowNorm(ph, "ln", ("f",), tiles=1)
            turn = ph.steps("turn", "turn")
            copied = ph.steps("copied", "c0", "c1")
            ALPHA = (2.0 * MUL) ** -0.5 / 4.0
            LO, HI = slice(0, MUL), slice(MUL, 2 * MUL)
            W00, W11, W01, W10 = range(4)
            MAPS = [(0, LO, W01, 1.0, 1), (0, HI, W11, 3.0 ** -0.5, 0),
                    (1, LO, W00, 1.0, 0), (1, HI, W10, 1.0, 1),
                    (2, LO, W01, 1.0, 2), (3, LO, W01, 1.0, 3),
                    (4, LO, W10, 1.0, 2), (4, HI, W10, 1.0, 3),
                    (5, LO, W11, 3.0 ** -0.5, 0), (5, HI, W11, 3.0 ** -0.5, 0)]

            def tile_of(dram, i):
                return dram[ds(i * TN, TN), :]
            with nc.Block() as block:
                @block.sync
                def _(e):
                    for k, name in enumerate(("00_0", "11_0", "01_1", "10_1")):
                        for half in (LO, HI):
                            e.dma_start(parts[half, k, :], A[f"L1_gnn_w_{name}"]).then_inc(s_w, 16)
                    e.dma_start(bout[:, :], A["L1_mix_bout"].partition_broadcast(TN)).then_inc(s_w, 16)

                    def load(i, u, h):
                        rows.wait(e, i - 2, "rows")
                        x_in.start(e.dma_start(xmT[:, u, :, :],
                                               xmT_d[ds(h, 1), :, :].rearrange("b p (c t n) -> (b p) c t n", c=DC, t=2)
                                               [:, :, u, :]), u)
                        sums3.wait(e, i - 2, "xb")
                        x_in.start(e.dma_start(x2[:, u, :], tile_of(x2_d, i)), u)

                    def store(i, u, h):
                        sums3.wait(e, i, "x3")
                        x_out.start(e.dma_start(tile_of(x3_d, i), x3[:, u, :]), u)
                        ln.norm.wait(e, i, "f")
                        f_out.start(e.dma_start(tile_of(f3_d, i), f3[:, u, :]), u)
                        copied.wait(e, i, "c1")
                        t_out.start(e.dma_start(f3T_d[ds(i, 1), :, :].rearrange("b p n -> (b p) n"),
                                                f3T[:, u, :, :].rearrange("p c n -> p (c n)")), u)
                    pipeline(e, 2 * NB, [(load, 0), (store, 3)])
                    for u in range(2):
                        for s in (x_out, f_out, t_out):
                            s.wait(e, u, NB - 1)
                    e.dma_start(fsum_d, fsum[:, :, :].rearrange("p c n -> p (c n)")).then_inc(s_o, 16)
                    e.wait_ge(s_o, 16)

                @block.gpsimd
                def _(e):
                    e.memset(wm[:, :, :], 0.0).then_inc(s_z, 1)
                    e.wait_ge(s_z, 1)
                    pipeline(e, 2 * NB, [(lambda i, u, h: ln.roots(e, i, u), 0)])

                @block.scalar
                def _(e):
                    def fix(i, u, h):
                        rows.wait(e, i - 2, "rows")
                        fixed.done(e.activation(mt[:, u, :, :], msg[:, :, ds(i * TN, TN)], ACT.Copy), "msg")

                    def copy(i, u, h):
                        turn.wait(e, i, "turn")
                        t_out.wait(e, u, h - 1)
                        for c in range(DC):
                            copied.done(e.activation(f3T[:, u, c, :], ps[:, 2 + u, c * TN:(c + 1) * TN], ACT.Copy,
                                                     accum_out=fsum[:, c, ds(i, 1)]), f"c{c}")
                    pipeline(e, 2 * NB, [(copy, 3), (fix, 0)])

                @block.tensor
                def _(e):
                    e.wait_ge(s_p, len(MAPS))

                    def product(i, u, h):
                        x_in.wait(e, u, h)
                        fixed.wait(e, i, "msg")
                        sums3.wait(e, i - 2, "x3")
                        for c in range(DC):
                            e.matmul(ps[0:TN, u, 0:D], xmT[:, u, c, :], mix1[:, c, :], start=(c == 0), stop=False)
                        for k in range(SL):
                            mm = e.matmul(ps[0:TN, u, 0:D], mt[:, u, k, :], wm[:, k, :],
                                          start=False, stop=(k == SL - 1))
                        rows.done(mm, "rows")

                    def turned(i, u, h):
                        ln.norm.wait(e, i, "f")
                        copied.wait(e, i - 2, "c1")
                        for c in range(DC):
                            mm = e.transpose(ps[:, 2 + u, c * TN:(c + 1) * TN], f3[:, u, c * P:(c + 1) * P],
                                             ident[0:TN, 0:TN])
                        turn.done(mm, "turn")
                    pipeline(e, 2 * NB, [(turned, 2), (product, 0)])

                @block.vector
                def _(e):
                    e.wait_ge(s_z, 1)
                    e.wait_ge(s_w, 9 * 16)
                    for slot, half, k, factor, m in MAPS:
                        to = wm[half, slot, 0:MUL] if m == 0 else wm[half, slot, MUL + m - 1:D:3]
                        e.tensor_scalar(to, parts[half, k, :], ALPHA * factor, None, ALU.mult).then_inc(s_p, 1)

                    def x3_of(i, u, h):
                        x_in.wait(e, u, h)
                        sums3.done(e.tensor_tensor(xb[:, u, :], x2[:, u, :], bout[:, :], ALU.add), "xb")
                        rows.wait(e, i, "rows")
                        sums3.wait(e, i, "xb")
                        x_out.wait(e, u, h - 1)
                        sums3.done(e.tensor_tensor(x3[:, u, :], ps[0:TN, u, 0:D], xb[:, u, :], ALU.add), "x3")
                        sums3.wait(e, i, "x3")
                        ln.row_stats(e, i, u, x3[:, u:u + 1, :])

                    def f3_of(i, u, h):
                        ln.root.wait(e, i, "root")
                        turn.wait(e, i - 2, "turn")
                        f_out.wait(e, u, h - 1)
                        ln.norm.done(ln.scaled(e, u, 0, f3[:, u, :], x3[:, u, :]), "f")
                    pipeline(e, 2 * NB, [(f3_of, 1), (x3_of, 0)])
        p7f.__exit__(None)
        layer1.close()

        with Phase("p11") as ph:
            FC = F1 // P
            w1 = ph.sb("w1", [P, 2, DC, F1])
            w2 = ph.sb("w2", [P, 2, FC, D])
            b1 = ph.sb("b1", [P, 2, FC])
            bias = ph.sb("bias", [TN, D])
            gamma = ph.sb("gamma", [TN, D])
            beta = ph.sb("beta", [TN, D])
            gates = ph.sb("gates", [P, 2])
            router = Phase("p10")
            fsum = router.sb("fsum", [P, DC, 2 * NB])
            mean = router.sb("mean", [P, DC])
            wr = router.sb("wr", [P, DC, NE1])
            br = router.sb("br", [1, NE1])
            lg = router.sb("lg", [1, NE1])
            ex = router.sb("ex", [1, NE1])
            rw = router.sb("rw", [1, NE1])
            one = router.sb("one", [1, 1])
            best = router.sb("best", [1, 2, 1])
            first = router.sb("first", [1, 2, 1])
            keys = router.sb("keys", [1, 1, NE1])
            rank = router.sb("rank", [1, NE1])
            picks = router.sb("picks", [1, 2, 1, NE1])
            gate = router.sb("gate", [1, 2])
            chosen = router.sb("chosen", [1, 2], I32)
            b2 = router.sb("b2", [1, 2, D])
            s_in, s_w, s_v, s_e, s_pe, s_sel = (router.sem(n) for n in ("in", "w", "v", "e", "pe", "sel"))
            CAPACITY = -(-N * 5 // (4 * NE1))
            with nc.Block() as block:
                @block.sync
                def _(e):
                    for dst, src in ((fsum[:, :, :].rearrange("p c n -> p (c n)"), fsum_d),
                                     (wr[:, :, :], chunked(A["L1_ffn_Wr"])),
                                     (br[:, :], A["L1_ffn_br"].rearrange("(a n) -> a n", a=1)),
                                     (gamma[:, :], A["L1_ffn_gamma"].partition_broadcast(TN)),
                                     (beta[:, :], A["L1_ffn_beta"].partition_broadcast(TN))):
                        e.dma_start(dst, src).then_inc(s_in, 16)
                    e.wait_ge(s_sel, 1)
                    for k in range(2):
                        x = e.value_load(chosen[0:1, k:k + 1], min_val=0, max_val=NE1 - 1)
                        for dst, src in ((w1[:, k, :, :], A["L1_ffn_W1"][ds(x, 1), :, :]
                                          .rearrange("e (c p) n -> p (e c) n", p=P)),
                                         (w2[:, k, :, :], A["L1_ffn_W2"][ds(x, 1), :, :]
                                          .rearrange("e (c p) n -> p (e c) n", p=P)),
                                         (b2[:, k, :], A["L1_ffn_b2"][ds(x, 1), :])):
                            e.dma_start(dst, src).then_inc(s_w, 16)
                        e.dma_start(b1[:, k, :], A["L1_ffn_b1"][ds(x, 1), :].rearrange("e (c p) -> p (e c)", p=P),
                                    allow_slow_non_contiguous=True).then_inc(s_w, 16)
                    e.wait_ge(s_w, 8 * 16)

                @block.tensor
                def _(e):
                    e.wait_ge(s_in, 5 * 16)
                    e.wait_ge(s_pe, 1)
                    for c in range(DC):
                        mm = e.matmul(ps[0:1, 0, 0:NE1], mean[:, c:c + 1], wr[:, c, :],
                                      start=(c == 0), stop=(c == DC - 1))
                    mm.then_inc(s_pe, 1)
                    e.wait_ge(s_pe, 3)
                    e.matmul(ps[:, 1, 0:2], ones[0:1, :], gate[:, :], start=True, stop=True).then_inc(s_pe, 1)
                    e.wait_ge(s_pe, 5)
                    for k in range(2):
                        mm = e.matmul(ps[0:TN, 2, 0:D], ones[0:1, 0:TN], b2[:, k, :], start=(k == 0), stop=(k == 1))
                    mm.then_inc(s_pe, 1)

                @block.scalar
                def _(e):
                    for k in range(2):
                        e.wait_ge(s_e, 2 * k + 1)
                        e.activation(ex[:, :], lg[:, :], ACT.Exp).then_inc(s_e, 1)
                    e.wait_ge(s_e, 5)
                    e.activation(gate[:, 1:2], one[:, :], ACT.Exp).then_inc(s_e, 1)

                @block.vector
                def _(e):
                    box = [0]

                    def step(ins):
                        chained(e, ins, s_v, box)

                    def softmax(k):
                        step(e.tensor_reduce(one[:, :], lg[:, :], AX, ALU.max))
                        step(e.tensor_scalar(lg[:, :], lg[:, :], one[:, 0:1], None, ALU.subtract))
                        e.sem_inc(s_e, 1)
                        e.wait_ge(s_e, 2 * k + 2)
                        step(e.tensor_reduce(one[:, :], ex[:, :], AX, ALU.add))
                        step(e.reciprocal(one[:, :], one[:, :]))
                        step(e.tensor_scalar(rw[:, :], ex[:, :], one[:, 0:1], None, ALU.mult))
                    e.wait_ge(s_in, 5 * 16)
                    step(e.tensor_reduce(mean[:, :], fsum[:, :, :], AX, ALU.add))
                    step(e.tensor_scalar(mean[:, :], mean[:, :], 1.0 / N, None, ALU.mult))
                    e.sem_inc(s_pe, 1)
                    step(e.tensor_scalar(rank[:, :], iota[0:1, 0:NE1], -1.0, 8.0, ALU.mult, ALU.add))
                    e.wait_ge(s_pe, 2)
                    step(e.tensor_tensor(lg[:, :], ps[0:1, 0, 0:NE1], br[:, :], ALU.add))
                    softmax(0)
                    step(e.tensor_scalar(lg[:, :], rw[:, :], float(N), None, ALU.mult))
                    step(e.reciprocal(lg[:, :], lg[:, :]))
                    step(e.tensor_scalar(lg[:, :], lg[:, :], float(CAPACITY), 1.0, ALU.mult, ALU.min))
                    step(e.tensor_tensor(lg[:, :], lg[:, :], rw[:, :], ALU.mult))
                    softmax(1)
                    pick_two(e, step, rw[:, :].unsqueeze(1), rank[:, :], best[:, :, :], first[:, :, :],
                             keys[:, :, :], picks[:, :, :, :])
                    step(e.tensor_scalar(chosen[:, :], first[:, :, 0], -1.0, 8.0, ALU.mult, ALU.add))
                    e.sem_inc(s_sel, 1)
                    step(e.tensor_tensor(one[:, :], best[:, 1, :], best[:, 0, :], ALU.subtract))
                    e.sem_inc(s_e, 1)
                    e.wait_ge(s_e, 6)
                    step(e.tensor_scalar(one[:, :], gate[:, 1:2], 1.0, None, ALU.add))
                    step(e.reciprocal(gate[:, 0:1], one[:, :]))
                    step(e.tensor_tensor(gate[:, 1:2], gate[:, 1:2], gate[:, 0:1], ALU.mult))
                    e.sem_inc(s_pe, 1)
                    e.wait_ge(s_pe, 4)
                    step(e.tensor_copy(gates[:, :], ps[:, 1, 0:2]))
                    e.wait_ge(s_w, 8 * 16)
                    for k in range(2):
                        step(e.tensor_scalar(b2[:, k, :], b2[:, k, :], gate[:, k:k + 1], None, ALU.mult))
                    e.sem_inc(s_pe, 1)
                    for k in range(2):
                        step(e.tensor_scalar(w2[:, k, :, :], w2[:, k, :, :], gates[:, k:k + 1], None, ALU.mult))
                    e.wait_ge(s_pe, 6)
                    step(e.tensor_copy(bias[:, :], ps[0:TN, 2, 0:D]))
            router.__exit__(None)

            f3T = ph.sb("f3T", [P, 2, 2, DC * TN])
            hid = ph.sb("hid", [P, 2, 2, FC, BN])
            f3 = ph.sb("f3", [TN, 2, 2, D])
            x3 = ph.sb("x3", [TN, 2, 2, D])
            z = ph.sb("z", [TN, 2, 2, D])
            y = ph.sb("y", [TN, 2, 2, D])
            c_in, f_in, x_in, y_out = (ph.landing(n, 2) for n in ("ci", "fi", "xi", "yo"))
            BANKS = [f"{q}" for q in range(FC)]
            up = ph.steps("up", *BANKS)
            act = ph.steps("act", *BANKS)
            down = ph.steps("down", "rows")
            sums = ph.steps("sums", "bias", "z")
            ln = RowNorm(ph, "ln", ("n0", "n1"))
            fin = ph.steps("fin", "beta", "gamma", "out")
            with nc.Block() as block:
                @block.sync
                def _(e):
                    def load_columns(i, u, h):
                        up.wait(e, i - 2, BANKS[-1])
                        c_in.start(e.dma_start(f3T[:, u, :, :], f3T_d[ds(i * 2, 2), :, :].rearrange("t p n -> p t n")), u)

                    def load_rows(i, u, h):
                        sums.wait(e, i - 2, "bias")
                        f_in.start(e.dma_start(f3[:, u, :, :], rows_of(f3_d, i)), u)
                        fin.wait(e, i - 2, "beta")
                        x_in.start(e.dma_start(x3[:, u, :, :], rows_of(x3_d, i)), u)

                    def store(i, u, h):
                        fin.wait(e, i, "out")
                        y_out.start(e.dma_start(rows_of(out, i), y[:, u, :, :]), u)
                    pipeline(e, NB, [(load_columns, 0), (store, 2), (load_rows, 0)])
                    for u in range(2):
                        y_out.wait(e, u, (NB - 1 - u) // 2)

                @block.tensor
                def _(e):
                    def layer_up(i, u, h):
                        c_in.wait(e, u, h)
                        for q in range(FC):
                            act.wait(e, i - 1, BANKS[q])
                            for m in range(2):
                                k, f = divmod(2 * q + m, FC)
                                for c in range(DC):
                                    mm = e.matmul(ps[:, q, m * BN:(m + 1) * BN], w1[:, k, c, f * P:(f + 1) * P],
                                                  f3T[:, u, :, c * TN:(c + 1) * TN],
                                                  start=(c == 0), stop=(c == DC - 1))
                            up.done(mm, BANKS[q])

                    def layer_down(i, u, h):
                        sums.wait(e, i - 2, "z")
                        act.wait(e, i, BANKS[-1])
                        for t in range(2):
                            for j in range(2 * FC):
                                k, f = divmod(j, FC)
                                mm = e.matmul(ps[0:TN, 4 + u, t * D:(t + 1) * D], hid[:, u, k, f, t * TN:(t + 1) * TN],
                                              w2[:, k, f, :], start=(j == 0), stop=(j == 2 * FC - 1))
                        down.done(mm, "rows")
                    pipeline(e, NB, [(layer_down, 1), (layer_up, 0)])

                @block.scalar
                def _(e):
                    def gelu(i, u, h):
                        down.wait(e, i - 2, "rows")
                        for q in range(FC):
                            up.wait(e, i, BANKS[q])
                            for m in range(2):
                                k, f = divmod(2 * q + m, FC)
                                ins = e.activation(hid[:, u, k, f, :], ps[:, q, m * BN:(m + 1) * BN], ACT.Gelu,
                                                   bias=b1[:, k, f:f + 1])
                            act.done(ins, BANKS[q])
                    pipeline(e, NB, [(gelu, 0)])

                @block.gpsimd
                def _(e):
                    pipeline(e, NB, [(lambda i, u, h: ln.roots(e, i, u), 0)])

                @block.vector
                def _(e):
                    def both(x):
                        return x[:, :].unsqueeze(1).broadcast_to([TN, 2, D])

                    def residual(i, u, h):
                        f_in.wait(e, u, h)
                        ln.norm.wait(e, i - 2, "n1")
                        sums.done(e.tensor_tensor(z[:, u, :, :], f3[:, u, :, :], both(bias), ALU.add), "bias")
                        down.wait(e, i, "rows")
                        sums.wait(e, i, "bias")
                        sums.done(e.tensor_tensor(z[:, u, :, :], ps[0:TN, 4 + u, :].rearrange("p (t f) -> p t f", t=2),
                                                  z[:, u, :, :], ALU.add), "z")
                        sums.wait(e, i, "z")
                        ln.row_stats(e, i, u, z[:, u, :, :])

                    def finish(i, u, h):
                        x_in.wait(e, u, h)
                        y_out.wait(e, u, h - 1)
                        ln.root.wait(e, i, "root")
                        for t in range(2):
                            ln.norm.done(ln.scaled(e, u, t, z[:, u, t, :], z[:, u, t, :]), f"n{t}")
                        fin.done(e.tensor_tensor(y[:, u, :, :], x3[:, u, :, :], both(beta), ALU.add), "beta")
                        ln.norm.wait(e, i, "n1")
                        fin.done(e.tensor_tensor(z[:, u, :, :], z[:, u, :, :], both(gamma), ALU.mult), "gamma")
                        fin.wait(e, i, "gamma")
                        fin.done(e.tensor_tensor(y[:, u, :, :], y[:, u, :, :], z[:, u, :, :], ALU.add), "out")
                    pipeline(e, NB, [(finish, 1), (residual, 0)])


_ORDER = [*range(MUL), *(MUL + 3 * i + m for m in range(3) for i in range(MUL))]


def lay_out(inputs):
    import numpy as _np
    arrays = {name: _np.asarray(a) for name, a in inputs.items()}
    wqkv = arrays.pop("L1_mix_Wqkv")
    inner = wqkv.shape[0] // 3
    arrays["L1_mix_Wq"] = wqkv[:inner][:, _ORDER]
    arrays["L1_mix_WkvT"] = wqkv[inner:].T[_ORDER]
    arrays["L1_mix_WoutT"] = arrays.pop("L1_mix_Wout").T
    return arrays


def kernel(**inputs):
    import numpy as _np
    import concourse.bacc as _bacc
    from concourse.bass_utils import run_bass_kernel_spmd as _run

    nc = _bacc.Bacc("TRN2", target_bir_lowering=False, num_devices=1)
    arrays, args = {}, {}
    for name, a in lay_out(inputs).items():
        a = _np.ascontiguousarray(a)
        arrays[f"in_{name}"] = a
        args[name] = nc.dram_tensor(f"in_{name}", a.shape, mybir.dt.from_np(a.dtype), kind="ExternalInput").ap()
    out = nc.dram_tensor("out_0", (N, D), F32, kind="ExternalOutput").ap()
    gps_kernel(nc, args, out)
    r = _run(nc, [arrays], core_ids=[0])
    return r.results[0]["out_0"]
```
